# Optimizing a Trainium2 kernel written in Bass

```python
import numpy as np
import jax
import jax.numpy as jnp

def _softmax(x, axis=-1):
    return jax.nn.softmax(x, axis=axis)

def _gelu(x):
    return jax.nn.gelu(x, approximate=True)

def _silu(x):
    return jax.nn.silu(x)

def _sigmoid(x):
    return jax.nn.sigmoid(x)

def _layernorm(x, axis=-1, eps=1e-05):
    m = jnp.mean(x, axis=axis, keepdims=True)
    v = jnp.var(x, axis=axis, keepdims=True)
    return (x - m) / jnp.sqrt(v + eps)

def _scatter_add(tgt, idx, src, axis=0):
    return tgt.at[idx].add(src)

def _segment_sum(src, seg, n):
    return jax.ops.segment_sum(src, seg, n)
kernel_name = 'mk_decoder_preln_d2_seqx_r4_5f9f77'

def setup_inputs(seed: int=0):
    np.random.seed(seed)
    _w = jnp.asarray

    def _rec_inputs():
        import jax
        import jax.numpy as jnp
        _rk = jax.random.key(seed)
        x = -0.0003929 + 0.9999 * jax.random.normal(jax.random.fold_in(_rk, 1), (8, 112, 512), jnp.float32)
        _lenS = 112 - jax.random.randint(jax.random.fold_in(_rk, 7), (8,), 0, max(1, 112 // 4) + 1, jnp.int32)
        _lenS2 = 375 - jax.random.randint(jax.random.fold_in(_rk, 8), (8,), 0, max(1, 375 // 4) + 1, jnp.int32)
        _ctx_2048P = jax.random.normal(jax.random.fold_in(_rk, 11), (8, 16, 512), jnp.float32)
        _ctx_2048c = jax.random.dirichlet(jax.random.fold_in(_rk, 511), 0.3 * jnp.ones((16,), jnp.float32), (8, 375))
        _ctx_2048t = jnp.einsum('bsk,bkd->bsd', _ctx_2048c, _ctx_2048P)
        _ctx_2048t = _ctx_2048t * jax.lax.rsqrt(jnp.mean(jnp.square(_ctx_2048t)) + 1e-12) * 0.953939
        ctx_2048 = -0.000514642 + 1.00011 * (_ctx_2048t + 0.3 * jax.random.normal(jax.random.fold_in(_rk, 611), (8, 375, 512), jnp.float32))
        _validS = jnp.arange(112)[None, :] < _lenS[:, None]
        _validS2 = jnp.arange(375)[None, :] < _lenS2[:, None]
        _causal = jnp.tril(jnp.ones((112, 112), dtype=bool))
        mask_BxS2_ik0 = jnp.where(jnp.broadcast_to(_validS2[:, :], (8, 375)), 0, 1).astype(jnp.int32)
        mask_BxS2_bk0 = jnp.logical_not(jnp.broadcast_to(_validS2[:, :], (8, 375)))
        return (x, ctx_2048, mask_BxS2_ik0, mask_BxS2_bk0)
    x, ctx_2048, mask_BxS2_ik0, mask_BxS2_bk0 = _rec_inputs()

    def _L0_attn_setup():
        import jax, jax.numpy as jnp
        import numpy as np
        D_MODEL = 512
        NUM_HEADS = 16
        HEAD_DIM = D_MODEL // NUM_HEADS
        BATCH = 2
        SEQ = 512
        key = jax.random.key(seed)
        ks = jax.random.split(key, 9)
        s = 1.0 / np.sqrt(D_MODEL)
        x = jax.random.normal(ks[0], (BATCH, SEQ, D_MODEL), dtype=jnp.float32)
        wq = jax.random.uniform(ks[1], (D_MODEL, D_MODEL), minval=-s, maxval=s, dtype=jnp.float32)
        bq = jax.random.uniform(ks[2], (D_MODEL,), minval=-s, maxval=s, dtype=jnp.float32)
        wk = jax.random.uniform(ks[3], (D_MODEL, D_MODEL), minval=-s, maxval=s, dtype=jnp.float32)
        bk = jax.random.uniform(ks[4], (D_MODEL,), minval=-s, maxval=s, dtype=jnp.float32)
        wv = jax.random.uniform(ks[5], (D_MODEL, D_MODEL), minval=-s, maxval=s, dtype=jnp.float32)
        bv = jax.random.uniform(ks[6], (D_MODEL,), minval=-s, maxval=s, dtype=jnp.float32)
        wo = jax.random.uniform(ks[7], (D_MODEL, D_MODEL), minval=-s, maxval=s, dtype=jnp.float32)
        bo = jax.random.uniform(ks[8], (D_MODEL,), minval=-s, maxval=s, dtype=jnp.float32)
        return {'x': x, 'wq': wq, 'bq': bq, 'wk': wk, 'bk': bk, 'wv': wv, 'bv': bv, 'wo': wo, 'bo': bo}
    _L0_attn_all = _L0_attn_setup()
    _L0_attn_in = {k: v for k, v in _L0_attn_all.items() if k in ('wq', 'bq', 'wk', 'bk', 'wv', 'bv', 'wo', 'bo')}
    del _L0_attn_all

    def _L0_xattn_setup():
        import jax, jax.numpy as jnp
        import numpy as np
        import math
        H = 512
        NH = 16
        HD = H // NH
        EPS_LN = 1e-05
        RES_SCALE_MAX = 0.3

        def _nan_clean(x, lim=10000.0):
            return jnp.nan_to_num(x, nan=0.0, posinf=lim, neginf=-lim)
        key = jax.random.key(seed)
        ks = jax.random.split(key, 12)
        B, S, T = (4, 512, 64)
        std = 1.0 / math.sqrt(H)
        return {'hidden_states': jax.random.normal(ks[0], (B, S, H), jnp.float32), 'audio_tokens': jax.random.normal(ks[1], (B, T, H), jnp.float32), 'attention_mask': jax.random.randint(ks[2], (B, T), 0, 2, jnp.int32), 'Wq': jax.random.normal(ks[3], (H, H), jnp.float32) * std, 'bq': jnp.zeros((H,), jnp.float32), 'Wk': jax.random.normal(ks[4], (H, H), jnp.float32) * std, 'bk': jnp.zeros((H,), jnp.float32), 'Wv': jax.random.normal(ks[5], (H, H), jnp.float32) * std, 'bv': jnp.zeros((H,), jnp.float32), 'Wo': jax.random.normal(ks[6], (H, H), jnp.float32) * std, 'bo': jnp.zeros((H,), jnp.float32), 'ln_gamma': jnp.ones((H,), jnp.float32), 'ln_beta': jnp.zeros((H,), jnp.float32), 'residual_scale': jnp.float32(0.05)}
    _L0_xattn_all = _L0_xattn_setup()
    _L0_xattn_in = {k: v for k, v in _L0_xattn_all.items() if k in ('Wq', 'bq', 'Wk', 'bk', 'Wv', 'bv', 'Wo', 'bo', 'ln_gamma', 'ln_beta', 'residual_scale')}
    del _L0_xattn_all

    def _L0_ffn_setup():
        import jax, jax.numpy as jnp
        import numpy as np
        H = 512
        NH = 32
        KVH = 4
        HD = 128
        E = 32
        TOPK = 8
        I = 256
        EPS = 1e-05
        THETA = 10000.0

        def _rmsnorm(x, w, eps=EPS):
            xf = x.astype(jnp.float32)
            var = jnp.mean(xf * xf, axis=-1, keepdims=True)
            return (w * (xf * jax.lax.rsqrt(var + eps))).astype(x.dtype)

        def _rope(x, pos):
            d = x.shape[-1]
            inv_freq = 1.0 / THETA ** (jnp.arange(0, d, 2, dtype=jnp.float32) / d)
            ang = pos.astype(jnp.float32)[:, None] * inv_freq[None, :]
            cos = jnp.cos(ang)[None, :, None, :]
            sin = jnp.sin(ang)[None, :, None, :]
            x1, x2 = jnp.split(x, 2, axis=-1)
            return jnp.concatenate([x1 * cos - x2 * sin, x1 * sin + x2 * cos], axis=-1)
        key = jax.random.key(seed)
        ks = jax.random.split(key, 16)
        s = 0.02
        n = lambda k, shape: jax.random.normal(k, shape, dtype=jnp.float32) * s
        return {'hidden_states': jax.random.normal(ks[0], (1, 128, H), dtype=jnp.float32), 'ln1_w': jnp.ones((H,), jnp.float32), 'ln2_w': jnp.ones((H,), jnp.float32), 'Wq': n(ks[1], (H, NH * HD)), 'Wk': n(ks[2], (H, KVH * HD)), 'Wv': n(ks[3], (H, KVH * HD)), 'Wo': n(ks[4], (NH * HD, H)), 'Wr': n(ks[5], (H, E)), 'expert_bias': jax.random.normal(ks[6], (E,), dtype=jnp.float32) * 0.1, 'Wg': n(ks[7], (E, H, I)), 'Wu': n(ks[8], (E, H, I)), 'Wd': n(ks[9], (E, I, H)), 'Wsg': n(ks[10], (H, I)), 'Wsu': n(ks[11], (H, I)), 'Wsd': n(ks[12], (I, H))}
    _L0_ffn_all = _L0_ffn_setup()
    _L0_ffn_in = {k: v for k, v in _L0_ffn_all.items() if k in ('ln1_w', 'ln2_w', 'Wq', 'Wk', 'Wv', 'Wo', 'Wr', 'expert_bias', 'Wg', 'Wu', 'Wd', 'Wsg', 'Wsu', 'Wsd')}
    del _L0_ffn_all

    def _L1_attn_setup():
        import jax, jax.numpy as jnp
        import numpy as np
        NUM_HEADS = 32
        MAX_BIAS_LENGTH = 256
        ROPE_BASE = 10000.0

        def _rope_cos_sin(seq_len, head_dim, dtype):
            half = head_dim // 2
            inv_freq = 1.0 / ROPE_BASE ** (jnp.arange(0, half, dtype=jnp.float32) / half)
            t = jnp.arange(seq_len, dtype=jnp.float32)
            freqs = jnp.outer(t, inv_freq)
            return (jnp.cos(freqs).astype(dtype), jnp.sin(freqs).astype(dtype))

        def _apply_rope(x, cos, sin):
            half = x.shape[-1] // 2
            x1, x2 = (x[..., :half], x[..., half:])
            c = cos[None, :, None, :]
            s = sin[None, :, None, :]
            return jnp.concatenate([x1 * c - x2 * s, x1 * s + x2 * c], axis=-1)
        key = jax.random.key(seed)
        ks = jax.random.split(key, 7)
        B, S, Dm = (2, 512, 512)
        std = 1.0 / np.sqrt(Dm)
        return {'hidden_states': jax.random.normal(ks[0], (B, S, Dm), jnp.float32), 'Wq': jax.random.normal(ks[1], (Dm, Dm), jnp.float32) * std, 'Wk': jax.random.normal(ks[2], (Dm, Dm), jnp.float32) * std, 'Wv': jax.random.normal(ks[3], (Dm, Dm), jnp.float32) * std, 'Wo': jax.random.normal(ks[4], (Dm, Dm), jnp.float32) * std, 'learnable_bias': jax.random.normal(ks[5], (NUM_HEADS, MAX_BIAS_LENGTH), jnp.float32) * 0.001, 'softmax_offset': jnp.zeros((NUM_HEADS,), jnp.float32)}
    _L1_attn_all = _L1_attn_setup()
    _L1_attn_in = {k: v for k, v in _L1_attn_all.items() if k in ('Wq', 'Wk', 'Wv', 'Wo', 'learnable_bias', 'softmax_offset')}
    del _L1_attn_all

    def _L1_xattn_setup():
        import jax, jax.numpy as jnp
        import numpy as np
        H = 512
        NH = 16
        HD = H // NH
        EPS = 1e-06

        def rmsnorm(x, w, eps=EPS):
            var = jnp.mean(x * x, axis=-1, keepdims=True)
            return x * jax.lax.rsqrt(var + eps) * w
        key = jax.random.key(seed)
        ks = jax.random.split(key, 9)
        B, L, M = (4, 1024, 64)
        s = 1.0 / np.sqrt(H)
        return {'hidden_states': jax.random.normal(ks[0], (B, L, H), dtype=jnp.float32), 'memory_tokens': jax.random.normal(ks[1], (B, M, H), dtype=jnp.float32), 'memory_mask': jax.random.randint(ks[2], (B, M), 0, 2).astype(bool), 'norm_w': jnp.ones((H,), dtype=jnp.float32), 'wq': jax.random.normal(ks[3], (H, H), dtype=jnp.float32) * s, 'wk': jax.random.normal(ks[4], (H, H), dtype=jnp.float32) * s, 'wv': jax.random.normal(ks[5], (H, H), dtype=jnp.float32) * s, 'wo': jax.random.normal(ks[6], (H, H), dtype=jnp.float32) * s, 'wg': jax.random.normal(ks[7], (H, H), dtype=jnp.float32) * s}
    _L1_xattn_all = _L1_xattn_setup()
    _L1_xattn_in = {k: v for k, v in _L1_xattn_all.items() if k in ('norm_w', 'wq', 'wk', 'wv', 'wo', 'wg')}
    del _L1_xattn_all

    def _L1_ffn_setup():
        import jax, jax.numpy as jnp
        import numpy as np
        DIM_IN = 512
        DIM_HIDDEN = 2048
        key = jax.random.key(seed)
        k_x, k_g, k_u, k_d = jax.random.split(key, 4)
        s_in = 1.0 / np.sqrt(DIM_IN)
        s_hid = 1.0 / np.sqrt(DIM_HIDDEN)
        x = jax.random.normal(k_x, (4, 512, DIM_IN), dtype=jnp.float32)
        w_gate = jax.random.uniform(k_g, (DIM_HIDDEN, DIM_IN), jnp.float32, -s_in, s_in)
        w_up = jax.random.uniform(k_u, (DIM_HIDDEN, DIM_IN), jnp.float32, -s_in, s_in)
        w_down = jax.random.uniform(k_d, (DIM_IN, DIM_HIDDEN), jnp.float32, -s_hid, s_hid)
        return {'x': x, 'w_gate': w_gate, 'w_up': w_up, 'w_down': w_down}
    _L1_ffn_all = _L1_ffn_setup()
    _L1_ffn_in = {k: v for k, v in _L1_ffn_all.items() if k in ('w_gate', 'w_up', 'w_down')}
    del _L1_ffn_all
    return {'x': x, 'ctx_2048': ctx_2048, 'mask_BxS2_ik0': mask_BxS2_ik0, 'mask_BxS2_bk0': mask_BxS2_bk0, 'L0_attn_wq': _L0_attn_in['wq'], 'L0_attn_bq': _L0_attn_in['bq'], 'L0_attn_wk': _L0_attn_in['wk'], 'L0_attn_bk': _L0_attn_in['bk'], 'L0_attn_wv': _L0_attn_in['wv'], 'L0_attn_bv': _L0_attn_in['bv'], 'L0_attn_wo': _L0_attn_in['wo'], 'L0_attn_bo': _L0_attn_in['bo'], 'L0_xattn_Wq': _L0_xattn_in['Wq'], 'L0_xattn_bq': _L0_xattn_in['bq'], 'L0_xattn_Wk': _L0_xattn_in['Wk'], 'L0_xattn_bk': _L0_xattn_in['bk'], 'L0_xattn_Wv': _L0_xattn_in['Wv'], 'L0_xattn_bv': _L0_xattn_in['bv'], 'L0_xattn_Wo': _L0_xattn_in['Wo'], 'L0_xattn_bo': _L0_xattn_in['bo'], 'L0_xattn_ln_gamma': _L0_xattn_in['ln_gamma'], 'L0_xattn_ln_beta': _L0_xattn_in['ln_beta'], 'L0_xattn_residual_scale': _L0_xattn_in['residual_scale'], 'L0_ffn_ln1_w': _L0_ffn_in['ln1_w'], 'L0_ffn_ln2_w': _L0_ffn_in['ln2_w'], 'L0_ffn_Wq': _L0_ffn_in['Wq'], 'L0_ffn_Wk': _L0_ffn_in['Wk'], 'L0_ffn_Wv': _L0_ffn_in['Wv'], 'L0_ffn_Wo': _L0_ffn_in['Wo'], 'L0_ffn_Wr': _L0_ffn_in['Wr'], 'L0_ffn_expert_bias': _L0_ffn_in['expert_bias'], 'L0_ffn_Wg': _L0_ffn_in['Wg'], 'L0_ffn_Wu': _L0_ffn_in['Wu'], 'L0_ffn_Wd': _L0_ffn_in['Wd'], 'L0_ffn_Wsg': _L0_ffn_in['Wsg'], 'L0_ffn_Wsu': _L0_ffn_in['Wsu'], 'L0_ffn_Wsd': _L0_ffn_in['Wsd'], 'L1_attn_Wq': _L1_attn_in['Wq'], 'L1_attn_Wk': _L1_attn_in['Wk'], 'L1_attn_Wv': _L1_attn_in['Wv'], 'L1_attn_Wo': _L1_attn_in['Wo'], 'L1_attn_learnable_bias': _L1_attn_in['learnable_bias'], 'L1_attn_softmax_offset': _L1_attn_in['softmax_offset'], 'L1_xattn_norm_w': _L1_xattn_in['norm_w'], 'L1_xattn_wq': _L1_xattn_in['wq'], 'L1_xattn_wk': _L1_xattn_in['wk'], 'L1_xattn_wv': _L1_xattn_in['wv'], 'L1_xattn_wo': _L1_xattn_in['wo'], 'L1_xattn_wg': _L1_xattn_in['wg'], 'L1_ffn_w_gate': _L1_ffn_in['w_gate'], 'L1_ffn_w_up': _L1_ffn_in['w_up'], 'L1_ffn_w_down': _L1_ffn_in['w_down']}

def reference(x, ctx_2048, mask_BxS2_ik0, mask_BxS2_bk0, L0_attn_wq, L0_attn_bq, L0_attn_wk, L0_attn_bk, L0_attn_wv, L0_attn_bv, L0_attn_wo, L0_attn_bo, L0_xattn_Wq, L0_xattn_bq, L0_xattn_Wk, L0_xattn_bk, L0_xattn_Wv, L0_xattn_bv, L0_xattn_Wo, L0_xattn_bo, L0_xattn_ln_gamma, L0_xattn_ln_beta, L0_xattn_residual_scale, L0_ffn_ln1_w, L0_ffn_ln2_w, L0_ffn_Wq, L0_ffn_Wk, L0_ffn_Wv, L0_ffn_Wo, L0_ffn_Wr, L0_ffn_expert_bias, L0_ffn_Wg, L0_ffn_Wu, L0_ffn_Wd, L0_ffn_Wsg, L0_ffn_Wsu, L0_ffn_Wsd, L1_attn_Wq, L1_attn_Wk, L1_attn_Wv, L1_attn_Wo, L1_attn_learnable_bias, L1_attn_softmax_offset, L1_xattn_norm_w, L1_xattn_wq, L1_xattn_wk, L1_xattn_wv, L1_xattn_wo, L1_xattn_wg, L1_ffn_w_gate, L1_ffn_w_up, L1_ffn_w_down):
    import jax
    import jax.numpy as jnp

    def _L0_attn_ref(x, wq, bq, wk, bk, wv, bv, wo, bo):
        import jax, jax.numpy as jnp
        import numpy as np
        D_MODEL = 512
        NUM_HEADS = 16
        HEAD_DIM = D_MODEL // NUM_HEADS
        BATCH = 2
        SEQ = 512
        b, n, _ = x.shape
        q = (x @ wq.T + bq).reshape(b, n, NUM_HEADS, HEAD_DIM).transpose(0, 2, 1, 3)
        k = (x @ wk.T + bk).reshape(b, n, NUM_HEADS, HEAD_DIM).transpose(0, 2, 1, 3)
        v = (x @ wv.T + bv).reshape(b, n, NUM_HEADS, HEAD_DIM).transpose(0, 2, 1, 3)
        scores = jnp.einsum('bhqd,bhkd->bhqk', q, k)
        causal = jnp.tril(jnp.ones((n, n), dtype=bool))
        scores = jnp.where(causal[None, None], scores, -jnp.inf)
        attn = jax.nn.softmax(scores / np.sqrt(HEAD_DIM), axis=-1)
        ctx = jnp.einsum('bhqk,bhkd->bhqd', attn, v)
        ctx = ctx.transpose(0, 2, 1, 3).reshape(b, n, D_MODEL)
        return ctx @ wo.T + bo

    def _L0_xattn_ref(hidden_states, audio_tokens, attention_mask, Wq, bq, Wk, bk, Wv, bv, Wo, bo, ln_gamma, ln_beta, residual_scale):
        import jax, jax.numpy as jnp
        import numpy as np
        import math
        H = 512
        NH = 16
        HD = H // NH
        EPS_LN = 1e-05
        RES_SCALE_MAX = 0.3

        def _nan_clean(x, lim=10000.0):
            return jnp.nan_to_num(x, nan=0.0, posinf=lim, neginf=-lim)
        B, S, _ = hidden_states.shape
        T = audio_tokens.shape[1]
        hs = _nan_clean(hidden_states).astype(jnp.float32)
        at = _nan_clean(audio_tokens).astype(jnp.float32)

        def proj(x, W, b, L):
            y = x @ W.T + b
            return y.reshape(B, L, NH, HD).transpose(0, 2, 1, 3)
        q = _nan_clean(proj(hs, Wq, bq, S))
        k = _nan_clean(proj(at, Wk, bk, T))
        v = _nan_clean(proj(at, Wv, bv, T))
        scale = max(math.sqrt(HD), 1e-08)
        scores = jnp.einsum('bhsd,bhtd->bhst', q, k) / scale
        scores = jnp.clip(scores, -50.0, 50.0)
        scores = jnp.nan_to_num(scores, nan=0.0, posinf=50.0, neginf=-50.0)
        attend = (attention_mask.astype(jnp.float32) > 0.5)[:, None, None, :]
        scores = jnp.where(attend, scores, -10000.0)
        scores = jnp.clip(scores, -50.0, 50.0)
        probs = jax.nn.softmax(scores, axis=-1)
        probs = jnp.nan_to_num(probs, nan=0.0, posinf=1.0, neginf=0.0)
        probs = probs / (probs.sum(axis=-1, keepdims=True) + 1e-08)
        ctx = jnp.einsum('bhst,bhtd->bhsd', probs, v)
        ctx = ctx.transpose(0, 2, 1, 3).reshape(B, S, H)
        delta = _nan_clean(ctx @ Wo.T + bo)
        rs = jnp.clip(residual_scale, 0.0, RES_SCALE_MAX)
        delta = rs * delta
        mu = delta.mean(axis=-1, keepdims=True)
        var = jnp.mean((delta - mu) ** 2, axis=-1, keepdims=True)
        delta = (delta - mu) / jnp.sqrt(var + EPS_LN) * ln_gamma + ln_beta
        return delta

    def _L0_ffn_ref(hidden_states, ln1_w, ln2_w, Wq, Wk, Wv, Wo, Wr, expert_bias, Wg, Wu, Wd, Wsg, Wsu, Wsd):
        import jax, jax.numpy as jnp
        import numpy as np
        H = 512
        NH = 32
        KVH = 4
        HD = 128
        E = 32
        TOPK = 8
        I = 256
        EPS = 1e-05
        THETA = 10000.0

        def _rmsnorm(x, w, eps=EPS):
            xf = x.astype(jnp.float32)
            var = jnp.mean(xf * xf, axis=-1, keepdims=True)
            return (w * (xf * jax.lax.rsqrt(var + eps))).astype(x.dtype)

        def _rope(x, pos):
            d = x.shape[-1]
            inv_freq = 1.0 / THETA ** (jnp.arange(0, d, 2, dtype=jnp.float32) / d)
            ang = pos.astype(jnp.float32)[:, None] * inv_freq[None, :]
            cos = jnp.cos(ang)[None, :, None, :]
            sin = jnp.sin(ang)[None, :, None, :]
            x1, x2 = jnp.split(x, 2, axis=-1)
            return jnp.concatenate([x1 * cos - x2 * sin, x1 * sin + x2 * cos], axis=-1)
        B, S, _ = hidden_states.shape
        resid = hidden_states
        h = _rmsnorm(hidden_states, ln1_w)
        pos = jnp.arange(S)
        q = (h @ Wq).reshape(B, S, NH, HD)
        k = (h @ Wk).reshape(B, S, KVH, HD)
        v = (h @ Wv).reshape(B, S, KVH, HD)
        q = _rope(q, pos)
        k = _rope(k, pos)
        rep = NH // KVH
        k = jnp.repeat(k, rep, axis=2)
        v = jnp.repeat(v, rep, axis=2)
        scores = jnp.einsum('bqhd,bkhd->bhqk', q, k) / jnp.sqrt(jnp.float32(HD))
        causal = jnp.tril(jnp.ones((S, S), dtype=bool))
        scores = jnp.where(causal[None, None], scores, jnp.float32(-1000000000.0))
        attn = jax.nn.softmax(scores, axis=-1)
        o = jnp.einsum('bhqk,bkhd->bqhd', attn, v).reshape(B, S, NH * HD) @ Wo
        x = resid + o
        resid = x
        h = _rmsnorm(x, ln2_w)
        t = h.reshape(-1, H)
        T = t.shape[0]
        router_scores = jax.nn.sigmoid(t @ Wr)
        _, idx = jax.lax.top_k(router_scores + expert_bias[None, :], TOPK)
        w = jnp.take_along_axis(router_scores, idx, axis=1)
        w = w / jnp.sum(w, axis=-1, keepdims=True)
        wfull = jnp.zeros((T, E), jnp.float32).at[jnp.arange(T)[:, None], idx].set(w)
        g = jnp.einsum('th,ehi->tei', t, Wg)
        u = jnp.einsum('th,ehi->tei', t, Wu)
        act = jax.nn.silu(g) * u
        moe = jnp.einsum('tei,te,eih->th', act, wfull, Wd)
        shared = jax.nn.silu(t @ Wsg) * (t @ Wsu) @ Wsd
        return resid + (moe + shared).reshape(B, S, H)

    def _L1_attn_ref(hidden_states, Wq, Wk, Wv, Wo, learnable_bias, softmax_offset):
        import jax, jax.numpy as jnp
        import numpy as np
        NUM_HEADS = 32
        MAX_BIAS_LENGTH = 256
        ROPE_BASE = 10000.0

        def _rope_cos_sin(seq_len, head_dim, dtype):
            half = head_dim // 2
            inv_freq = 1.0 / ROPE_BASE ** (jnp.arange(0, half, dtype=jnp.float32) / half)
            t = jnp.arange(seq_len, dtype=jnp.float32)
            freqs = jnp.outer(t, inv_freq)
            return (jnp.cos(freqs).astype(dtype), jnp.sin(freqs).astype(dtype))

        def _apply_rope(x, cos, sin):
            half = x.shape[-1] // 2
            x1, x2 = (x[..., :half], x[..., half:])
            c = cos[None, :, None, :]
            s = sin[None, :, None, :]
            return jnp.concatenate([x1 * c - x2 * s, x1 * s + x2 * c], axis=-1)
        B, S, Dm = hidden_states.shape
        H = NUM_HEADS
        D = Dm // H
        scale = D ** (-0.5)
        q = (hidden_states @ Wq.T).reshape(B, S, H, D)
        k = (hidden_states @ Wk.T).reshape(B, S, H, D)
        v = (hidden_states @ Wv.T).reshape(B, S, H, D)
        cos, sin = _rope_cos_sin(S, D, q.dtype)
        q = _apply_rope(q, cos, sin)
        k = _apply_rope(k, cos, sin)
        q = q.transpose(0, 2, 1, 3)
        k = k.transpose(0, 2, 1, 3)
        v = v.transpose(0, 2, 1, 3)
        scores = jnp.einsum('bhid,bhjd->bhij', q, k) * scale
        i = jnp.arange(S)[:, None]
        j = jnp.arange(S)[None, :]
        diag = i - j
        causal = diag >= 0
        in_band = causal & (diag < MAX_BIAS_LENGTH)
        bias = jnp.where(in_band, learnable_bias[:, jnp.clip(diag, 0, MAX_BIAS_LENGTH - 1)], 0.0)
        scores = scores + bias[None]
        scores = jnp.where(causal[None, None], scores, -jnp.inf)
        off = softmax_offset[None, :, None]
        m = jnp.maximum(jnp.max(scores, axis=-1), off)
        p = jnp.exp(scores - m[..., None])
        denom = jnp.sum(p, axis=-1) + jnp.exp(off - m)
        out = jnp.einsum('bhij,bhjd->bhid', p, v) / denom[..., None]
        out = out.transpose(0, 2, 1, 3).reshape(B, S, Dm)
        return out @ Wo.T

    def _L1_xattn_ref(hidden_states, memory_tokens, memory_mask, norm_w, wq, wk, wv, wo, wg):
        import jax, jax.numpy as jnp
        import numpy as np
        H = 512
        NH = 16
        HD = H // NH
        EPS = 1e-06

        def rmsnorm(x, w, eps=EPS):
            var = jnp.mean(x * x, axis=-1, keepdims=True)
            return x * jax.lax.rsqrt(var + eps) * w
        B, L, C = hidden_states.shape
        M = memory_tokens.shape[1]
        scale = HD ** (-0.5)
        x = rmsnorm(hidden_states, norm_w)
        q = (x @ wq.T).reshape(B, L, NH, HD)
        k = (memory_tokens @ wk.T).reshape(B, M, NH, HD)
        v = (memory_tokens @ wv.T).reshape(B, M, NH, HD)
        attn = jnp.einsum('blhd,bmhd->bhlm', q, k) * scale
        attn = jnp.where(memory_mask[:, None, None, :], attn, -jnp.inf)
        attn = jax.nn.softmax(attn, axis=-1)
        attn = jnp.nan_to_num(attn, nan=0.0)
        out = jnp.einsum('bhlm,bmhd->blhd', attn, v).reshape(B, L, C)
        out = out @ wo.T
        gate = jax.nn.sigmoid(x @ wg.T)
        return gate * out

    def _L1_ffn_ref(x, w_gate, w_up, w_down):
        import jax, jax.numpy as jnp
        import numpy as np
        DIM_IN = 512
        DIM_HIDDEN = 2048
        gate = jnp.einsum('bsd,hd->bsh', x, w_gate)
        up = jnp.einsum('bsd,hd->bsh', x, w_up)
        gated = jax.nn.silu(gate) * up
        return jnp.einsum('bsh,dh->bsd', gated, w_down)
    x = x + _L0_attn_ref(_layernorm(x, axis=-1), L0_attn_wq, L0_attn_bq, L0_attn_wk, L0_attn_bk, L0_attn_wv, L0_attn_bv, L0_attn_wo, L0_attn_bo)
    x = x + _L0_xattn_ref(_layernorm(x, axis=-1), ctx_2048, mask_BxS2_ik0, L0_xattn_Wq, L0_xattn_bq, L0_xattn_Wk, L0_xattn_bk, L0_xattn_Wv, L0_xattn_bv, L0_xattn_Wo, L0_xattn_bo, L0_xattn_ln_gamma, L0_xattn_ln_beta, L0_xattn_residual_scale)
    x = x + _L0_ffn_ref(_layernorm(x, axis=-1), L0_ffn_ln1_w, L0_ffn_ln2_w, L0_ffn_Wq, L0_ffn_Wk, L0_ffn_Wv, L0_ffn_Wo, L0_ffn_Wr, L0_ffn_expert_bias, L0_ffn_Wg, L0_ffn_Wu, L0_ffn_Wd, L0_ffn_Wsg, L0_ffn_Wsu, L0_ffn_Wsd)
    x = x + _L1_attn_ref(_layernorm(x, axis=-1), L1_attn_Wq, L1_attn_Wk, L1_attn_Wv, L1_attn_Wo, L1_attn_learnable_bias, L1_attn_softmax_offset)
    x = x + _L1_xattn_ref(_layernorm(x, axis=-1), ctx_2048, mask_BxS2_bk0, L1_xattn_norm_w, L1_xattn_wq, L1_xattn_wk, L1_xattn_wv, L1_xattn_wo, L1_xattn_wg)
    x = x + _L1_ffn_ref(_layernorm(x, axis=-1), L1_ffn_w_gate, L1_ffn_w_up, L1_ffn_w_down)
    return x

_drawn_inputs = setup_inputs


def setup_inputs(seed=0):
    import zlib

    import numpy as np

    out = dict(_drawn_inputs(seed))
    spreads = {'L0_xattn_bq': (0.0, 0.279),
     'L0_xattn_bk': (0.0, 2.0),
     'L0_xattn_bv': (0.0, 0.1),
     'L0_xattn_bo': (0.0, 0.1),
     'L0_xattn_ln_gamma': (1.0, 0.2),
     'L0_xattn_ln_beta': (0.0, 0.1),
     'L0_ffn_ln1_w': (1.0, 0.2),
     'L0_ffn_ln2_w': (1.0, 0.6),
     'L1_attn_softmax_offset': (0.0, 2.0),
     'L1_xattn_norm_w': (1.0, 0.6)}
    factors = {'L0_attn_wq': 3.348,
     'L0_attn_bq': 8.0,
     'L0_attn_wk': 2.972,
     'L0_attn_bk': 64.0,
     'L0_attn_bv': 4.967,
     'L0_attn_bo': 3.099,
     'L0_ffn_Wq': 8.0,
     'L0_ffn_Wk': 8.0,
     'L0_ffn_Wr': 8.0,
     'L0_ffn_expert_bias': 8.0,
     'L0_ffn_Wg': 8.0,
     'L0_ffn_Wu': 8.0,
     'L0_ffn_Wd': 8.0,
     'L0_ffn_Wsg': 4.104,
     'L0_ffn_Wsu': 3.99,
     'L0_ffn_Wsd': 3.98,
     'L1_attn_learnable_bias': 64.0,
     'L1_attn_Wq': 7.331,
     'L1_attn_Wk': 7.287,
     'L1_xattn_wq': 6.453,
     'L1_xattn_wk': 6.494,
     'L1_xattn_wv': 3.377,
     'L1_xattn_wo': 3.33,
     'L1_xattn_wg': 7.279,
     'L1_ffn_w_gate': 8.0,
     'L1_ffn_w_up': 8.0,
     'L1_ffn_w_down': 8.0}
    for name, (base, spread) in spreads.items():
        noise = np.random.default_rng([zlib.crc32(name.encode()), seed]).standard_normal(out[name].shape)
        drawn = base * np.exp(spread * noise) if base else spread * noise
        out[name] = jnp.asarray(drawn.astype(out[name].dtype))
    for name, factor in factors.items():
        out[name] = (out[name] * factor).astype(out[name].dtype)
    return out
```

```python
from collections import namedtuple
from contextlib import ExitStack, contextmanager

import numpy as np

import concourse.bass as bass
from concourse import mybir

F32 = mybir.dt.float32
F32R = mybir.dt.float32r
BF16 = mybir.dt.bfloat16
I32 = mybir.dt.int32
U8 = mybir.dt.uint8
ALU = mybir.AluOpType
ACT = mybir.ActivationFunctionType
AX_X = mybir.AxisListType.X

P = 128
B, S, D = 8, 112, 512
KC = D // P
T = B * S
NH = 2
HB = B // NH
HT = T // NH
S2 = 375
CK = 3
CW = S2 // CK
S2P = S2 + 1
PVW = 100
NEG = -1.0e30
ROPE_BASE = 10000.0
E_MOE, TOPK, EI = 32, 8, 256
NC = EI // P
EW = 2 * KC * EI + NC * D
FFN = 2048
NG = 4
GQ = 8

CONSTS = {}
_at = 0
for _name, _w in (("ident", P), ("hm32", 4), ("hm8", 8), ("causal", S),
                  ("cos16", S), ("sin16", S), ("cos128", S), ("sin128", S), ("power", B)):
    CONSTS[_name] = (_at, _w)
    _at += _w
NCONST = _at
ROWS = {}
_at = 0
for _name, _w in (("a_bv", D), ("a_bo", D), ("x_bv", D), ("x_bo", D), ("gamma", D), ("beta", D),
                  ("ln1_w", D), ("ln2_w", D), ("norm_w", D), ("expert_bias", E_MOE),
                  ("offset", 32), ("res_scale", 1)):
    ROWS[_name] = (_at, _w)
    _at += _w
NROW = _at


@contextmanager
def semaphores(nc, name):
    taken = []

    def sem(n):
        taken.append(nc.alloc_semaphore(f"{name}_{n}"))
        return taken[-1]

    yield sem
    nc.clear_and_free_semaphores(taken)
    nc.all_engine_barrier()


def normalise(nc, g, name, src, kind, eps2=0.0, w=None, keep=None):
    with ExitStack() as ctx:
        def sb(n, shape):
            return ctx.enter_context(nc.sbuf_tensor(f"{name}_{n}", shape, F32))

        sem = ctx.enter_context(semaphores(nc, name))

        h = keep if keep is not None else (src if kind == "rms" else sb("h", [S, B, D]))
        y = h if kind == "ln" else sb("y", [S, B, D])
        junk = sb("junk", [S, D])
        stats = sb("stats", [S, B, 6])
        mv = sb("mv", [S, B, 2])
        var = sb("var", [S, B])
        rstd = sb("rstd", [S, B])
        ssq = sb("ssq", [S, B])
        ms = sb("ms", [S, B])
        rrms = sb("rrms", [S, B])
        stats_done, aggr_done, var_done, rstd_done, h_done = map(sem, ("stats", "aggr", "var", "rstd", "h"))
        ssq_done, ms_done, rrms_done, y_done = map(sem, ("ssq", "ms", "rrms", "y"))
        tr_done, hi_done, lo_done = map(sem, ("tr", "hi", "lo"))
        ready = h_done if kind == "ln" else y_done
        block = ctx.enter_context(nc.Block())

        @block.vector
        def _(dve):
            if kind != "rms":
                for b in range(B):
                    dve.bn_stats(stats[:, b, :], src[:, b, :]).then_inc(stats_done, 1)
                for b in range(B):
                    dve.wait_ge(stats_done, b + 1)
                    dve.bn_aggr(mv[:, b, :], stats[:, b, :]).then_inc(aggr_done, 1)
                dve.wait_ge(aggr_done, B)
                dve.tensor_scalar(var[:, :], mv[:, :, 1], 1e-5, None, ALU.add).then_inc(var_done, 1)
                dve.wait_ge(rstd_done, 1)
                for b in range(B):
                    dve.tensor_scalar(h[:, b, :], src[:, b, :], mv[:, b, 0:1], rstd[:, b:b + 1],
                                      ALU.subtract, ALU.mult).then_inc(h_done, 1)
            if kind != "ln":
                dve.wait_ge(ssq_done, B)
                dve.tensor_scalar(ms[:, :], ssq[:, :], 1.0 / D, eps2, ALU.mult, ALU.add).then_inc(ms_done, 1)
                dve.wait_ge(rrms_done, 1)
                for b in range(B):
                    dve.scalar_tensor_tensor(y[:, b, :], h[:, b, :], rrms[:, b:b + 1], w,
                                             ALU.mult, ALU.mult).then_inc(y_done, 1)
            for b in range(B):
                dve.wait_ge(hi_done, b + 1)
                dve.tensor_tensor(g.hT_lo[:, :, b * S:(b + 1) * S],
                                  g.bank[b % 4][:, 0:KC * S].rearrange("p (k s) -> p k s", k=KC),
                                  g.hT_hi[:, :, b * S:(b + 1) * S].bitcast(F32),
                                  ALU.subtract).then_inc(lo_done, 1)

        @block.gpsimd
        def _(pool):
            if kind != "rms":
                pool.wait_ge(var_done, 1)
                pool.tensor_tensor(rstd[:, :], var[:, :], g.const("power")[0:S, :], ALU.pow).then_inc(rstd_done, 1)
            if kind != "ln":
                pool.wait_ge(ms_done, 1)
                pool.tensor_tensor(rrms[:, :], ms[:, :], g.const("power")[0:S, :], ALU.pow).then_inc(rrms_done, 1)

        @block.scalar
        def _(act):
            if kind != "ln":
                for b in range(B):
                    if kind == "ln_rms":
                        act.wait_ge(h_done, b + 1)
                    if b:
                        act.wait_ge(ssq_done, b)
                    act.activation(junk[:, :], h[:, b, :], ACT.Square,
                                   accum_out=ssq[:, b:b + 1]).then_inc(ssq_done, 1)
            for b in range(B):
                act.wait_ge(tr_done, b + 1)
                act.activation(g.hT_hi[:, :, b * S:(b + 1) * S],
                               g.bank[b % 4][:, 0:KC * S].rearrange("p (k s) -> p k s", k=KC),
                               ACT.Copy).then_inc(hi_done, 1)

        @block.tensor
        def _(pe):
            for b in range(B):
                pe.wait_ge(ready, b + 1)
                if b >= 4:
                    pe.wait_ge(lo_done, b - 3)
                for k in range(KC):
                    t = pe.transpose(g.bank[b % 4][:, k * S:(k + 1) * S], y[:, b, k * P:(k + 1) * P],
                                     g.const("ident")[0:S, 0:S])
                t.then_inc(tr_done, 1)


def mm3(pe, out, w_hi, w_lo, x_hi, x_lo, first, last):
    pe.matmul(out, w_hi, x_hi, start=first, stop=False)
    pe.matmul(out, w_hi, x_lo, start=False, stop=False)
    return pe.matmul(out, w_lo, x_hi, start=False, stop=last)


def project(nc, g, name, w_dram, M, out, bias=None, scale=None, rope=None, value=None):
    with ExitStack() as ctx:
        def sb(n, shape, dt=F32):
            return ctx.enter_context(nc.sbuf_tensor(f"{name}_{n}", shape, dt))

        sem = ctx.enter_context(semaphores(nc, name))

        raw = sb("raw", [P, 2, KC * P])
        w_hi = sb("w_hi", [P, 2, KC * P], F32R)
        w_lo = sb("w_lo", [P, 2, KC * P], F32R)
        raw_in = [sem("raw_in0"), sem("raw_in1")]
        hi_done, lo_done, mm_done, out_done = map(sem, ("hi", "lo", "mm", "out"))
        if rope:
            turned = sb("turned", [P, 4, HT])
            cosd = sb("cosd", [P, 4, HT])
            swap_done, sin_done, cos_done = map(sem, ("swap", "sin", "cos"))
        if value:
            v_dram, v_out, heads, hd, v_bias = value
            v_raw = sb("v_raw", [P, KC, D])
            v_hi = sb("v_hi", [P, KC, D], F32R)
            v_lo = sb("v_lo", [P, KC, D], F32R)
            v_in, v_set, v_hi_done, v_lo_done, v_mm, v_done = map(
                sem, ("v_in", "v_set", "v_hi", "v_lo", "v_mm", "v_done"))
        block = ctx.enter_context(nc.Block())

        def tokens(ap):
            return ap.rearrange("p (b s) -> p b s", b=HB)

        def table(ap):
            return ap.unsqueeze(1).broadcast_to([P, HB, S])

        @block.sync
        def _(sp):
            for u in range(2):
                sp.dma_start(raw[:, u, :], w_dram[u]).then_inc(raw_in[u], 16)
            if value:
                sp.dma_start(v_raw[:, :, :], v_dram).then_inc(v_in, 16)
            if M > 2:
                with sp.Fori(0, M // 2 - 1) as i:
                    for u in range(2):
                        sp.wait_ge(lo_done, 2 * i + u + 1)
                        sp.dma_start(raw[:, u, :], w_dram[2 * i + u + 2]).then_inc(raw_in[u], 16)

        @block.scalar
        def _(act):
            with act.Fori(0, M // 2) as i:
                for u in range(2):
                    act.wait_ge(raw_in[u], 16 * i + 16)
                    act.wait_ge(mm_done, 4 * i + 2 * u + 2)
                    act.activation(w_hi[:, u, :], raw[:, u, :], ACT.Copy).then_inc(hi_done, 1)
                if rope:
                    for u in range(2):
                        for t in range(NH):
                            r = 2 * u + t
                            act.wait_ge(mm_done, 4 * i + r + 5)
                            act.wait_ge(out_done, 4 * i + r + 1)
                            act.activation(turned[0:64, r, :], g.bank[r][64:P, 0:HT], ACT.Copy).then_inc(swap_done, 1)
                            act.activation(turned[64:P, r, :], g.bank[r][0:64, 0:HT], ACT.Copy).then_inc(swap_done, 1)
            if value:
                act.wait_ge(v_in, 16)
                act.activation(v_hi[:, :, :], v_raw[:, :, :], ACT.Copy).then_inc(v_hi_done, 1)
            if value and heads is None:
                for b in range(B):
                    act.wait_ge(v_mm, b + 1)
                    act.activation(v_out[:, b, :], g.bank[4 + b % 4][0:S, :], ACT.Sigmoid).then_inc(v_done, 1)

        @block.gpsimd
        def _(pool):
            if value and hd not in (None, P):
                pool.memset(v_out[:, :, :], 0.0).then_inc(v_set, 1)
                pool.wait_ge(v_set, 1)
                pool.memset(v_out[:, :, 0:heads * (hd + 1)].rearrange("p b (h e) -> p b h e", e=hd + 1)[:, :, :, hd],
                            1.0).then_inc(v_set, 1)
            with pool.Fori(0, M // 2) as i:
                for u in range(2):
                    pool.wait_ge(hi_done, 2 * i + u + 1)
                    pool.wait_ge(mm_done, 4 * i + 2 * u + 2)
                    pool.tensor_tensor(w_lo[:, u, :], raw[:, u, :], w_hi[:, u, :].bitcast(F32),
                                       ALU.subtract).then_inc(lo_done, 1)
                if rope:
                    for r in range(4):
                        pool.wait_ge(swap_done, 8 * i + 2 * r + 2)
                        pool.tensor_tensor(tokens(turned[:, r, :]), tokens(turned[:, r, :]), table(rope[1]),
                                           ALU.mult).then_inc(sin_done, 1)

        @block.vector
        def _(dve):
            dve.sem_inc(out_done, 4)
            with dve.Fori(0, M // 2) as i:
                for u in range(2):
                    for t in range(NH):
                        r = 2 * u + t
                        dve.wait_ge(mm_done, 4 * i + r + 5)
                        dst = out[:, 2 * i + u, t * HT:(t + 1) * HT]
                        if rope:
                            dve.wait_ge(swap_done, 8 * i + 2 * r + 2)
                            dve.tensor_tensor(tokens(cosd[:, r, :]), tokens(g.bank[r][:, 0:HT]), table(rope[0]),
                                              ALU.mult).then_inc(cos_done, 1)
                        elif bias is not None:
                            dve.tensor_scalar(dst, g.bank[r][:, 0:HT], bias[:, bass.ds(2 * i + u, 1)], scale or 1.0,
                                              ALU.add, ALU.mult).then_inc(out_done, 1)
                        else:
                            dve.tensor_scalar(dst, g.bank[r][:, 0:HT], scale or 1.0, None,
                                              ALU.mult).then_inc(out_done, 1)
                    if rope:
                        for t in range(NH):
                            r = 2 * u + t
                            dve.wait_ge(sin_done, 4 * i + r + 1)
                            dve.wait_ge(cos_done, 4 * i + r + 1)
                            dve.tensor_tensor(out[:, 2 * i + u, t * HT:(t + 1) * HT], cosd[:, r, :], turned[:, r, :],
                                              ALU.add).then_inc(out_done, 1)
            if value:
                dve.wait_ge(v_hi_done, 1)
                dve.tensor_tensor(v_lo[:, :, :], v_raw[:, :, :], v_hi[:, :, :].bitcast(F32),
                                  ALU.subtract).then_inc(v_lo_done, 1)
                if hd not in (None, P):
                    dve.wait_ge(v_set, 2)
                for b in range(B if heads is not None else 0):
                    dve.wait_ge(v_mm, b + 1)
                    if hd == P:
                        dst = v_out[0:S, b, :].rearrange("p (h e) -> p h e", e=hd)
                    else:
                        dst = v_out[0:S, b, 0:heads * (hd + 1)].rearrange("p (h e) -> p h e", e=hd + 1)[:, :, 0:hd]
                    src = g.bank[4 + b % 4][0:S, :].rearrange("p (h e) -> p h e", e=hd)
                    if v_bias is not None:
                        dve.tensor_tensor(dst, src, v_bias.rearrange("p (h e) -> p h e", e=hd),
                                          ALU.add).then_inc(v_done, 1)
                    else:
                        dve.tensor_copy(dst, src).then_inc(v_done, 1)

        @block.tensor
        def _(pe):
            pe.sem_inc(mm_done, 4)
            with pe.Fori(0, M // 2) as i:
                for u in range(2):
                    pe.wait_ge(lo_done, 2 * i + u + 1)
                    for t in range(NH):
                        r = 2 * u + t
                        pe.wait_ge(out_done, 4 * i + r + 1)
                        for k in range(KC):
                            x = mm3(pe, g.bank[r][:, 0:HT], w_hi[:, u, k * P:(k + 1) * P], w_lo[:, u, k * P:(k + 1) * P],
                                    g.hT_hi[:, k, t * HT:(t + 1) * HT], g.hT_lo[:, k, t * HT:(t + 1) * HT],
                                    k == 0, k == KC - 1)
                        x.then_inc(mm_done, 1)
            if value:
                pe.wait_ge(v_lo_done, 1)
                for b in range(B):
                    if b >= 4:
                        pe.wait_ge(v_done, b - 3)
                    for k in range(KC):
                        x = mm3(pe, g.bank[4 + b % 4][0:S, :], g.hT_hi[:, k, b * S:(b + 1) * S],
                                g.hT_lo[:, k, b * S:(b + 1) * S], v_hi[:, k, :], v_lo[:, k, :], k == 0, k == KC - 1)
                    x.then_inc(v_mm, 1)


def self_attention(nc, g, name, x, qT, kT, v, heads, hd, scale, head_mask, bias, wo_dram, wo_bias=None, sink=None):
    G = heads // 4
    per_chunk = heads // KC // 4
    NK = S + 1 if sink is not None else S
    VE = hd + 1
    with ExitStack() as ctx:
        def sb(n, shape, dt=F32):
            return ctx.enter_context(nc.sbuf_tensor(f"{name}_{n}", shape, dt))

        sem = ctx.enter_context(semaphores(nc, name))

        wo = sb("wo", [P, KC, D])
        q_now = sb("q_now", [P, KC, S])
        k_diag = sb("k_diag", [P, 4, 4, S])
        s_rows = sb("s_rows", [S, G if sink is not None else 4, 4, NK])
        p_rows = sb("p_rows", [S, 4, 4, NK])
        pT = sb("pT", [NK, 2, 4, S])
        top = sb("top", [S, 4, 4])
        o_rows = sb("o_rows", [S, heads, VE])
        r_den = sb("r_den", [S, heads])
        o_norm = sb("o_norm", [S, D])
        oT = sb("oT", [P, KC, S])
        ps_s = g.bank[0:2]
        ps_t = g.bank[2:4]
        ps_o = g.bank[4:6]
        ps_c = g.bank[6]
        ps_y = g.bank[7]
        (wo_in, kd_done, q_done, s_done, sr_done, top_done, sub_done, exp_done, t_done, pT_done, pv_done, or_done,
         den_done, on_done, c_done, oT_done, y_done, add_done, bo_done, sink_done, free_seen) = map(sem, (
             "wo_in", "kd", "q", "s", "sr", "top", "sub", "exp", "t", "pT", "pv", "or", "den", "on", "c", "oT",
             "y", "add", "bo", "sink", "free_seen"))
        block = ctx.enter_context(nc.Block())

        def sr(grp):
            return s_rows[:, grp if sink is not None else grp % 4]

        def each_batch(e, body):
            body(0, True, False)
            with e.Fori(1, B - 1) as b:
                body(b, False, False)
            body(B - 1, False, True)

        @block.sync
        def _(sp):
            sp.dma_start(wo[:, :, :], wo_dram).then_inc(wo_in, 16)

        @block.gpsimd
        def _(pool):
            def diagonal(b, grp):
                c = grp // per_chunk
                j0 = 4 * (grp % per_chunk)
                pool.tensor_tensor(
                    k_diag[:, grp % 4], kT[:, c, bass.ds(b * S, S)].unsqueeze(1).broadcast_to([P, 4, S]),
                    head_mask[:, j0:j0 + 4].unsqueeze(2).broadcast_to([P, 4, S]), ALU.mult).then_inc(kd_done, 1)

            def subtract(n, grp):
                pool.wait_ge(top_done, n + 1)
                pool.tensor_tensor(p_rows[:, grp % 4], sr(grp),
                                   top[:, grp % 4, :].unsqueeze(2).broadcast_to([S, 4, NK]),
                                   ALU.subtract).then_inc(sub_done, 1)

            def body(b, first, last):
                if wo_bias is not None:
                    pool.tensor_tensor(x[:, bass.ds(b, 1), :], x[:, bass.ds(b, 1), :], wo_bias.unsqueeze(1),
                                       ALU.add).then_inc(bo_done, 1)
                for grp in range(G):
                    n = b * G + grp
                    if not (last and grp + 4 >= G):
                        pool.wait_ge(s_done, n + 1)
                        pool.sem_inc(free_seen, 1)
                        diagonal(b + (grp + 4) // G, (grp + 4) % G)
                    if not (last and grp + 2 >= G):
                        subtract(n + 2, (grp + 2) % G)

            if sink is not None:
                pool.tensor_copy(s_rows[:, :, :, S], sink.rearrange("p (g h) -> p g h", h=4)).then_inc(sink_done, 1)
            for grp in range(4):
                diagonal(0, grp)
            for grp in range(2):
                if sink is not None and grp == 0:
                    pool.wait_ge(sink_done, 1)
                subtract(grp, grp)
            each_batch(pool, body)

        @block.scalar
        def _(act):
            def take_q(b):
                act.activation(q_now[:, :, :], qT[:, :, bass.ds(b * S, S)], ACT.Copy).then_inc(q_done, 1)

            def exponent(n, grp):
                act.wait_ge(sub_done, n + 1)
                act.activation(p_rows[:, grp % 4], p_rows[:, grp % 4], ACT.Exp).then_inc(exp_done, 1)

            def body(b, first, last):
                for grp in range(G):
                    n = b * G + grp
                    act.wait_ge(t_done, n + 1)
                    act.activation(pT[:, grp % 2], ps_t[grp % 2][0:NK, 0:4 * S].rearrange("p (h s) -> p h s", h=4),
                                   ACT.Copy).then_inc(pT_done, 1)
                    if grp == G - 2 and not last:
                        act.wait_ge(s_done, n + 2)
                        take_q(b + 1)
                    if not (last and grp + 1 >= G):
                        exponent(n + 1, (grp + 1) % G)
                    if grp == 1 and not first:
                        collect(b - 1)

            def collect(b):
                act.wait_ge(c_done, b + 1)
                act.activation(oT[:, :, :], ps_c[:, 0:KC * S].rearrange("p (k s) -> p k s", k=KC),
                               ACT.Copy).then_inc(oT_done, 1)

            take_q(0)
            exponent(0, 0)
            each_batch(act, body)
            collect(B - 1)

        @block.vector
        def _(dve):
            def scale_bias_max(n, grp):
                dve.wait_ge(s_done, n + 1)
                dve.scalar_tensor_tensor(sr(grp)[:, :, 0:S], ps_s[grp % 2][0:S, 0:4 * S].rearrange("p (h s) -> p h s", h=4),
                                         scale, bias(grp), ALU.mult, ALU.add).then_inc(sr_done, 1)
                dve.wait_ge(sr_done, n + 1)
                dve.tensor_reduce(top[:, grp % 4, :], sr(grp), AX_X, ALU.max).then_inc(top_done, 1)

            def add(b):
                dve.wait_ge(y_done, b + 1)
                dve.wait_ge(bo_done, b + 1) if wo_bias is not None else None
                dve.tensor_tensor(x[:, bass.ds(b, 1), :], ps_y[0:S, :].unsqueeze(1), x[:, bass.ds(b, 1), :],
                                  ALU.add).then_inc(add_done, 1)

            def body(b, first, last):
                for grp in range(G):
                    n = b * G + grp
                    if not (last and grp + 2 >= G):
                        scale_bias_max(n + 2, (grp + 2) % G)
                    dve.wait_ge(pv_done, n + 1)
                    dve.tensor_copy(o_rows[:, 4 * grp:4 * grp + 4, :],
                                    ps_o[grp % 2][0:S, 0:4 * PVW].rearrange("p (h e) -> p h e", h=4)[:, :, 0:VE]
                                    ).then_inc(or_done, 1)
                    if grp == 3 and not first:
                        add(b - 1)
                dve.wait_ge(or_done, b * G + G + 2)
                dve.reciprocal(r_den[:, :], o_rows[:, :, hd]).then_inc(den_done, 1)
                dve.wait_ge(den_done, b + 1)
                dve.tensor_tensor(o_norm[:, :].rearrange("p (h e) -> p h e", h=heads), o_rows[:, :, 0:hd],
                                  r_den[:, :].unsqueeze(2).broadcast_to([S, heads, hd]), ALU.mult).then_inc(on_done, 1)

            dve.sem_inc(or_done, 2)
            if sink is not None:
                dve.wait_ge(sink_done, 1)
            for grp in range(2):
                scale_bias_max(grp, grp)
            each_batch(dve, body)
            add(B - 1)

        @block.tensor
        def _(pe):
            def scores(n, b, grp):
                pe.wait_ge(kd_done, n + 1)
                pe.wait_ge(q_done, b + 1)
                pe.matmul(ps_s[grp % 2][0:S, 0:4 * S], q_now[:, grp // per_chunk, :], k_diag[:, grp % 4],
                          start=True, stop=True).then_inc(s_done, 1)

            def context_rows(b):
                pe.wait_ge(on_done, b + 1)
                for k in range(KC):
                    t = pe.transpose(ps_c[:, k * S:(k + 1) * S], o_norm[:, k * P:(k + 1) * P],
                                     g.const("ident")[0:S, 0:S])
                t.then_inc(c_done, 1)

            def out_rows(b):
                pe.wait_ge(oT_done, b + 1)
                for k in range(KC):
                    y = pe.matmul(ps_y[0:S, :], oT[:, k, :], wo[:, k, :], start=(k == 0), stop=(k == KC - 1))
                y.then_inc(y_done, 1)

            def body(b, first, last):
                for grp in range(G):
                    n = b * G + grp
                    pe.wait_ge(exp_done, n + 1)
                    for j in range(4):
                        t = pe.transpose(ps_t[grp % 2][0:NK, j * S:(j + 1) * S], p_rows[:, grp % 4, j, :],
                                         g.const("ident")[0:S, 0:S])
                    t.then_inc(t_done, 1)
                    if not (last and grp + 2 >= G):
                        pe.wait_ge(sr_done, n + 1)
                        scores(n + 2, b + (grp + 2) // G, (grp + 2) % G)
                    if grp == 1 and not first:
                        context_rows(b - 1)
                    if grp == 2 and not first:
                        out_rows(b - 1)
                    pe.wait_ge(pT_done, n + 1)
                    pe.wait_ge(or_done, n + 1)
                    for j in range(4):
                        h = 4 * grp + j
                        o = pe.matmul(ps_o[grp % 2][0:S, j * PVW:(j + 1) * PVW], pT[:, grp % 2, j, :],
                                      v[0:NK, bass.ds(b, 1), VE * h:VE * h + PVW], start=True, stop=True)
                    o.then_inc(pv_done, 1)

            pe.wait_ge(wo_in, 16)
            for grp in range(2):
                scores(grp, 0, grp)
            each_batch(pe, body)
            context_rows(B - 1)
            out_rows(B - 1)


def cross_attention(nc, g, name, x, qT, ctx_dram, wk_dram, wv_dram, wo_dram, kind, k_bias=None, v_bias=None,
                    mask_cols=None, mask_row=None, gate=None, norm=None):
    H, HD, VE = 16, 32, 33
    clip = kind == "clip"
    with ExitStack() as ctx:
        def sb(n, shape, dt=F32):
            return ctx.enter_context(nc.sbuf_tensor(f"{name}_{n}", shape, dt))

        sem = ctx.enter_context(semaphores(nc, name))

        w_raw = sb("w_raw", [P, 2, KC * D])
        w_hi = sb("w_hi", [P, 2, KC, D], F32R)
        w_lo = sb("w_lo", [P, 2, KC, D], F32R)
        wo = sb("wo", [P, KC, D])
        c_raw = sb("c_raw", [P, KC, S2P])
        c_hi = sb("c_hi", [P, KC, S2P], F32R)
        c_lo = sb("c_lo", [P, KC, S2P], F32R)
        kT = sb("kT", [P, KC, S2P])
        v = sb("v", [CW, CK, vw(H, HD)])
        q_diag = sb("q_diag", [P, KC, 4, S])
        o_rows = sb("o_rows", [S, H, VE])
        r_den = sb("r_den", [S, H])
        o_norm = sb("o_norm", [S, D])
        oT = sb("oT", [P, KC, S])
        y_rows = sb("y_rows", [S, D])
        (w_in, wo_in, w_hi_done, w_lo_done, c_in, c_hi_done, c_lo_done, pad_done, v_set, kv_mm, kv_done, qd_done,
         s_done, exp_done, pv_done, or_done, den_done, r_done, on_done, c_done, oT_done, y_done, add_done,
         rows_done, one_done, free_seen, st_seen) = map(sem, (
             "w_in", "wo_in", "w_hi", "w_lo", "c_in", "c_hi", "c_lo", "pad", "v_set", "kv_mm", "kv", "qd", "s", "exp",
             "pv", "or", "den", "r", "on", "c", "oT", "y", "add", "rows", "one", "free_seen", "st_seen"))
        if clip:
            s_clip = sb("s_clip", [CW, CK, 4, S])
            pT = sb("pT", [CW, 2, CK, 4, S])
            stats = sb("stats", [S, 6])
            mv = sb("mv", [S, 2])
            var = sb("var", [S, 1])
            rstd = sb("rstd", [S, 1])
            scaled = sb("scaled", [S, D])
            clip_done, beta_done, st_done, mv_done, var_done, rstd_done, sc_done = map(
                sem, ("clip", "beta", "st", "mv", "var", "rstd", "sc"))
            ps_s, ps_kv = g.bank[0:3], g.bank[3:5]
        else:
            p_rows = sb("p_rows", [S, 2, S2])
            pT = sb("pT", [CW, 2, CK, S])
            n_top = sb("n_top", [S, H])
            one_row = sb("one_row", [1, S], BF16)
            top_done, t_done, pT_done = map(sem, ("top", "t", "pT"))
            ps_s, ps_t = g.bank[0:2], g.bank[2:4]
            ps_kv = ps_t
        ps_o, ps_y = g.bank[5:7], g.bank[7]
        SU = CK * KC if clip else H
        S0, KV0, OR0 = SU, 2, 2
        block = ctx.enter_context(nc.Block())

        def each_batch(e, body):
            body(0, True, False)
            with e.Fori(1, B - 1) as b:
                body(b, False, False)
            body(B - 1, False, True)

        @block.sync
        def _(sp):
            sp.dma_start(w_raw[:, 0, :], wk_dram).then_inc(w_in, 16)
            sp.dma_start(c_raw[:, :, 0:S2], ctx_dram[0]).then_inc(c_in, 16)
            sp.dma_start(w_raw[:, 1, :], wv_dram).then_inc(w_in, 16)
            sp.dma_start(wo[:, :, :], wo_dram).then_inc(wo_in, 16)
            with sp.Fori(0, B - 1) as b:
                sp.wait_ge(c_lo_done, b + 1)
                sp.dma_start(c_raw[:, :, 0:S2], ctx_dram[bass.ds(b + 1, 1)].squeeze(0)).then_inc(c_in, 16)

        @block.gpsimd
        def _(pool):
            def split_low(b):
                pool.wait_ge(c_hi_done, b + 1)
                pool.tensor_tensor(c_lo[:, :, :], c_raw[:, :, :], c_hi[:, :, :].bitcast(F32),
                                   ALU.subtract).then_inc(c_lo_done, 1)

            def body(b, first, last):
                for c in range(KC):
                    pool.wait_ge(s_done, SU * b + (SU // KC) * (c + 1))
                    pool.sem_inc(free_seen, 1)
                    pool.tensor_tensor(q_diag[:, c], qT[:, c, bass.ds(b * S, S)].unsqueeze(1).broadcast_to([P, 4, S]),
                                       g.const("hm32").unsqueeze(2).broadcast_to([P, 4, S]),
                                       ALU.mult).then_inc(qd_done, 1)
                if clip:
                    pool.tensor_tensor(x[:, bass.ds(b, 1), :], x[:, bass.ds(b, 1), :], norm.beta.unsqueeze(1),
                                       ALU.add).then_inc(beta_done, 1)
                    if not first:
                        root(b - 1)
                if not last:
                    split_low(b + 1)

            def root(b):
                pool.wait_ge(var_done, b + 1)
                pool.tensor_tensor(rstd[:, :], var[:, :], g.const("power")[0:S, 0:1], ALU.pow).then_inc(rstd_done, 1)

            pool.memset(c_raw[:, :, S2:S2P], 0.0).then_inc(pad_done, 1)
            pool.memset(v[:, :, :], 0.0).then_inc(v_set, 1)
            pool.wait_ge(v_set, 1)
            pool.memset(v[:, :, 0:H * VE].rearrange("p c (h e) -> p c h e", e=VE)[:, :, :, HD], 1.0).then_inc(v_set, 1)
            if not clip:
                pool.memset(one_row[:, :], 1.0).then_inc(v_set, 1)
            for i in range(2):
                pool.wait_ge(w_hi_done, i + 1)
                pool.tensor_tensor(w_lo[:, i].rearrange("p k n -> p (k n)"), w_raw[:, i, :],
                                   w_hi[:, i].rearrange("p k n -> p (k n)").bitcast(F32),
                                   ALU.subtract).then_inc(w_lo_done, 1)
                if i == 0:
                    split_low(0)
            each_batch(pool, body)
            if clip:
                root(B - 1)

        @block.scalar
        def _(act):
            def split_high(b):
                act.wait_ge(c_in, 16 * b + 16)
                act.wait_ge(c_lo_done, b) if not isinstance(b, int) or b else None
                act.wait_ge(kv_mm, 7 * b) if not isinstance(b, int) or b else None
                act.activation(c_hi[:, :, :], c_raw[:, :, :], ACT.Copy).then_inc(c_hi_done, 1)

            def collect(b):
                act.wait_ge(c_done, b + 1)
                act.activation(oT[:, :, :], ps_y[:, 0:KC * S].rearrange("p (k s) -> p k s", k=KC),
                               ACT.Copy).then_inc(oT_done, 1)

            def body(b, first, last):
                if not first:
                    collect(b - 1)
                for u in range(SU):
                    n = SU * b + u
                    if clip:
                        act.wait_ge(clip_done, n + 1 + CK)
                        act.activation(pT[:, u // CK % 2, u % CK], s_clip[:, u % CK], ACT.Exp).then_inc(exp_done, 1)
                    else:
                        act.wait_ge(top_done, n + 1)
                        act.activation(p_rows[:, u % 2, :], ps_s[u % 2][0:S, 0:S2], ACT.Exp,
                                       bias=n_top[:, u:u + 1]).then_inc(exp_done, 1)
                    if u == 3 and not last:
                        split_high(b + 1)

            act.wait_ge(w_in, 32)
            act.activation(w_hi[:, 0].rearrange("p k n -> p (k n)"), w_raw[:, 0, :], ACT.Copy).then_inc(w_hi_done, 1)
            act.wait_ge(pad_done, 1)
            split_high(0)
            act.activation(w_hi[:, 1].rearrange("p k n -> p (k n)"), w_raw[:, 1, :], ACT.Copy).then_inc(w_hi_done, 1)
            each_batch(act, body)
            collect(B - 1)

        @block.vector
        def _(dve):
            def keys_values(b, m):
                dve.wait_ge(kv_mm, 7 * b + m + 1)
                if m < KC:
                    if k_bias is not None:
                        dve.tensor_scalar(kT[:, m, :], ps_kv[m % 2][:, 0:S2P], k_bias[:, m:m + 1], None,
                                          ALU.add).then_inc(kv_done, 1)
                    else:
                        dve.tensor_copy(kT[:, m, :], ps_kv[m % 2][:, 0:S2P]).then_inc(kv_done, 1)
                    return
                c = m - KC
                rows = v[:, c, 0:H * VE].rearrange("p (h e) -> p h e", e=VE)
                src = ps_kv[m % 2][0:CW, :].rearrange("p (h e) -> p h e", e=HD)
                if clip:
                    dve.tensor_tensor(rows[:, :, 0:HD], src, v_bias.rearrange("p (h e) -> p h e", e=HD),
                                      ALU.add).then_inc(kv_done, 1)
                else:
                    m_col = mask_cols[:, bass.ds(b * CK + c, 1)]
                    dve.tensor_scalar(rows[:, :, HD], g.ones[0:CW, 0:H], m_col, None, ALU.mult).then_inc(one_done, 1)
                    dve.tensor_scalar(rows[:, :, 0:HD], src, m_col, None, ALU.mult).then_inc(kv_done, 1)

            def clip_scores(n, b, kc):
                dve.wait_ge(s_done, S0 + n + 1)
                dve.wait_ge(exp_done, n + 1)
                dve.tensor_scalar(s_clip[:, kc], ps_s[kc][0:CW, 0:4 * S].rearrange("p (h s) -> p h s", h=4),
                                  -50.0, mask_cols[:, bass.ds(b * CK + kc, 1)], ALU.max, ALU.min).then_inc(clip_done, 1)

            def top(n, h):
                dve.wait_ge(s_done, S0 + n + 1)
                dve.tensor_reduce(n_top[:, h:h + 1], ps_s[h % 2][0:S, 0:S2], AX_X, ALU.max,
                                  negate=True).then_inc(top_done, 1)

            def out_group(b, c):
                dve.wait_ge(pv_done, 4 * b + c + 1)
                dve.tensor_copy(o_rows[:, 4 * c:4 * c + 4, :],
                                ps_o[c % 2][0:S, 0:4 * PVW].rearrange("p (h e) -> p h e", h=4)[:, :, 0:VE]
                                ).then_inc(or_done, 1)

            def normalise_rows(b):
                dve.wait_ge(or_done, 4 * b + 4 + OR0)
                if clip:
                    dve.reciprocal(r_den[:, :], o_rows[:, :, HD]).then_inc(r_done, 1)
                else:
                    dve.tensor_scalar(r_den[:, :], o_rows[:, :, HD], 1e-30, None, ALU.max).then_inc(den_done, 1)
                    dve.wait_ge(den_done, b + 1)
                    dve.reciprocal(r_den[:, :], r_den[:, :]).then_inc(r_done, 1)
                dve.wait_ge(r_done, b + 1)
                dve.tensor_tensor(o_norm[:, :].rearrange("p (h e) -> p h e", h=H), o_rows[:, :, 0:HD],
                                  r_den[:, :].unsqueeze(2).broadcast_to([S, H, HD]), ALU.mult).then_inc(on_done, 1)

            def add(b):
                xb = x[:, bass.ds(b, 1), :].squeeze(1)
                dve.wait_ge(y_done, b + 1)
                if clip:
                    dve.scalar_tensor_tensor(y_rows[:, :], ps_y[0:S, :], norm.rs, norm.bo_rs,
                                             ALU.mult, ALU.add).then_inc(rows_done, 1)
                    dve.wait_ge(rows_done, b + 1)
                    dve.bn_stats(stats[:, :], y_rows[:, :]).then_inc(st_done, 1)
                    dve.wait_ge(st_done, b + 1)
                    dve.sem_inc(st_seen, 1)
                    dve.bn_aggr(mv[:, :], stats[:, :]).then_inc(mv_done, 1)
                    dve.wait_ge(mv_done, b + 1)
                    dve.tensor_scalar(var[:, :], mv[:, 1:2], 1e-5, None, ALU.add).then_inc(var_done, 1)
                    dve.scalar_tensor_tensor(scaled[:, :], y_rows[:, :], mv[:, 0:1], norm.gamma,
                                             ALU.subtract, ALU.mult).then_inc(sc_done, 1)
                    dve.wait_ge(sc_done, b + 1)
                    dve.wait_ge(rstd_done, b + 1)
                    dve.wait_ge(beta_done, b + 1)
                    dve.scalar_tensor_tensor(xb, scaled[:, :], rstd[:, 0:1], xb, ALU.mult, ALU.add).then_inc(add_done, 1)
                else:
                    dve.tensor_tensor(y_rows[:, :], ps_y[0:S, :], gate[:, bass.ds(b, 1), :].squeeze(1),
                                      ALU.mult).then_inc(rows_done, 1)
                    dve.wait_ge(rows_done, b + 1)
                    dve.tensor_tensor(xb, xb, y_rows[:, :], ALU.add).then_inc(add_done, 1)

            def body(b, first, last):
                for m in range(KC + CK):
                    keys_values(b, m)
                if clip:
                    for u in range(2 * CK):
                        clip_scores(SU * b + u, b, u % CK)
                    if not first:
                        add(b - 1)
                    for c in range(KC):
                        out_group(b, c)
                        for kc in range(CK):
                            if c + 2 < KC:
                                clip_scores(SU * b + (c + 2) * CK + kc, b, kc)
                else:
                    top(H * b, 0)
                    top(H * b + 1, 1)
                    if not first:
                        add(b - 1)
                    for h in range(H):
                        n = H * b + h
                        dve.wait_ge(t_done, n + 1)
                        dve.tensor_copy(pT[:, h % 2], ps_t[h % 2][0:CW, 0:CK * S].rearrange("p (c s) -> p c s", c=CK)
                                        ).then_inc(pT_done, 1)
                        if h + 2 < H:
                            top(n + 2, h + 2)
                        if h % 4 == 0 and h:
                            out_group(b, h // 4 - 1)
                    out_group(b, KC - 1)
                normalise_rows(b)

            dve.sem_inc(kv_done, KV0)
            dve.sem_inc(or_done, OR0)
            if clip:
                dve.sem_inc(clip_done, CK)
                dve.sem_inc(exp_done, CK)
            dve.wait_ge(v_set, 2)
            each_batch(dve, body)
            add(B - 1)

        @block.tensor
        def _(pe):
            def keys(b, m):
                pe.wait_ge(kv_done, 7 * b + m + 1)
                for k in range(KC):
                    y = mm3(pe, ps_kv[m % 2][:, 0:S2P], w_hi[:, 0, k, m * P:(m + 1) * P], w_lo[:, 0, k, m * P:(m + 1) * P],
                            c_hi[:, k, :], c_lo[:, k, :], k == 0, k == KC - 1)
                y.then_inc(kv_mm, 1)

            def values(b, c):
                pe.wait_ge(kv_done, 7 * b + KC + c + 1)
                for k in range(KC):
                    y = mm3(pe, ps_kv[(KC + c) % 2][0:CW, :], c_hi[:, k, c * CW:(c + 1) * CW],
                            c_lo[:, k, c * CW:(c + 1) * CW], w_hi[:, 1, k, :], w_lo[:, 1, k, :], k == 0, k == KC - 1)
                y.then_inc(kv_mm, 1)

            def context_rows(b):
                pe.wait_ge(on_done, b + 1)
                for k in range(KC):
                    t = pe.transpose(ps_y[:, k * S:(k + 1) * S], o_norm[:, k * P:(k + 1) * P],
                                     g.const("ident")[0:S, 0:S])
                t.then_inc(c_done, 1)

            def out_rows(b):
                pe.wait_ge(oT_done, b + 1)
                for k in range(KC):
                    y = pe.matmul(ps_y[0:S, :], oT[:, k, :], wo[:, k, :], start=(k == 0), stop=(k == KC - 1))
                y.then_inc(y_done, 1)

            def scores_clip(b, c):
                pe.wait_ge(qd_done, KC * b + c + 1)
                for kc in range(CK):
                    n = SU * b + c * CK + kc
                    pe.wait_ge(clip_done, n + 1)
                    pe.matmul(ps_s[kc][0:CW, 0:4 * S], kT[:, c, kc * CW:(kc + 1) * CW], q_diag[:, c],
                              start=True, stop=True).then_inc(s_done, 1)

            def pv_clip(b, c):
                pe.wait_ge(exp_done, SU * b + (c + 1) * CK + CK)
                pe.wait_ge(or_done, KC * b + c + 1)
                for j in range(4):
                    for kc in range(CK):
                        o = pe.matmul(ps_o[c % 2][0:S, j * PVW:(j + 1) * PVW], pT[:, c % 2, kc, j, :],
                                      v[:, kc, VE * (4 * c + j):VE * (4 * c + j) + PVW],
                                      start=(kc == 0), stop=(kc == CK - 1))
                o.then_inc(pv_done, 1)

            def scores_max(b, h):
                pe.wait_ge(qd_done, KC * b + h // 4 + 1)
                pe.matmul(ps_s[h % 2][0:S, 0:S2], q_diag[:, h // 4, h % 4, :], kT[:, h // 4, 0:S2], start=True, stop=False)
                pe.matmul(ps_s[h % 2][0:S, 0:S2], one_row[:, :], mask_row[:, bass.ds(b * S2, S2)],
                          start=False, stop=True).then_inc(s_done, 1)

            def turn(b, h):
                pe.wait_ge(exp_done, H * b + h + 1)
                for kc in range(CK):
                    t = pe.transpose(ps_t[h % 2][0:CW, kc * S:(kc + 1) * S], p_rows[:, h % 2, kc * CW:(kc + 1) * CW],
                                     g.const("ident")[0:S, 0:S])
                t.then_inc(t_done, 1)

            def pv_max(b, h):
                pe.wait_ge(pT_done, H * b + h + 1)
                if h % 4 == 0:
                    pe.wait_ge(or_done, KC * b + h // 4 + 1)
                for kc in range(CK):
                    o = pe.matmul(ps_o[h // 4 % 2][0:S, h % 4 * PVW:(h % 4 + 1) * PVW], pT[:, h % 2, kc, :],
                                  v[:, kc, VE * h:VE * h + PVW], start=(kc == 0), stop=(kc == CK - 1))
                if h % 4 == 3:
                    o.then_inc(pv_done, 1)

            def body(b, first, last):
                pe.wait_ge(c_lo_done, b + 1)
                for m in range(KC):
                    keys(b, m)
                if not first:
                    context_rows(b - 1)
                if first:
                    pe.wait_ge(w_lo_done, 2)
                for c in range(CK):
                    values(b, c)
                if not first:
                    out_rows(b - 1)
                pe.wait_ge(kv_done, 7 * b + KC + KV0)
                if clip:
                    scores_clip(b, 0)
                    scores_clip(b, 1)
                    pe.wait_ge(kv_done, 7 * b + KC + CK + KV0)
                    for c in range(KC):
                        pv_clip(b, c)
                        if c + 2 < KC:
                            scores_clip(b, c + 2)
                else:
                    scores_max(b, 0)
                    scores_max(b, 1)
                    pe.wait_ge(kv_done, 7 * b + KC + CK + KV0)
                    for h in range(H):
                        turn(b, h)
                        if h + 2 < H:
                            scores_max(b, h + 2)
                        if h:
                            pv_max(b, h - 1)
                    pv_max(b, H - 1)

            pe.sem_inc(s_done, S0)
            pe.wait_ge(w_lo_done, 1)
            pe.wait_ge(wo_in, 16)
            if not clip:
                pe.wait_ge(v_set, 3)
            each_batch(pe, body)
            context_rows(B - 1)
            out_rows(B - 1)


def group_attention(nc, g, name, x2, q, kT, v, grp, wo_dram, causal):
    W = 4 * S
    scale = float(P) ** -0.5
    with ExitStack() as ctx:
        def sb(n, shape, dt=F32):
            return ctx.enter_context(nc.sbuf_tensor(f"{name}_{n}", shape, dt))

        sem = ctx.enter_context(semaphores(nc, name))

        wo_raw = sb("wo_raw", [P, 2, 2 * D])
        wo_hi = sb("wo_hi", [P, GQ * D], F32R)
        wo_lo = sb("wo_lo", [P, GQ * D], F32R)
        q_now = sb("q_now", [P, 2, 4, S])
        s_rows = sb("s_rows", [S, 2, 4, S])
        p_rows = sb("p_rows", [S, 2, 4, S])
        pT = sb("pT", [S, 2, 4, S])
        top = sb("top", [S, 2, 4])
        den = sb("den", [S, 2, 4])
        r_den = sb("r_den", [S, 2, 4])
        o_norm = sb("o_norm", [S, 2, 4, P])
        oT_hi = sb("oT_hi", [P, 2, 4, S], F32R)
        oT_lo = sb("oT_lo", [P, 2, 4, S], F32R)
        ps_s, ps_t, ps_o, ps_y = g.bank[0:2], g.bank[2:4], g.bank[4:6], g.bank[6:8]
        wo_in = [sem("wo_in0"), sem("wo_in1")]
        (wo_hi_done, wo_lo_done, q_done, s_done, sr_done, top_done, sub_done, exp_done, den_done, r_done,
         t_done, pT_done, pv_done, on_done, c_done, oh_done, ol_done, y_done, add_done) = map(sem, (
             "wo_hi", "wo_lo", "q", "s", "sr", "top", "sub", "exp", "den", "r", "t", "pT", "pv", "on",
             "c", "oh", "ol", "y", "add"))
        block = ctx.enter_context(nc.Block())

        def heads(ap):
            return ap[:, 0:W].rearrange("p (h s) -> p h s", h=4)

        def each_batch(e, body):
            with e.Fori(0, B - 1) as b:
                body(b, False)
            body(B - 1, True)

        @block.sync
        def _(sp):
            for i in range(4):
                if i >= 2:
                    sp.wait_ge(wo_lo_done, i - 1)
                sp.dma_start(wo_raw[:, i % 2, :], wo_dram[:, i * 2 * D:(i + 1) * 2 * D]).then_inc(wo_in[i % 2], 16)

        @block.gpsimd
        def _(pool):
            def subtract(n, u):
                pool.wait_ge(top_done, n + 1)
                pool.tensor_tensor(p_rows[:, u], s_rows[:, u], top[:, u, :].unsqueeze(2).broadcast_to([S, 4, S]),
                                   ALU.subtract).then_inc(sub_done, 1)

            def body(b, last):
                if not last:
                    for u in range(2):
                        pool.wait_ge(t_done, 2 * b + u + 1)
                        pool.wait_ge(den_done, 2 * b + u + 1)
                        subtract(2 * b + 2 + u, u)

            for u in range(2):
                subtract(u, u)
            for i in range(4):
                at = slice(i * 2 * D, (i + 1) * 2 * D)
                pool.wait_ge(wo_hi_done, i + 1)
                pool.tensor_tensor(wo_lo[:, at], wo_raw[:, i % 2, :], wo_hi[:, at].bitcast(F32), ALU.subtract).then_inc(wo_lo_done, 1)
            each_batch(pool, body)

        @block.scalar
        def _(act):
            def take_q(b, u):
                act.activation(q_now[:, u], q[:, 4 * u:4 * u + 4, bass.ds(b * S, S)], ACT.Copy).then_inc(q_done, 1)

            def exponent(n, u):
                act.wait_ge(sub_done, n + 1)
                act.activation(p_rows[:, u], p_rows[:, u], ACT.Exp).then_inc(exp_done, 1)

            def body(b, last):
                if not last:
                    for u in range(2):
                        act.wait_ge(s_done, 2 * b + u + 1)
                        take_q(b + 1, u)
                for u in range(2):
                    act.wait_ge(t_done, 2 * b + u + 1)
                    act.activation(pT[:, u], heads(ps_t[u][0:S]), ACT.Copy).then_inc(pT_done, 1)
                for u in range(2):
                    act.wait_ge(c_done, 2 * b + u + 1)
                    act.activation(oT_hi[:, u], heads(ps_t[u]), ACT.Copy).then_inc(oh_done, 1)
                if not last:
                    for u in range(2):
                        exponent(2 * b + 2 + u, u)

            for u in range(2):
                take_q(0, u)
            for u in range(2):
                exponent(u, u)
                for i in range(2 * u, 2 * u + 2):
                    at = slice(i * 2 * D, (i + 1) * 2 * D)
                    act.wait_ge(wo_in[i % 2], 16 * (i // 2) + 16)
                    act.activation(wo_hi[:, at], wo_raw[:, i % 2, :], ACT.Copy).then_inc(wo_hi_done, 1)
            each_batch(act, body)

        @block.vector
        def _(dve):
            def scale_mask_max(n, u):
                dve.wait_ge(s_done, n + 1)
                dve.scalar_tensor_tensor(s_rows[:, u], heads(ps_s[u][0:S]), scale, causal, ALU.mult,
                                         ALU.add).then_inc(sr_done, 1)
                dve.wait_ge(sr_done, n + 1)
                dve.tensor_reduce(top[:, u, :], s_rows[:, u], AX_X, ALU.max).then_inc(top_done, 1)

            def body(b, last):
                for u in range(2):
                    dve.wait_ge(exp_done, 2 * b + u + 1)
                    dve.tensor_reduce(den[:, u, :], p_rows[:, u], AX_X, ALU.add).then_inc(den_done, 1)
                for u in range(2):
                    dve.wait_ge(den_done, 2 * b + u + 1)
                    dve.reciprocal(r_den[:, u, :], den[:, u, :]).then_inc(r_done, 1)
                for u in range(2):
                    dve.wait_ge(r_done, 2 * b + u + 1)
                    dve.wait_ge(pv_done, 2 * b + u + 1)
                    dve.tensor_tensor(o_norm[:, u], ps_o[u][0:S, :].rearrange("p (h e) -> p h e", h=4),
                                      r_den[:, u, :].unsqueeze(2).broadcast_to([S, 4, P]), ALU.mult).then_inc(on_done, 1)
                for u in range(2):
                    if not last:
                        scale_mask_max(2 * b + 2 + u, u)
                    dve.wait_ge(oh_done, 2 * b + u + 1)
                    dve.tensor_tensor(oT_lo[:, u], heads(ps_t[u]), oT_hi[:, u].bitcast(F32),
                                      ALU.subtract).then_inc(ol_done, 1)
                for u in range(2):
                    dve.wait_ge(y_done, 2 * b + u + 1)
                    dve.wait_ge(add_done, 2 * b + u + 2)
                    dve.tensor_tensor(x2[:, bass.ds(b, 1), :], ps_y[u][0:S, :].unsqueeze(1), x2[:, bass.ds(b, 1), :],
                                      ALU.add).then_inc(add_done, 1)

            dve.sem_inc(add_done, 2)
            for u in range(2):
                scale_mask_max(u, u)
            each_batch(dve, body)

        @block.tensor
        def _(pe):
            def scores(n, b, u):
                pe.wait_ge(q_done, n + 1)
                for j in range(4):
                    s = pe.matmul(ps_s[u][0:S, j * S:(j + 1) * S], q_now[:, u, j, :], kT[:, grp, bass.ds(b * S, S)],
                                  start=True, stop=True)
                s.then_inc(s_done, 1)

            def body(b, last):
                for u in range(2):
                    pe.wait_ge(exp_done, 2 * b + u + 1)
                    for j in range(4):
                        t = pe.transpose(ps_t[u][0:S, j * S:(j + 1) * S], p_rows[:, u, j, :], g.const("ident")[0:S, 0:S])
                    t.then_inc(t_done, 1)
                for u in range(2):
                    pe.wait_ge(pT_done, 2 * b + u + 1)
                    for j in range(4):
                        o = pe.matmul(ps_o[u][0:S, j * P:(j + 1) * P], pT[:, u, j, :],
                                      v[:, bass.ds(b, 1), grp * P:(grp + 1) * P], start=True, stop=True)
                    o.then_inc(pv_done, 1)
                for u in range(2):
                    if not last:
                        pe.wait_ge(sr_done, 2 * b + u + 1)
                        scores(2 * b + 2 + u, b + 1, u)
                    pe.wait_ge(on_done, 2 * b + u + 1)
                    for j in range(4):
                        t = pe.transpose(ps_t[u][:, j * S:(j + 1) * S], o_norm[:, u, j, :], g.const("ident")[0:S, 0:S])
                    t.then_inc(c_done, 1)
                for u in range(2):
                    pe.wait_ge(ol_done, 2 * b + u + 1)
                    pe.wait_ge(add_done, 2 * b + u + 1)
                    for j in range(4):
                        at = slice((4 * u + j) * D, (4 * u + j + 1) * D)
                        y = mm3(pe, ps_y[u][0:S, :], oT_hi[:, u, j, :], oT_lo[:, u, j, :], wo_hi[:, at], wo_lo[:, at],
                                j == 0, j == 3)
                    y.then_inc(y_done, 1)

            for u in range(2):
                scores(u, 0, u)
            pe.wait_ge(wo_lo_done, 4)
            each_batch(pe, body)


def route(nc, g, name, wr_dram, bias, shares_dram, x, x2):
    with ExitStack() as ctx:
        def sb(n, shape, dt=F32):
            return ctx.enter_context(nc.sbuf_tensor(f"{name}_{n}", shape, dt))

        sem = ctx.enter_context(semaphores(nc, name))

        wr = sb("wr", [P, KC, E_MOE])
        wr_hi = sb("wr_hi", [P, KC, E_MOE], F32R)
        wr_lo = sb("wr_lo", [P, KC, E_MOE], F32R)
        score = sb("score", [S, B, E_MOE])
        biased = sb("biased", [S, B, E_MOE])
        largest = sb("largest", [S, B, TOPK])
        replaced = sb("replaced", [S, B, E_MOE])
        total = sb("total", [S, B])
        r_total = sb("r_total", [S, B])
        shares = sb("shares", [E_MOE + 1, T])
        wr_in, hi_done, lo_done, mm_done, sig_done, step, t_done, sh_done, one_done, stored, x_done = map(sem, (
            "wr_in", "hi", "lo", "mm", "sig", "step", "t", "sh", "one", "stored", "x"))
        block = ctx.enter_context(nc.Block())

        @block.sync
        def _(sp):
            sp.dma_start(wr[:, :, :], wr_dram).then_inc(wr_in, 16)
            sp.wait_ge(sh_done, NH)
            sp.wait_ge(one_done, 1)
            sp.dma_start(shares_dram, shares[:, :]).then_inc(stored, 16)
            sp.wait_ge(stored, 16)

        @block.gpsimd
        def _(pool):
            pool.memset(shares[E_MOE:E_MOE + 1, :], 1.0).then_inc(one_done, 1)
            pool.wait_ge(one_done, 1)
            pool.tensor_tensor(x[:, :, :], x[:, :, :], x2[:, :, :], ALU.add).then_inc(x_done, 1)

        @block.scalar
        def _(act):
            act.wait_ge(wr_in, 16)
            act.activation(wr_hi[:, :, :], wr[:, :, :], ACT.Copy).then_inc(hi_done, 1)
            act.wait_ge(mm_done, 1)
            act.activation(score[:, :, :], g.bank[0][0:S, 0:B * E_MOE].rearrange("p (b e) -> p b e", b=B),
                           ACT.Sigmoid).then_inc(sig_done, 1)
            for t in range(NH):
                act.wait_ge(t_done, t + 1)
                act.activation(shares[0:E_MOE, t * HT:(t + 1) * HT], g.bank[1 + t][0:E_MOE, 0:HT], ACT.Copy).then_inc(sh_done, 1)

        @block.vector
        def _(dve):
            dve.wait_ge(hi_done, 1)
            dve.tensor_tensor(wr_lo[:, :, :], wr[:, :, :], wr_hi[:, :, :].bitcast(F32), ALU.subtract).then_inc(lo_done, 1)
            dve.wait_ge(sig_done, 1)
            dve.tensor_tensor(biased[:, :, :], score[:, :, :], bias.unsqueeze(1).broadcast_to([S, B, E_MOE]),
                              ALU.add).then_inc(step, 1)
            dve.wait_ge(step, 1)
            for b in range(B):
                dve.max(largest[:, b, :], biased[:, b, :]).then_inc(step, 1)
            for b in range(B):
                dve.wait_ge(step, 2 + b)
                dve.match_replace(replaced[:, b, :], largest[:, b, :], biased[:, b, :], NEG).then_inc(step, 1)
            dve.wait_ge(step, 1 + 2 * B)
            dve.tensor_tensor(biased[:, :, :], biased[:, :, :], replaced[:, :, :], ALU.not_equal).then_inc(step, 1)
            dve.wait_ge(step, 2 + 2 * B)
            dve.tensor_tensor(biased[:, :, :], biased[:, :, :], score[:, :, :], ALU.mult).then_inc(step, 1)
            dve.wait_ge(step, 3 + 2 * B)
            dve.tensor_reduce(total[:, :], biased[:, :, :], AX_X, ALU.add).then_inc(step, 1)
            dve.wait_ge(step, 4 + 2 * B)
            dve.reciprocal(r_total[:, :], total[:, :]).then_inc(step, 1)
            dve.wait_ge(step, 5 + 2 * B)
            dve.tensor_tensor(score[:, :, :], biased[:, :, :], r_total[:, :].unsqueeze(2).broadcast_to([S, B, E_MOE]),
                              ALU.mult).then_inc(step, 1)

        @block.tensor
        def _(pe):
            pe.wait_ge(lo_done, 1)
            for b in range(B):
                for k in range(KC):
                    y = mm3(pe, g.bank[0][0:S, b * E_MOE:(b + 1) * E_MOE], g.hT_hi[:, k, b * S:(b + 1) * S],
                            g.hT_lo[:, k, b * S:(b + 1) * S], wr_hi[:, k, :], wr_lo[:, k, :], k == 0, k == KC - 1)
            y.then_inc(mm_done, 1)
            pe.wait_ge(step, 6 + 2 * B)
            for b in range(B):
                t = pe.transpose(g.bank[1 + b // HB][0:E_MOE, b % HB * S:(b % HB + 1) * S], score[:, b, :],
                                 g.const("ident")[0:S, 0:S])
                if b % HB == HB - 1:
                    t.then_inc(t_done, 1)


def experts(nc, g, name, w_dram, E, acc, shares_dram=None):
    NP_ = 3
    PW = EW // NP_
    U = NH * NC
    DT = NH * KC
    with ExitStack() as ctx:
        def sb(n, shape, dt=F32):
            return ctx.enter_context(nc.sbuf_tensor(f"{name}_{n}", shape, dt))

        sem = ctx.enter_context(semaphores(nc, name))

        raw = sb("raw", [P, EW])
        w_hi = sb("w_hi", [P, 2, EW], F32R)
        w_lo = sb("w_lo", [P, 2, EW], F32R)
        silu = sb("silu", [P, NC, HT])
        prod = sb("prod", [P, NC, HT])
        a_hi = sb("a_hi", [P, NH, NC, HT], F32R)
        a_lo = sb("a_lo", [P, NH, NC, HT], F32R)
        share = sb("share", [P, 2, T]) if shares_dram is not None else None
        ps_g, ps_u, ps_d = g.bank[0:2], g.bank[2:4], g.bank[4:8]
        (raw_in, hi_done, lo_done, gu_done, silu_done, prod_done, sh_done, ah_done, al_done, d_done, acc_done,
         zero) = map(sem, ("raw_in", "hi", "lo", "gu", "silu", "prod", "sh", "ah", "al", "d", "acc", "zero"))
        share_in = [sem("share_in0"), sem("share_in1")]
        block = ctx.enter_context(nc.Block())
        PR0, AC0, D0, SH0 = NC, KC, DT, 2 * U

        def each_expert(eng, body):
            body(0, 0, True, False)
            n = (E - 2) // 2
            with eng.Fori(0, n) as i:
                body(2 * i + 1, 1, False, False)
                body(2 * i + 2, 0, False, False)
            if E % 2:
                body(E - 2, 1, False, False)
                body(E - 1, 0, False, True)
            else:
                body(E - 1, 1, False, True)

        @block.sync
        def _(sp):
            def body(e, slot, first, last):
                if not first:
                    sp.wait_ge(lo_done, NP_ * e)
                sp.dma_start(raw[:, :], w_dram[bass.ds(e, 1)].squeeze(0)).then_inc(raw_in, 16)
                if share is not None:
                    sp.wait_ge(sh_done, U * e + U)
                    sp.dma_start(share[:, slot, :],
                                 shares_dram[bass.ds(e, 1), :].squeeze(0).partition_broadcast(P)).then_inc(share_in[slot], 16)

            each_expert(sp, body)

        @block.gpsimd
        def _(pool):
            def split_low(e, slot, i):
                pool.wait_ge(hi_done, NP_ * e + i + 1)
                pool.tensor_tensor(w_lo[:, slot, i * PW:(i + 1) * PW], raw[:, i * PW:(i + 1) * PW],
                                   w_hi[:, slot, i * PW:(i + 1) * PW].bitcast(F32), ALU.subtract).then_inc(lo_done, 1)

            def body(e, slot, first, last):
                for n in range(U):
                    t, c = divmod(n, NC)
                    if share is not None:
                        if n == 0:
                            pool.wait_ge(share_in[slot], 8 * (e - slot) + 16)
                        pool.wait_ge(prod_done, U * e + n + 1 + PR0)
                        pool.tensor_tensor(prod[:, c, :], prod[:, c, :], share[:, slot, t * HT:(t + 1) * HT],
                                           ALU.mult).then_inc(sh_done, 1)
                    if n < NP_ and not last:
                        split_low(e + 1, 1 - slot, n)

            if share is not None:
                pool.sem_inc(sh_done, SH0)
            for i in range(NP_):
                split_low(0, 0, i)
            each_expert(pool, body)

        @block.scalar
        def _(act):
            def split_high(e, slot, i):
                if i == 0:
                    act.wait_ge(raw_in, 16 * e + 16)
                act.activation(w_hi[:, slot, i * PW:(i + 1) * PW], raw[:, i * PW:(i + 1) * PW], ACT.Copy).then_inc(hi_done, 1)

            def body(e, slot, first, last):
                for n in range(U):
                    t, c = divmod(n, NC)
                    act.wait_ge(gu_done, U * e + n + 1)
                    act.activation(silu[:, c, :], ps_g[c][:, 0:HT], ACT.Silu).then_inc(silu_done, 1)
                    if share is not None:
                        act.wait_ge(sh_done, U * e + n + 1 + SH0)
                    else:
                        act.wait_ge(prod_done, U * e + n + 1 + PR0)
                    act.activation(a_hi[:, t, c, :], prod[:, c, :], ACT.Copy).then_inc(ah_done, 1)
                    if n < NP_ and not last:
                        if n == 0:
                            act.wait_ge(d_done, DT * e + D0)
                        split_high(e + 1, 1 - slot, n)

            for i in range(NP_):
                split_high(0, 0, i)
            each_expert(act, body)

        @block.vector
        def _(dve):
            def add(e, t):
                for f in range(KC):
                    n = DT * e + KC * t + f
                    dve.wait_ge(d_done, n + 1 + D0)
                    dst = acc[:, f, t * HT:(t + 1) * HT]
                    dve.tensor_tensor(dst, ps_d[f][:, 0:HT], dst, ALU.add).then_inc(acc_done, 1)

            def unit(e, n):
                t, c = divmod(n, NC)
                dve.wait_ge(silu_done, U * e + n + 1)
                dve.tensor_tensor(prod[:, c, :], ps_u[c][:, 0:HT], silu[:, c, :], ALU.mult).then_inc(prod_done, 1)
                dve.wait_ge(ah_done, U * e + n + 1)
                dve.tensor_tensor(a_lo[:, t, c, :], prod[:, c, :], a_hi[:, t, c, :].bitcast(F32),
                                  ALU.subtract).then_inc(al_done, 1)

            def body(e, slot, first, last):
                unit(e, 0)
                if not first:
                    add(e - 1, 1)
                unit(e, 1)
                unit(e, 2)
                add(e, 0)
                unit(e, 3)

            dve.sem_inc(prod_done, PR0)
            dve.sem_inc(acc_done, AC0)
            dve.memset(acc[:, :, :], 0.0).then_inc(zero, 1)
            dve.wait_ge(zero, 1)
            each_expert(dve, body)
            add(E - 1, 1)

        @block.tensor
        def _(pe):
            def gate_up(e, slot, n):
                t, c = divmod(n, NC)
                pe.wait_ge(prod_done, U * e + n + 1)
                for ps, base in ((ps_g, 0), (ps_u, KC * EI)):
                    for k in range(KC):
                        at = slice(base + k * EI + c * P, base + k * EI + (c + 1) * P)
                        y = mm3(pe, ps[c][:, 0:HT], w_hi[:, slot, at], w_lo[:, slot, at],
                                g.hT_hi[:, k, t * HT:(t + 1) * HT], g.hT_lo[:, k, t * HT:(t + 1) * HT],
                                k == 0, k == KC - 1)
                y.then_inc(gu_done, 1)

            def down(e, slot, t):
                pe.wait_ge(al_done, U * e + NC * (t + 1))
                for f in range(KC):
                    n = DT * e + KC * t + f
                    pe.wait_ge(acc_done, n + 1)
                    for c in range(NC):
                        at = slice(2 * KC * EI + c * D + f * P, 2 * KC * EI + c * D + (f + 1) * P)
                        y = mm3(pe, ps_d[f][:, 0:HT], w_hi[:, slot, at], w_lo[:, slot, at], a_hi[:, t, c, :],
                                a_lo[:, t, c, :], c == 0, c == NC - 1)
                    y.then_inc(d_done, 1)

            def body(e, slot, first, last):
                pe.wait_ge(lo_done, NP_ * (e + 1))
                gate_up(e, slot, 0)
                if not first:
                    down(e - 1, 1 - slot, 1)
                gate_up(e, slot, 1)
                gate_up(e, slot, 2)
                down(e, slot, 0)
                gate_up(e, slot, 3)

            pe.sem_inc(d_done, D0)
            each_expert(pe, body)
            down(E - 1, (E - 1) % 2, 1)


def add_back(nc, g, name, x, acc, out=None):
    with semaphores(nc, name) as sem, nc.Block() as block:
        t_done, x_done, stored = map(sem, ("t", "x", "stored"))

        @block.tensor
        def _(pe):
            for b in range(B):
                if b >= 4:
                    pe.wait_ge(x_done, b - 3)
                for k in range(KC):
                    t = pe.transpose(g.bank[b % 4][0:S, k * P:(k + 1) * P], acc[:, k, b * S:(b + 1) * S], g.const("ident"))
                t.then_inc(t_done, 1)

        @block.vector
        def _(dve):
            for b in range(B):
                dve.wait_ge(t_done, b + 1)
                dve.tensor_tensor(x[:, b, :], g.bank[b % 4][0:S, :], x[:, b, :], ALU.add).then_inc(x_done, 1)

        if out is not None:
            @block.sync
            def _(sp):
                for i in range(2):
                    sp.wait_ge(x_done, HB * (i + 1))
                    sp.dma_start(out[HB * i:HB * (i + 1)].rearrange("b s d -> s b d"), x[:, HB * i:HB * (i + 1), :]
                                 ).then_inc(stored, 16)
                sp.wait_ge(stored, 32)


@contextmanager
def transposed(nc, g, name):
    with nc.sbuf_tensor(f"{name}_hT_hi", [P, KC, T], F32R) as hi, nc.sbuf_tensor(f"{name}_hT_lo", [P, KC, T], F32R) as lo:
        g.hT_hi, g.hT_lo = hi, lo
        yield


def vw(heads, hd):
    return heads * (hd + 1) + PVW - (hd + 1)


class Shared:
    pass


OutputNorm = namedtuple("OutputNorm", "rs bo_rs gamma beta")


def program(nc, a, out, stages=99, start=0):
    with ExitStack() as ctx:
        def sb(n, shape, dt=F32):
            return ctx.enter_context(nc.sbuf_tensor(n, shape, dt))

        g = Shared()
        g.bank = [ctx.enter_context(nc.psum_tensor(f"bank{i}", [P, 512], F32)) for i in range(8)]
        consts = sb("consts", [P, NCONST])
        rows = sb("rows", [P, NROW])
        pvec = sb("pvec", [P, 16])
        x = sb("x", [S, B, D])
        g.const = lambda n: consts[:, CONSTS[n][0]:CONSTS[n][0] + CONSTS[n][1]]
        g.row = lambda n: rows[:, ROWS[n][0]:ROWS[n][0] + ROWS[n][1]]
        x_mask = sb("x_mask", [CW, B * CK], I32)
        x_high = sb("x_high", [CW, B * CK])
        y_mask = sb("y_mask", [CW, B * CK], U8)
        y_valid = sb("y_valid", [CW, B * CK])
        g.ones = sb("ones", [P, 32])
        rs = sb("rs", [P, 1])
        shares = nc.dram_tensor("shares", (E_MOE + 1, T), F32).ap()
        loaded = nc.alloc_semaphore("loaded")
        ready = nc.alloc_semaphore("ready")
        stored = nc.alloc_semaphore("stored")

        with nc.Block() as block:
            @block.sync
            def _(sp):
                sp.dma_start(x[:, :, :], a["x"].rearrange("b s d -> s b d")).then_inc(loaded, 16)
                sp.dma_start(consts[:, :], a["consts"]).then_inc(loaded, 16)
                sp.dma_start(pvec[:, :], a["pvec"]).then_inc(loaded, 16)
                sp.dma_start(rows[:, :], a["rows"].partition_broadcast(P)).then_inc(loaded, 16)
                sp.dma_start(x_mask[:, :], a["x_mask"]).then_inc(loaded, 16)
                sp.dma_start(y_mask[:, :], a["y_mask"]).then_inc(loaded, 16)

            @block.vector
            def _(dve):
                dve.memset(g.ones[:, :], 1.0).then_inc(ready, 1)
                dve.wait_ge(loaded, 16 * 6)
                dve.tensor_scalar(x_high[:, :], x_mask[:, :], 0.5, 100.0, ALU.is_gt, ALU.mult).then_inc(ready, 1)
                dve.tensor_copy(y_valid[:, :], y_mask[:, :]).then_inc(ready, 1)
                dve.tensor_scalar(rs[:, :], g.row("res_scale"), 0.0, 0.3, ALU.max, ALU.min).then_inc(ready, 1)
                dve.wait_ge(ready, 4)
                dve.tensor_scalar(x_high[:, :], x_high[:, :], 50.0, None, ALU.subtract).then_inc(ready, 1)

        if start <= 1 <= stages:
            with ExitStack() as st:
                qk = st.enter_context(nc.sbuf_tensor("a_qk", [P, 2 * KC, T], F32))
                v = st.enter_context(nc.sbuf_tensor("a_v", [S, B, vw(16, 32)], F32))
                with transposed(nc, g, "a"):
                    normalise(nc, g, "a_norm", x, "ln")
                    project(nc, g, "a_proj", a["a_wqk"], 2 * KC, qk, bias=pvec[:, 0:8],
                            value=(a["a_wv"], v, 16, 32, g.row("a_bv")[0:S]))
                causal = g.const("causal")[0:S].unsqueeze(1).broadcast_to([S, 4, S])
                self_attention(nc, g, "a_att", x, qk[:, 0:KC], qk[:, KC:2 * KC], v, 16, 32, 32 ** -0.5,
                               g.const("hm32"), lambda grp: causal, a["a_wo"], wo_bias=g.row("a_bo")[0:S])

        if start <= 2 <= stages:
            with ExitStack() as st:
                q = st.enter_context(nc.sbuf_tensor("x_q", [P, KC, T], F32))
                bo_rs = st.enter_context(nc.sbuf_tensor("bo_rs", [P, D], F32))
                with nc.Block() as block:
                    @block.vector
                    def _(dve):
                        dve.tensor_scalar(bo_rs[:, :], g.row("x_bo"), rs[:, 0:1], None, ALU.mult)

                with transposed(nc, g, "x"):
                    normalise(nc, g, "x_norm", x, "ln")
                    project(nc, g, "x_proj", a["x_wq"], KC, q, bias=pvec[:, 8:12], scale=32 ** -0.5)
                cross_attention(nc, g, "x_att", x, q, a["ctxT"], a["x_wk"], a["x_wv"], a["x_wo"], "clip", k_bias=pvec[:, 12:16],
                                v_bias=g.row("x_bv")[0:CW], mask_cols=x_high,
                                norm=OutputNorm(rs=rs[0:S, 0:1], bo_rs=bo_rs[0:S, :], gamma=g.row("gamma")[0:S],
                                                     beta=g.row("beta")[0:S]))

        if start <= 3 <= stages:
            with nc.sbuf_tensor("f_x2", [S, B, D], F32) as x2:
                with ExitStack() as st:
                    v = st.enter_context(nc.sbuf_tensor("f_v", [S, B, D], F32))
                    kT = st.enter_context(nc.sbuf_tensor("f_kT", [P, NG, T], F32))
                    causal = g.const("causal")[0:S].unsqueeze(1).broadcast_to([S, 4, S])
                    rope = (g.const("cos128"), g.const("sin128"))
                    with transposed(nc, g, "f"):
                        normalise(nc, g, "f_norm", x, "ln_rms", eps2=1e-5, w=g.row("ln1_w")[0:S], keep=x2)
                        project(nc, g, "f_k", a["f_wk"], NG, kT, rope=rope, value=(a["f_wv"], v, NG, P, None))
                        for grp in range(NG):
                            with nc.sbuf_tensor(f"f_q{grp}", [P, GQ, T], F32) as q:
                                project(nc, g, f"f_q{grp}_proj", a["f_wq"][grp], GQ, q, rope=rope)
                                group_attention(nc, g, f"f_att{grp}", x2, q, kT, v, grp, a["f_wo"][grp], causal)
                with ExitStack() as st:
                    acc = st.enter_context(nc.sbuf_tensor("m_acc", [P, KC, T], F32))
                    with transposed(nc, g, "m"):
                        normalise(nc, g, "m_norm", x2, "rms", eps2=1e-5, w=g.row("ln2_w")[0:S])
                        route(nc, g, "m_route", a["m_wr"], g.row("expert_bias")[0:S], shares, x, x2)
                        experts(nc, g, "m_exp", a["m_w"], E_MOE + 1, acc, shares)
                    add_back(nc, g, "m_add", x, acc)

        if start <= 4 <= stages:
            with ExitStack() as st:
                qk = st.enter_context(nc.sbuf_tensor("b_qk", [P, 2 * KC, T], F32))
                v = st.enter_context(nc.sbuf_tensor("b_v", [S + 1, B, vw(32, 16)], F32))
                bias = st.enter_context(nc.sbuf_tensor("b_bias", [S, 32, S], F32))
                bias_in = nc.alloc_semaphore("b_bias_in")
                with nc.Block() as block:
                    @block.sync
                    def _(sp):
                        sp.dma_start(bias[:, :, :], a["b_bias"]).then_inc(bias_in, 16)
                        sp.wait_ge(bias_in, 16)
                with transposed(nc, g, "b"):
                    normalise(nc, g, "b_norm", x, "ln")
                    project(nc, g, "b_proj", a["b_wqk"], 2 * KC, qk, rope=(g.const("cos16"), g.const("sin16")),
                            value=(a["b_wv"], v, 32, 16, None))
                self_attention(nc, g, "b_att", x, qk[:, 0:KC], qk[:, KC:2 * KC], v, 32, 16, 16 ** -0.5,
                               g.const("hm8"), lambda grp: bias[:, 4 * grp:4 * grp + 4, :], a["b_wo"],
                               sink=g.row("offset")[0:S])

        if start <= 5 <= stages:
            with ExitStack() as st:
                q = st.enter_context(nc.sbuf_tensor("y_q", [P, KC, T], F32))
                y_mask_row = st.enter_context(nc.sbuf_tensor("y_mask_row", [1, B * S2], U8))
                y_bias = st.enter_context(nc.sbuf_tensor("y_bias", [1, B * S2], BF16))
                mask_in = nc.alloc_semaphore("y_mask_in")
                with nc.Block() as block:
                    @block.sync
                    def _(sp):
                        sp.dma_start(y_mask_row[:, :], a["y_mask_row"]).then_inc(mask_in, 16)

                    @block.vector
                    def _(dve):
                        dve.wait_ge(mask_in, 16)
                        dve.tensor_scalar(y_bias[:, :], y_mask_row[:, :], 1.0, -NEG, ALU.subtract, ALU.mult)

                gate = st.enter_context(nc.sbuf_tensor("y_gate", [S, B, D], F32))
                with transposed(nc, g, "y"):
                    normalise(nc, g, "y_norm", x, "ln_rms", eps2=1e-6, w=g.row("norm_w")[0:S])
                    project(nc, g, "y_proj", a["y_wq"], KC, q, scale=32 ** -0.5, value=(a["y_wg"], gate, None, None, None))
                cross_attention(nc, g, "y_att", x, q, a["ctxT"], a["y_wk"], a["y_wv"], a["y_wo"], "max", mask_cols=y_valid,
                                mask_row=y_bias, gate=gate)

        if start <= 6 <= stages:
            with ExitStack() as st:
                acc = st.enter_context(nc.sbuf_tensor("z_acc", [P, KC, T], F32))
                with transposed(nc, g, "z"):
                    normalise(nc, g, "z_norm", x, "ln")
                    experts(nc, g, "z_exp", a["z_w"], FFN // EI, acc)
                add_back(nc, g, "z_add", x, acc, out)
            return

        with nc.Block() as block:
            @block.sync
            def _(sp):
                sp.dma_start(out.rearrange("b s d -> s b d"), x[:, :, :]).then_inc(stored, 16)
                sp.wait_ge(stored, 16)


def chunked(w):
    k, m = w.shape[0] // P, w.shape[1] // P
    return np.ascontiguousarray(w.reshape(k, P, m, P).transpose(2, 1, 0, 3).reshape(m, P, k * P))


def by_partition(w):
    return np.ascontiguousarray(w.reshape(-1, P, w.shape[1]).transpose(1, 0, 2))


def expert_rows(gate, up, down):
    e = gate.shape[0]
    gu = [w.reshape(e, KC, P, EI).transpose(0, 2, 1, 3).reshape(e, P, KC * EI) for w in (gate, up)]
    return np.concatenate(gu + [down.reshape(e, NC, P, D).transpose(0, 2, 1, 3).reshape(e, P, NC * D)], axis=2)


def packed(i):
    o = {}
    c = np.zeros((P, NCONST), np.float32)

    def put(name, v):
        c[:v.shape[0], CONSTS[name][0]:CONSTS[name][0] + v.shape[1]] = v

    put("ident", np.eye(P, dtype=np.float32))
    put("hm32", (np.arange(P)[:, None] // 32 == np.arange(4)).astype(np.float32))
    put("hm8", (np.arange(P)[:, None] % 64 // 8 == np.arange(8)).astype(np.float32))
    put("causal", np.where(np.tril(np.ones((S, S), bool)), 0.0, NEG).astype(np.float32))
    put("power", np.full((P, B), -0.5, np.float32))
    for hd in (16, 128):
        half = hd // 2
        inv = (1.0 / np.float32(ROPE_BASE) ** (np.arange(half, dtype=np.float32) / np.float32(half))).astype(np.float32)
        angle = (np.arange(S, dtype=np.float32)[None, :] * inv[:, None]).astype(np.float32)
        at = np.arange(P) % 64 % half
        sign = np.where(np.arange(P) < 64, -1.0, 1.0).astype(np.float32)[:, None]
        put(f"cos{hd}", np.cos(angle)[at])
        put(f"sin{hd}", np.sin(angle)[at] * sign)
    o["consts"] = c
    r = {"a_bv": "L0_attn_bv", "a_bo": "L0_attn_bo", "x_bv": "L0_xattn_bv", "x_bo": "L0_xattn_bo",
         "gamma": "L0_xattn_ln_gamma", "beta": "L0_xattn_ln_beta", "ln1_w": "L0_ffn_ln1_w", "ln2_w": "L0_ffn_ln2_w",
         "norm_w": "L1_xattn_norm_w", "expert_bias": "L0_ffn_expert_bias", "offset": "L1_attn_softmax_offset",
         "res_scale": "L0_xattn_residual_scale"}
    o["rows"] = np.concatenate([np.reshape(i[r[n]], -1) for n in ROWS])
    o["pvec"] = np.concatenate([i[n].reshape(KC, P).T for n in ("L0_attn_bq", "L0_attn_bk", "L0_xattn_bq", "L0_xattn_bk")],
                               axis=1)
    o["x"] = i["x"]
    o["a_wqk"] = chunked(np.concatenate([i["L0_attn_wq"].T, i["L0_attn_wk"].T], axis=1))
    o["a_wv"] = by_partition(i["L0_attn_wv"].T)
    o["a_wo"] = by_partition(i["L0_attn_wo"].T)
    o["f_wk"] = chunked(i["L0_ffn_Wk"])
    o["f_wv"] = by_partition(i["L0_ffn_Wv"])
    o["f_wq"] = chunked(i["L0_ffn_Wq"]).reshape(NG, GQ, P, KC * P)
    o["f_wo"] = i["L0_ffn_Wo"].reshape(NG, GQ, P, D).transpose(0, 2, 1, 3).reshape(NG, P, GQ * D)
    o["m_wr"] = by_partition(i["L0_ffn_Wr"])
    o["m_w"] = expert_rows(*(np.concatenate([i["L0_ffn_" + n], i["L0_ffn_" + m][None]])
                             for n, m in (("Wg", "Wsg"), ("Wu", "Wsu"), ("Wd", "Wsd"))))
    o["z_w"] = expert_rows(*(i["L1_ffn_" + n].reshape(FFN // EI, EI, D).transpose(0, 2, 1) for n in ("w_gate", "w_up")),
                           i["L1_ffn_w_down"].T.reshape(FFN // EI, EI, D))
    at = np.arange(D).reshape(KC, 8, 2, 8).transpose(0, 2, 1, 3).reshape(-1)
    o["b_wqk"] = chunked(np.concatenate([i["L1_attn_Wq"].T[:, at], i["L1_attn_Wk"].T[:, at]], axis=1))
    o["b_wv"] = by_partition(i["L1_attn_Wv"].T)
    o["b_wo"] = by_partition(i["L1_attn_Wo"].T)
    back = np.arange(S)[:, None] - np.arange(S)[None, :]
    o["b_bias"] = np.where(back[:, None, :] >= 0, i["L1_attn_learnable_bias"][:, np.maximum(back, 0)].transpose(1, 0, 2),
                           np.float32(NEG)).astype(np.float32)
    o["ctxT"] = i["ctx_2048"].transpose(0, 2, 1).reshape(B, KC, P, S2).transpose(0, 2, 1, 3)
    for n, src in (("x_wq", "L0_xattn_Wq"), ("y_wq", "L1_xattn_wq")):
        o[n] = chunked(i[src].T)
    for n, src in (("x_wk", "L0_xattn_Wk"), ("x_wv", "L0_xattn_Wv"), ("y_wk", "L1_xattn_wk"), ("y_wv", "L1_xattn_wv")):
        o[n] = by_partition(i[src].T).reshape(P, KC * D)
    for n, src in (("x_wo", "L0_xattn_Wo"), ("y_wo", "L1_xattn_wo"), ("y_wg", "L1_xattn_wg")):
        o[n] = by_partition(i[src].T)
    for n, src in (("x_mask", "mask_BxS2_ik0"), ("y_mask", "mask_BxS2_bk0")):
        o[n] = i[src].reshape(B, CK, CW).transpose(2, 0, 1).reshape(CW, B * CK)
    o["y_mask_row"] = i["mask_BxS2_bk0"].reshape(1, B * S2)
    return {k: np.ascontiguousarray(v) for k, v in o.items()}


def kernel(**inputs):
    import concourse.bacc as bacc
    from concourse.bass_utils import run_bass_kernel_spmd

    arrays = packed({k: np.asarray(v) for k, v in inputs.items()})
    nc = bacc.Bacc("TRN2", target_bir_lowering=False, num_devices=1)
    aps = {k: nc.dram_tensor(f"in_{k}", v.shape, mybir.dt.from_np(v.dtype), kind="ExternalInput").ap()
           for k, v in arrays.items()}
    out = nc.dram_tensor("out", (B, S, D), F32, kind="ExternalOutput").ap()
    program(nc, aps, out)
    r = run_bass_kernel_spmd(nc, [{f"in_{k}": v for k, v in arrays.items()}], core_ids=[0])
    return r.results[0]["out"]
```

```python
from collections import namedtuple
from contextlib import ExitStack, contextmanager

import numpy as np

import concourse.bass as bass
from concourse import mybir

F32 = mybir.dt.float32
F32R = mybir.dt.float32r
BF16 = mybir.dt.bfloat16
I32 = mybir.dt.int32
U8 = mybir.dt.uint8
ALU = mybir.AluOpType
ACT = mybir.ActivationFunctionType
AX_X = mybir.AxisListType.X

P = 128
B, S, D = 8, 112, 512
KC = D // P
T = B * S
NH = 2
HB = B // NH
HT = T // NH
S2 = 375
CK = 3
CW = S2 // CK
S2P = S2 + 1
PVW = 100
NEG = -1.0e30
ROPE_BASE = 10000.0
E_MOE, TOPK, EI = 32, 8, 256
NC = EI // P
NP_ = 3
EW = 2 * KC * EI + NC * D
FFN = 2048
NG = 4
GQ = 8

PW = EW // NP_

CONSTS = {}
_at = 0
for _name, _w in (("ident", P), ("hm32", 4), ("hm8", 8), ("causal", S),
                  ("cos16", S), ("sin16", S), ("cos128", S), ("sin128", S), ("power", B)):
    CONSTS[_name] = (_at, _w)
    _at += _w
NCONST = _at
ROWS = {}
_at = 0
for _name, _w in (("a_bv", D), ("a_bo", D), ("x_bv", D), ("x_bo", D), ("gamma", D), ("beta", D),
                  ("ln1_w", D), ("ln2_w", D), ("norm_w", D), ("expert_bias", E_MOE),
                  ("offset", 32), ("res_scale", 1)):
    ROWS[_name] = (_at, _w)
    _at += _w
NROW = _at


@contextmanager
def semaphores(nc, name):
    taken = []

    def sem(n):
        taken.append(nc.alloc_semaphore(f"{name}_{n}"))
        return taken[-1]

    yield sem
    nc.clear_and_free_semaphores(taken)
    nc.all_engine_barrier()


class Early:

    def __init__(self, srcs, raws, his, los, reuses=False):
        self.srcs, self.raws, self.his, self.los, self.reuses = srcs, raws, his, los, reuses

    def add(self, src, raw, hi, lo):
        for pieces, piece in ((self.srcs, src), (self.raws, raw), (self.his, hi), (self.los, lo)):
            pieces.append(piece)

    def load(self, sp, loaded):
        for src, raw in zip(self.srcs, self.raws):
            sp.dma_start(raw, src).then_inc(loaded, 16)

    def split_high(self, act, loaded, hi_done):
        act.wait_ge(loaded, 16 * len(self.raws))
        for raw, hi in zip(self.raws, self.his):
            act.activation(hi, raw, ACT.Copy).then_inc(hi_done, 1)

    def split_low(self, pool, hi_done, lo_done):
        for n, (raw, hi, lo) in enumerate(zip(self.raws, self.his, self.los)):
            pool.wait_ge(hi_done, n + 1)
            pool.tensor_tensor(lo, raw, hi.bitcast(F32), ALU.subtract).then_inc(lo_done, 1)


def normalise(nc, g, name, src, kind, eps2=0.0, w=None, keep=None, early=None,
              first=False):
    with ExitStack() as ctx:
        def sb(n, shape):
            return ctx.enter_context(nc.sbuf_tensor(f"{name}_{n}", shape, F32))

        sem = ctx.enter_context(semaphores(nc, name))

        h = keep if keep is not None else (src if kind == "rms" else sb("h", [S, B, D]))
        y = h if kind == "ln" else sb("y", [S, B, D])
        junk = sb("junk", [S, D])
        stats = g.stats
        mv = sb("mv", [S, B, 2])
        var = sb("var", [S, B])
        rstd = sb("rstd", [S, B])
        ssq = sb("ssq", [S, B])
        ms = sb("ms", [S, B])
        rrms = sb("rrms", [S, B])
        stats_done, aggr_done, var_done, rstd_done, h_done = map(sem, ("stats", "aggr", "var", "rstd", "h"))
        ssq_done, ms_done, rrms_done, y_done = map(sem, ("ssq", "ms", "rrms", "y"))
        tr_done, hi_done, lo_done = map(sem, ("tr", "hi", "lo"))
        ready = h_done if kind == "ln" else y_done
        if early:
            early_in, early_hi, early_lo = map(sem, ("early_in", "early_hi", "early_lo"))
        block = ctx.enter_context(nc.Block())

        if early:
            @block.sync
            def _(sp):
                early.load(sp, early_in)

        @block.vector
        def _(dve):
            if kind != "rms":
                for b in range(B):
                    if first:
                        dve.bn_stats(stats[:, b, :], src[:, b, :]).then_inc(stats_done, 1)
                for b in range(B):
                    if first:
                        dve.wait_ge(stats_done, b + 1)
                    dve.bn_aggr(mv[:, b, :], stats[:, b, :]).then_inc(aggr_done, 1)
                dve.wait_ge(aggr_done, B)
                dve.tensor_scalar(var[:, :], mv[:, :, 1], 1e-5, None, ALU.add).then_inc(var_done, 1)
                dve.wait_ge(rstd_done, 1)
                if kind == "ln_rms":
                    dve.tensor_tensor(ssq[:, :], rstd[:, :], rstd[:, :], ALU.mult).then_inc(ssq_done, 1)
                    dve.wait_ge(ssq_done, 1)
                    dve.tensor_tensor(ssq[:, :], ssq[:, :], mv[:, :, 1], ALU.mult).then_inc(ssq_done, 1)
                    dve.wait_ge(ssq_done, 2)
                    dve.tensor_scalar(ms[:, :], ssq[:, :], eps2, None, ALU.add).then_inc(ms_done, 1)
                for b in range(B):
                    dve.tensor_scalar(h[:, b, :], src[:, b, :], mv[:, b, 0:1], rstd[:, b:b + 1],
                                      ALU.subtract, ALU.mult).then_inc(h_done, 1)
            if kind == "rms":
                dve.wait_ge(ssq_done, B)
                dve.tensor_scalar(ms[:, :], ssq[:, :], 1.0 / D, eps2, ALU.mult, ALU.add).then_inc(ms_done, 1)
            if kind != "ln":
                dve.wait_ge(rrms_done, 1)
                for b in range(B):
                    if kind == "ln_rms":
                        dve.wait_ge(h_done, b + 1)
                    dve.scalar_tensor_tensor(y[:, b, :], h[:, b, :], rrms[:, b:b + 1], w,
                                             ALU.mult, ALU.mult).then_inc(y_done, 1)
            for b in range(B):
                dve.wait_ge(hi_done, b + 1)
                dve.tensor_tensor(g.hT_lo[:, :, b * S:(b + 1) * S],
                                  g.bank[b % 4][:, 0:KC * S].rearrange("p (k s) -> p k s", k=KC),
                                  g.hT_hi[:, :, b * S:(b + 1) * S].bitcast(F32),
                                  ALU.subtract).then_inc(lo_done, 1)

        @block.gpsimd
        def _(pool):
            if kind != "rms":
                pool.wait_ge(var_done, 1)
                pool.tensor_tensor(rstd[:, :], var[:, :], g.const("power")[0:S, :], ALU.pow).then_inc(rstd_done, 1)
            if kind != "ln":
                pool.wait_ge(ms_done, 1)
                pool.tensor_tensor(rrms[:, :], ms[:, :], g.const("power")[0:S, :], ALU.pow).then_inc(rrms_done, 1)
            if early:
                early.split_low(pool, early_hi, early_lo)

        @block.scalar
        def _(act):
            if kind == "rms":
                for b in range(B):
                    if b:
                        act.wait_ge(ssq_done, b)
                    act.activation(junk[:, :], h[:, b, :], ACT.Square,
                                   accum_out=ssq[:, b:b + 1]).then_inc(ssq_done, 1)
            if early:
                early.split_high(act, early_in, early_hi)
            for b in range(B):
                act.wait_ge(tr_done, b + 1)
                act.activation(g.hT_hi[:, :, b * S:(b + 1) * S],
                               g.bank[b % 4][:, 0:KC * S].rearrange("p (k s) -> p k s", k=KC),
                               ACT.Copy).then_inc(hi_done, 1)

        @block.tensor
        def _(pe):
            for b in range(B):
                pe.wait_ge(ready, b + 1)
                if b >= 4:
                    pe.wait_ge(lo_done, b - 3)
                for k in range(KC):
                    t = pe.transpose(g.bank[b % 4][:, k * S:(k + 1) * S], y[:, b, k * P:(k + 1) * P],
                                     g.const("ident")[0:S, 0:S])
                t.then_inc(tr_done, 1)


def mm3(pe, out, w_hi, w_lo, x_hi, x_lo, first, last):
    pe.matmul(out, w_hi, x_hi, start=first, stop=False)
    pe.matmul(out, w_hi, x_lo, start=False, stop=False)
    return pe.matmul(out, w_lo, x_hi, start=False, stop=last)


def project(nc, g, name, w_dram, M, out, weights, bias=None, scale=None, rope=None, value=None, also=None,
            early=None):
    with ExitStack() as ctx:
        def sb(n, shape, dt=F32):
            return ctx.enter_context(nc.sbuf_tensor(f"{name}_{n}", shape, dt))

        sem = ctx.enter_context(semaphores(nc, name))

        raw, w_hi, w_lo = weights
        if also:
            also_dram, also_raw, also_all_hi, also_all_lo = also
            AW = also_raw.shape[1]
            also_in, also_hi, also_lo, also_seen = map(sem, ("also_in", "also_hi", "also_lo", "also_seen"))
        if early:
            early_in, early_hi, early_lo = map(sem, ("early_in", "early_hi", "early_lo"))
        raw_in = [sem("raw_in0"), sem("raw_in1")]
        hi_done, lo_done, mm_done, out_done = map(sem, ("hi", "lo", "mm", "out"))
        if rope:
            turned = sb("turned", [P, 4, HT])
            cosd = sb("cosd", [P, 4, HT])
            swap_done, sin_done, cos_done = map(sem, ("swap", "sin", "cos"))
        if value:
            v_dram, v_out, heads, hd, v_bias = value
            v_raw = sb("v_raw", [P, KC, D])
            v_hi = sb("v_hi", [P, KC, D], F32R)
            v_lo = sb("v_lo", [P, KC, D], F32R)
            v_in, v_set, v_hi_done, v_lo_done, v_mm, v_done = map(
                sem, ("v_in", "v_set", "v_hi", "v_lo", "v_mm", "v_done"))
        block = ctx.enter_context(nc.Block())

        def each_pair(e, body):
            with e.Fori(0, M // 2 - 1) as i:
                body(i, False)
            body(M // 2 - 1, True)

        def tokens(ap):
            return ap.rearrange("p (b s) -> p b s", b=HB)

        def table(ap):
            return ap.unsqueeze(1).broadcast_to([P, HB, S])

        @block.sync
        def _(sp):
            for u in range(2):
                sp.dma_start(raw[:, u, :], w_dram[2 + u]).then_inc(raw_in[u], 16)
            if value:
                sp.dma_start(v_raw[:, :, :], v_dram).then_inc(v_in, 16)
            if also:
                sp.dma_start(also_raw[:, :], also_dram[:, 0:AW]).then_inc(also_in, 16)

            def more_also(i):
                if also:
                    sp.wait_ge(also_lo, i)
                    sp.dma_start(also_raw[:, :], also_dram[:, bass.ds(i * AW, AW)]).then_inc(also_in, 16)

            if M > 4:
                with sp.Fori(1, M // 2 - 1) as i:
                    for u in range(2):
                        sp.wait_ge(lo_done, 2 * i + u + 1)
                        sp.dma_start(raw[:, u, :], w_dram[bass.ds(2 * i + u + 2, 1)].squeeze(0)).then_inc(raw_in[u], 16)
                    more_also(i)
            more_also(M // 2 - 1)
            if early:
                if early.reuses:
                    sp.wait_ge(lo_done, M)
                early.load(sp, early_in)

        @block.scalar
        def _(act):
            def split_high(i, u):
                act.wait_ge(raw_in[u], 16 * i)
                act.activation(w_hi[:, u, :], raw[:, u, :], ACT.Copy).then_inc(hi_done, 1)

            def body(i, last):
                for u in range(2):
                    if not last:
                        act.wait_ge(mm_done, 4 * i + 2 * u + 2)
                        split_high(i + 1, u)
                    for t in range(NH if rope else 0):
                        r = 2 * u + t
                        act.wait_ge(mm_done, 4 * i + r + 1)
                        act.wait_ge(out_done, 4 * i + r + 1)
                        act.activation(turned[0:64, r, :], g.bank[r][64:P, 0:HT], ACT.Copy).then_inc(swap_done, 1)
                        act.activation(turned[64:P, r, :], g.bank[r][0:64, 0:HT], ACT.Copy).then_inc(swap_done, 1)
                if also:
                    act.wait_ge(also_in, 16 * i + 16)
                    act.activation(also_all_hi[:, bass.ds(i * AW, AW)], also_raw[:, :], ACT.Copy).then_inc(also_hi, 1)

            act.sem_inc(hi_done, 2)
            each_pair(act, body)
            if early and not early.reuses:
                early.split_high(act, early_in, early_hi)
            if value:
                act.wait_ge(v_in, 16)
                act.activation(v_hi[:, :, :], v_raw[:, :, :], ACT.Copy).then_inc(v_hi_done, 1)
            if early and early.reuses:
                act.wait_ge(mm_done, 2 * M)
                early.split_high(act, early_in, early_hi)
            if value and heads is None:
                for b in range(B):
                    act.wait_ge(v_mm, b + 1)
                    act.activation(v_out[:, b, :], g.bank[4 + b % 4][0:S, :], ACT.Sigmoid).then_inc(v_done, 1)

        @block.gpsimd
        def _(pool):
            pool.sem_inc(lo_done, 2)
            if value and hd not in (None, P):
                pool.memset(v_out[:, :, :], 0.0).then_inc(v_set, 1)
                pool.wait_ge(v_set, 1)
                pool.memset(v_out[:, :, 0:heads * (hd + 1)].rearrange("p b (h e) -> p b h e", e=hd + 1)[:, :, :, hd],
                            1.0).then_inc(v_set, 1)
            def split_low(i, u):
                pool.wait_ge(hi_done, 2 * i + u + 1)
                pool.tensor_tensor(w_lo[:, u, :], raw[:, u, :], w_hi[:, u, :].bitcast(F32),
                                   ALU.subtract).then_inc(lo_done, 1)

            def body(i, last):
                for u in range(2):
                    if not last:
                        split_low(i + 1, u)
                    for t in range(NH if rope else 0):
                        r = 2 * u + t
                        pool.wait_ge(swap_done, 8 * i + 2 * r + 2)
                        pool.tensor_tensor(tokens(turned[:, r, :]), tokens(turned[:, r, :]), table(rope[1]),
                                           ALU.mult).then_inc(sin_done, 1)
                if also:
                    pool.wait_ge(also_hi, i + 1)
                    pool.sem_inc(also_seen, 1)
                    pool.tensor_tensor(also_all_lo[:, bass.ds(i * AW, AW)], also_raw[:, :],
                                       also_all_hi[:, bass.ds(i * AW, AW)].bitcast(F32), ALU.subtract).then_inc(also_lo, 1)

            each_pair(pool, body)
            if early and early.reuses:
                early.split_low(pool, early_hi, early_lo)

        @block.vector
        def _(dve):
            dve.sem_inc(out_done, 4)
            with dve.Fori(0, M // 2) as i:
                for u in range(2):
                    for t in range(NH):
                        r = 2 * u + t
                        dve.wait_ge(mm_done, 4 * i + r + 1)
                        dst = out[:, 2 * i + u, t * HT:(t + 1) * HT]
                        if rope:
                            dve.wait_ge(swap_done, 8 * i + 2 * r + 2)
                            dve.tensor_tensor(tokens(cosd[:, r, :]), tokens(g.bank[r][:, 0:HT]), table(rope[0]),
                                              ALU.mult).then_inc(cos_done, 1)
                        elif bias is not None:
                            dve.tensor_scalar(dst, g.bank[r][:, 0:HT], bias[:, bass.ds(2 * i + u, 1)], scale or 1.0,
                                              ALU.add, ALU.mult).then_inc(out_done, 1)
                        else:
                            dve.tensor_scalar(dst, g.bank[r][:, 0:HT], scale or 1.0, None,
                                              ALU.mult).then_inc(out_done, 1)
                    if rope:
                        for t in range(NH):
                            r = 2 * u + t
                            dve.wait_ge(sin_done, 4 * i + r + 1)
                            dve.wait_ge(cos_done, 4 * i + r + 1)
                            dve.tensor_tensor(out[:, 2 * i + u, t * HT:(t + 1) * HT], cosd[:, r, :], turned[:, r, :],
                                              ALU.add).then_inc(out_done, 1)
            if early and not early.reuses:
                early.split_low(dve, early_hi, early_lo)
            if value:
                dve.wait_ge(v_hi_done, 1)
                dve.tensor_tensor(v_lo[:, :, :], v_raw[:, :, :], v_hi[:, :, :].bitcast(F32),
                                  ALU.subtract).then_inc(v_lo_done, 1)
                if hd not in (None, P):
                    dve.wait_ge(v_set, 2)
                for b in range(B if heads is not None else 0):
                    dve.wait_ge(v_mm, b + 1)
                    if hd == P:
                        dst = v_out[0:S, b, :].rearrange("p (h e) -> p h e", e=hd)
                    else:
                        dst = v_out[0:S, b, 0:heads * (hd + 1)].rearrange("p (h e) -> p h e", e=hd + 1)[:, :, 0:hd]
                    src = g.bank[4 + b % 4][0:S, :].rearrange("p (h e) -> p h e", e=hd)
                    if v_bias is not None:
                        dve.tensor_tensor(dst, src, v_bias.rearrange("p (h e) -> p h e", e=hd),
                                          ALU.add).then_inc(v_done, 1)
                    else:
                        dve.tensor_copy(dst, src).then_inc(v_done, 1)

        @block.tensor
        def _(pe):
            with pe.Fori(0, M // 2) as i:
                for u in range(2):
                    pe.wait_ge(lo_done, 2 * i + u + 1)
                    for t in range(NH):
                        r = 2 * u + t
                        pe.wait_ge(out_done, 4 * i + r + 1)
                        for k in range(KC):
                            x = mm3(pe, g.bank[r][:, 0:HT], w_hi[:, u, k * P:(k + 1) * P], w_lo[:, u, k * P:(k + 1) * P],
                                    g.hT_hi[:, k, t * HT:(t + 1) * HT], g.hT_lo[:, k, t * HT:(t + 1) * HT],
                                    k == 0, k == KC - 1)
                        x.then_inc(mm_done, 1)
            if value:
                pe.wait_ge(v_lo_done, 1)
                for b in range(B):
                    if b >= 4:
                        pe.wait_ge(v_done, b - 3)
                    for k in range(KC):
                        x = mm3(pe, g.bank[4 + b % 4][0:S, :], g.hT_hi[:, k, b * S:(b + 1) * S],
                                g.hT_lo[:, k, b * S:(b + 1) * S], v_hi[:, k, :], v_lo[:, k, :], k == 0, k == KC - 1)
                    x.then_inc(v_mm, 1)


def self_attention(nc, g, name, x, qT, kT, v, heads, hd, scale, head_mask, bias, wo_dram, wo_bias=None, sink=None,
                   bias_load=None):
    G = heads // 4
    per_chunk = heads // KC // 4
    NK = S + 1 if sink is not None else S
    VE = hd + 1
    with ExitStack() as ctx:
        def sb(n, shape, dt=F32):
            return ctx.enter_context(nc.sbuf_tensor(f"{name}_{n}", shape, dt))

        sem = ctx.enter_context(semaphores(nc, name))

        wo = sb("wo", [P, KC, D])
        q_now = sb("q_now", [P, KC, S])
        k_diag = sb("k_diag", [P, 4, 4, S])
        s_rows = sb("s_rows", [S, G if sink is not None else 4, 4, NK])
        p_rows = sb("p_rows", [S, 4, 4, NK])
        pT = sb("pT", [NK, 2, 4, S])
        top = sb("top", [S, 4, 4])
        o_rows = sb("o_rows", [S, heads, VE])
        r_den = sb("r_den", [S, heads])
        o_norm = sb("o_norm", [S, D])
        oT = sb("oT", [P, KC, S])
        ps_s = g.bank[0:2]
        ps_t = g.bank[2:4]
        ps_o = g.bank[4:6]
        ps_c = g.bank[6]
        ps_y = g.bank[7]
        (wo_in, kd_done, q_done, s_done, sr_done, top_done, sub_done, exp_done, t_done, pT_done, pv_done, or_done,
         den_done, on_done, c_done, oT_done, y_done, add_done, bo_done, sink_done, free_seen) = map(sem, (
             "wo_in", "kd", "q", "s", "sr", "top", "sub", "exp", "t", "pT", "pv", "or", "den", "on", "c", "oT",
             "y", "add", "bo", "sink", "free_seen"))
        if bias_load:
            bias_in = sem("bias_in")
        block = ctx.enter_context(nc.Block())

        def sr(grp):
            return s_rows[:, grp if sink is not None else grp % 4]

        def each_batch(e, body):
            body(0, True, False)
            with e.Fori(1, B - 1) as b:
                body(b, False, False)
            body(B - 1, False, True)

        @block.sync
        def _(sp):
            if bias_load:
                sp.dma_start(bias_load[0][:, :, :], bias_load[1]).then_inc(bias_in, 16)
            sp.dma_start(wo[:, :, :], wo_dram).then_inc(wo_in, 16)

        @block.gpsimd
        def _(pool):
            def diagonal(b, grp):
                c = grp // per_chunk
                j0 = 4 * (grp % per_chunk)
                pool.tensor_tensor(
                    k_diag[:, grp % 4], kT[:, c, bass.ds(b * S, S)].unsqueeze(1).broadcast_to([P, 4, S]),
                    head_mask[:, j0:j0 + 4].unsqueeze(2).broadcast_to([P, 4, S]), ALU.mult).then_inc(kd_done, 1)

            def subtract(n, grp):
                pool.wait_ge(top_done, n + 1)
                pool.tensor_tensor(p_rows[:, grp % 4], sr(grp),
                                   top[:, grp % 4, :].unsqueeze(2).broadcast_to([S, 4, NK]),
                                   ALU.subtract).then_inc(sub_done, 1)

            def body(b, first, last):
                if wo_bias is not None:
                    pool.tensor_tensor(x[:, bass.ds(b, 1), :], x[:, bass.ds(b, 1), :], wo_bias.unsqueeze(1),
                                       ALU.add).then_inc(bo_done, 1)
                for grp in range(G):
                    n = b * G + grp
                    if not (last and grp + 4 >= G):
                        pool.wait_ge(s_done, n + 1)
                        pool.sem_inc(free_seen, 1)
                        diagonal(b + (grp + 4) // G, (grp + 4) % G)
                    if not (last and grp + 2 >= G):
                        subtract(n + 2, (grp + 2) % G)

            if sink is not None:
                pool.tensor_copy(s_rows[:, :, :, S], sink.rearrange("p (g h) -> p g h", h=4)).then_inc(sink_done, 1)
            for grp in range(4):
                diagonal(0, grp)
            for grp in range(2):
                if sink is not None and grp == 0:
                    pool.wait_ge(sink_done, 1)
                subtract(grp, grp)
            each_batch(pool, body)

        @block.scalar
        def _(act):
            def take_q(b):
                act.activation(q_now[:, :, :], qT[:, :, bass.ds(b * S, S)], ACT.Copy).then_inc(q_done, 1)

            def exponent(n, grp):
                act.wait_ge(sub_done, n + 1)
                act.activation(p_rows[:, grp % 4], p_rows[:, grp % 4], ACT.Exp).then_inc(exp_done, 1)

            def body(b, first, last):
                for grp in range(G):
                    n = b * G + grp
                    act.wait_ge(t_done, n + 1)
                    act.activation(pT[:, grp % 2], ps_t[grp % 2][0:NK, 0:4 * S].rearrange("p (h s) -> p h s", h=4),
                                   ACT.Copy).then_inc(pT_done, 1)
                    if grp == G - 2 and not last:
                        act.wait_ge(s_done, n + 2)
                        take_q(b + 1)
                    if not (last and grp + 1 >= G):
                        exponent(n + 1, (grp + 1) % G)
                    if grp == 1 and not first:
                        collect(b - 1)

            def collect(b):
                act.wait_ge(c_done, b + 1)
                act.activation(oT[:, :, :], ps_c[:, 0:KC * S].rearrange("p (k s) -> p k s", k=KC),
                               ACT.Copy).then_inc(oT_done, 1)

            take_q(0)
            exponent(0, 0)
            each_batch(act, body)
            collect(B - 1)

        @block.vector
        def _(dve):
            def scale_bias_max(n, grp):
                dve.wait_ge(s_done, n + 1)
                dve.scalar_tensor_tensor(sr(grp)[:, :, 0:S], ps_s[grp % 2][0:S, 0:4 * S].rearrange("p (h s) -> p h s", h=4),
                                         scale, bias(grp), ALU.mult, ALU.add).then_inc(sr_done, 1)
                dve.wait_ge(sr_done, n + 1)
                dve.tensor_reduce(top[:, grp % 4, :], sr(grp), AX_X, ALU.max).then_inc(top_done, 1)

            def add(b):
                dve.wait_ge(y_done, b + 1)
                dve.wait_ge(bo_done, b + 1) if wo_bias is not None else None
                dve.tensor_tensor(x[:, bass.ds(b, 1), :], ps_y[0:S, :].unsqueeze(1), x[:, bass.ds(b, 1), :],
                                  ALU.add).then_inc(add_done, 1)

            def row_stats(b):
                dve.wait_ge(add_done, b + 1)
                dve.bn_stats(g.stats[:, bass.ds(b, 1), :].squeeze(1), x[:, bass.ds(b, 1), :].squeeze(1))

            def body(b, first, last):
                for grp in range(G):
                    n = b * G + grp
                    if not (last and grp + 2 >= G):
                        scale_bias_max(n + 2, (grp + 2) % G)
                    dve.wait_ge(pv_done, n + 1)
                    dve.tensor_copy(o_rows[:, 4 * grp:4 * grp + 4, :],
                                    ps_o[grp % 2][0:S, 0:4 * PVW].rearrange("p (h e) -> p h e", h=4)[:, :, 0:VE]
                                    ).then_inc(or_done, 1)
                    if grp == 3 and not first:
                        add(b - 1)
                dve.wait_ge(or_done, b * G + G + 2)
                dve.reciprocal(r_den[:, :], o_rows[:, :, hd]).then_inc(den_done, 1)
                dve.wait_ge(den_done, b + 1)
                dve.tensor_tensor(o_norm[:, :].rearrange("p (h e) -> p h e", h=heads), o_rows[:, :, 0:hd],
                                  r_den[:, :].unsqueeze(2).broadcast_to([S, heads, hd]), ALU.mult).then_inc(on_done, 1)
                if not first:
                    row_stats(b - 1)

            dve.sem_inc(or_done, 2)
            if sink is not None:
                dve.wait_ge(sink_done, 1)
            if bias_load:
                dve.wait_ge(bias_in, 16)
            for grp in range(2):
                scale_bias_max(grp, grp)
            each_batch(dve, body)
            add(B - 1)
            row_stats(B - 1)

        @block.tensor
        def _(pe):
            def scores(n, b, grp):
                pe.wait_ge(kd_done, n + 1)
                pe.wait_ge(q_done, b + 1)
                pe.matmul(ps_s[grp % 2][0:S, 0:4 * S], q_now[:, grp // per_chunk, :], k_diag[:, grp % 4],
                          start=True, stop=True).then_inc(s_done, 1)

            def context_rows(b):
                pe.wait_ge(on_done, b + 1)
                for k in range(KC):
                    t = pe.transpose(ps_c[:, k * S:(k + 1) * S], o_norm[:, k * P:(k + 1) * P],
                                     g.const("ident")[0:S, 0:S])
                t.then_inc(c_done, 1)

            def out_rows(b):
                pe.wait_ge(oT_done, b + 1)
                for k in range(KC):
                    y = pe.matmul(ps_y[0:S, :], oT[:, k, :], wo[:, k, :], start=(k == 0), stop=(k == KC - 1))
                y.then_inc(y_done, 1)

            def body(b, first, last):
                for grp in range(G):
                    n = b * G + grp
                    pe.wait_ge(exp_done, n + 1)
                    for j in range(4):
                        t = pe.transpose(ps_t[grp % 2][0:NK, j * S:(j + 1) * S], p_rows[:, grp % 4, j, :],
                                         g.const("ident")[0:S, 0:S])
                    t.then_inc(t_done, 1)
                    if not (last and grp + 2 >= G):
                        pe.wait_ge(sr_done, n + 1)
                        scores(n + 2, b + (grp + 2) // G, (grp + 2) % G)
                    if grp == 1 and not first:
                        context_rows(b - 1)
                    if grp == 2 and not first:
                        out_rows(b - 1)
                    pe.wait_ge(pT_done, n + 1)
                    pe.wait_ge(or_done, n + 1)
                    for j in range(4):
                        h = 4 * grp + j
                        o = pe.matmul(ps_o[grp % 2][0:S, j * PVW:(j + 1) * PVW], pT[:, grp % 2, j, :],
                                      v[0:NK, bass.ds(b, 1), VE * h:VE * h + PVW], start=True, stop=True)
                    o.then_inc(pv_done, 1)

            for grp in range(2):
                scores(grp, 0, grp)
            pe.wait_ge(wo_in, 16)
            each_batch(pe, body)
            context_rows(B - 1)
            out_rows(B - 1)


def cross_attention(nc, g, name, x, qT, ctx_dram, context, w_hi, w_lo, wo_dram, kind, k_bias=None, v_bias=None,
                    mask_cols=None, mask_row=None, gate=None, norm=None):
    H, HD, VE = 16, 32, 33
    clip = kind == "clip"
    with ExitStack() as ctx:
        def sb(n, shape, dt=F32):
            return ctx.enter_context(nc.sbuf_tensor(f"{name}_{n}", shape, dt))

        sem = ctx.enter_context(semaphores(nc, name))

        wo = sb("wo", [P, KC, D])
        c_raw, c_hi, c_lo = context
        kT = sb("kT", [P, KC, S2P])
        v = sb("v", [CW, CK, vw(H, HD)])
        q_diag = sb("q_diag", [P, KC, 4, S])
        o_rows = sb("o_rows", [S, H, VE])
        r_den = sb("r_den", [S, H])
        o_norm = sb("o_norm", [S, D])
        oT = sb("oT", [P, KC, S])
        y_rows = sb("y_rows", [S, D])
        (wo_in, c_in, c_hi_done, c_lo_done, v_set, kv_mm, kv_done, qd_done,
         s_done, exp_done, pv_done, or_done, den_done, r_done, on_done, c_done, oT_done, y_done, add_done,
         rows_done, one_done, free_seen, st_seen) = map(sem, (
             "wo_in", "c_in", "c_hi", "c_lo", "v_set", "kv_mm", "kv", "qd", "s", "exp",
             "pv", "or", "den", "r", "on", "c", "oT", "y", "add", "rows", "one", "free_seen", "st_seen"))
        if clip:
            s_clip = sb("s_clip", [CW, CK, 4, S])
            pT = sb("pT", [CW, 2, CK, 4, S])
            stats = sb("stats", [S, 6])
            mv = sb("mv", [S, 2])
            var = sb("var", [S, 1])
            rstd = sb("rstd", [S, 1])
            scaled = sb("scaled", [S, D])
            clip_done, beta_done, st_done, mv_done, var_done, rstd_done, sc_done = map(
                sem, ("clip", "beta", "st", "mv", "var", "rstd", "sc"))
            ps_s, ps_kv = g.bank[0:3], g.bank[3:5]
        else:
            p_rows = sb("p_rows", [S, 2, S2])
            pT = sb("pT", [CW, 2, CK, S])
            n_top = sb("n_top", [S, H])
            one_row = sb("one_row", [1, S], BF16)
            top_done, t_done, pT_done = map(sem, ("top", "t", "pT"))
            ps_s, ps_t = g.bank[0:2], g.bank[2:4]
            ps_kv = ps_t
        ps_o, ps_y = g.bank[5:7], g.bank[7]
        SU = CK * KC if clip else H
        S0, KV0, OR0 = SU, 2, 2
        block = ctx.enter_context(nc.Block())

        def each_batch(e, body):
            body(0, True, False)
            with e.Fori(1, B - 1) as b:
                body(b, False, False)
            body(B - 1, False, True)

        @block.sync
        def _(sp):
            sp.dma_start(wo[:, :, :], wo_dram).then_inc(wo_in, 16)
            with sp.Fori(0, B - 1) as b:
                sp.wait_ge(c_lo_done, b + 1)
                sp.dma_start(c_raw[:, :, :], ctx_dram[bass.ds(b + 1, 1)].squeeze(0)).then_inc(c_in, 16)

        @block.gpsimd
        def _(pool):
            def split_low(b):
                pool.wait_ge(c_hi_done, b + 1)
                pool.tensor_tensor(c_lo[:, :, :], c_raw[:, :, :], c_hi[:, :, :].bitcast(F32),
                                   ALU.subtract).then_inc(c_lo_done, 1)

            def body(b, first, last):
                for c in range(KC):
                    pool.wait_ge(s_done, SU * b + (SU // KC) * (c + 1))
                    pool.sem_inc(free_seen, 1)
                    pool.tensor_tensor(q_diag[:, c], qT[:, c, bass.ds(b * S, S)].unsqueeze(1).broadcast_to([P, 4, S]),
                                       g.const("hm32").unsqueeze(2).broadcast_to([P, 4, S]),
                                       ALU.mult).then_inc(qd_done, 1)
                if clip:
                    pool.tensor_tensor(x[:, bass.ds(b, 1), :], x[:, bass.ds(b, 1), :], norm.beta.unsqueeze(1),
                                       ALU.add).then_inc(beta_done, 1)
                    if not first:
                        root(b - 1)
                if not last:
                    split_low(b + 1)

            def root(b):
                pool.wait_ge(var_done, b + 1)
                pool.tensor_tensor(rstd[:, :], var[:, :], g.const("power")[0:S, 0:1], ALU.pow).then_inc(rstd_done, 1)

            pool.sem_inc(c_lo_done, 1)
            pool.memset(v[:, :, :], 0.0).then_inc(v_set, 1)
            pool.wait_ge(v_set, 1)
            pool.memset(v[:, :, 0:H * VE].rearrange("p c (h e) -> p c h e", e=VE)[:, :, :, HD], 1.0).then_inc(v_set, 1)
            if not clip:
                pool.memset(one_row[:, :], 1.0).then_inc(v_set, 1)
            each_batch(pool, body)
            if clip:
                root(B - 1)

        @block.scalar
        def _(act):
            def split_high(b):
                act.wait_ge(c_in, 16 * b)
                act.wait_ge(c_lo_done, b) if not isinstance(b, int) or b else None
                act.wait_ge(kv_mm, 7 * b) if not isinstance(b, int) or b else None
                act.activation(c_hi[:, :, :], c_raw[:, :, :], ACT.Copy).then_inc(c_hi_done, 1)

            def collect(b):
                act.wait_ge(c_done, b + 1)
                act.activation(oT[:, :, :], ps_y[:, 0:KC * S].rearrange("p (k s) -> p k s", k=KC),
                               ACT.Copy).then_inc(oT_done, 1)

            def body(b, first, last):
                if not first:
                    collect(b - 1)
                for u in range(SU):
                    n = SU * b + u
                    if clip:
                        act.wait_ge(clip_done, n + 1 + CK)
                        act.activation(pT[:, u // CK % 2, u % CK], s_clip[:, u % CK], ACT.Exp).then_inc(exp_done, 1)
                    else:
                        act.wait_ge(top_done, n + 1)
                        act.activation(p_rows[:, u % 2, :], ps_s[u % 2][0:S, 0:S2], ACT.Exp,
                                       bias=n_top[:, u:u + 1]).then_inc(exp_done, 1)
                    if u == 3 and not last:
                        split_high(b + 1)

            act.sem_inc(c_hi_done, 1)
            each_batch(act, body)
            collect(B - 1)

        @block.vector
        def _(dve):
            def keys_values(b, m):
                dve.wait_ge(kv_mm, 7 * b + m + 1)
                if m < KC:
                    if k_bias is not None:
                        dve.tensor_scalar(kT[:, m, :], ps_kv[m % 2][:, 0:S2P], k_bias[:, m:m + 1], None,
                                          ALU.add).then_inc(kv_done, 1)
                    else:
                        dve.tensor_copy(kT[:, m, :], ps_kv[m % 2][:, 0:S2P]).then_inc(kv_done, 1)
                    return
                c = m - KC
                rows = v[:, c, 0:H * VE].rearrange("p (h e) -> p h e", e=VE)
                src = ps_kv[m % 2][0:CW, :].rearrange("p (h e) -> p h e", e=HD)
                if clip:
                    dve.tensor_tensor(rows[:, :, 0:HD], src, v_bias.rearrange("p (h e) -> p h e", e=HD),
                                      ALU.add).then_inc(kv_done, 1)
                else:
                    m_col = mask_cols[:, bass.ds(b * CK + c, 1)]
                    dve.tensor_scalar(rows[:, :, HD], g.ones[0:CW, 0:H], m_col, None, ALU.mult).then_inc(one_done, 1)
                    dve.tensor_scalar(rows[:, :, 0:HD], src, m_col, None, ALU.mult).then_inc(kv_done, 1)

            def clip_scores(n, b, kc):
                dve.wait_ge(s_done, S0 + n + 1)
                dve.wait_ge(exp_done, n + 1)
                dve.tensor_scalar(s_clip[:, kc], ps_s[kc][0:CW, 0:4 * S].rearrange("p (h s) -> p h s", h=4),
                                  -50.0, mask_cols[:, bass.ds(b * CK + kc, 1)], ALU.max, ALU.min).then_inc(clip_done, 1)

            def top(n, h):
                dve.wait_ge(s_done, S0 + n + 1)
                dve.tensor_reduce(n_top[:, h:h + 1], ps_s[h % 2][0:S, 0:S2], AX_X, ALU.max,
                                  negate=True).then_inc(top_done, 1)

            def out_group(b, c):
                dve.wait_ge(pv_done, 4 * b + c + 1)
                dve.tensor_copy(o_rows[:, 4 * c:4 * c + 4, :],
                                ps_o[c % 2][0:S, 0:4 * PVW].rearrange("p (h e) -> p h e", h=4)[:, :, 0:VE]
                                ).then_inc(or_done, 1)

            def normalise_rows(b):
                dve.wait_ge(or_done, 4 * b + 4 + OR0)
                if clip:
                    dve.reciprocal(r_den[:, :], o_rows[:, :, HD]).then_inc(r_done, 1)
                else:
                    dve.tensor_scalar(r_den[:, :], o_rows[:, :, HD], 1e-30, None, ALU.max).then_inc(den_done, 1)
                    dve.wait_ge(den_done, b + 1)
                    dve.reciprocal(r_den[:, :], r_den[:, :]).then_inc(r_done, 1)
                dve.wait_ge(r_done, b + 1)
                dve.tensor_tensor(o_norm[:, :].rearrange("p (h e) -> p h e", h=H), o_rows[:, :, 0:HD],
                                  r_den[:, :].unsqueeze(2).broadcast_to([S, H, HD]), ALU.mult).then_inc(on_done, 1)

            def add(b):
                xb = x[:, bass.ds(b, 1), :].squeeze(1)
                dve.wait_ge(y_done, b + 1)
                if clip:
                    dve.scalar_tensor_tensor(y_rows[:, :], ps_y[0:S, :], norm.rs, norm.bo_rs,
                                             ALU.mult, ALU.add).then_inc(rows_done, 1)
                    dve.wait_ge(rows_done, b + 1)
                    dve.bn_stats(stats[:, :], y_rows[:, :]).then_inc(st_done, 1)
                    dve.wait_ge(st_done, b + 1)
                    dve.sem_inc(st_seen, 1)
                    dve.bn_aggr(mv[:, :], stats[:, :]).then_inc(mv_done, 1)
                    dve.wait_ge(mv_done, b + 1)
                    dve.tensor_scalar(var[:, :], mv[:, 1:2], 1e-5, None, ALU.add).then_inc(var_done, 1)
                    dve.scalar_tensor_tensor(scaled[:, :], y_rows[:, :], mv[:, 0:1], norm.gamma,
                                             ALU.subtract, ALU.mult).then_inc(sc_done, 1)
                    dve.wait_ge(sc_done, b + 1)
                    dve.wait_ge(rstd_done, b + 1)
                    dve.wait_ge(beta_done, b + 1)
                    dve.scalar_tensor_tensor(xb, scaled[:, :], rstd[:, 0:1], xb, ALU.mult, ALU.add).then_inc(add_done, 1)
                else:
                    dve.tensor_tensor(y_rows[:, :], ps_y[0:S, :], gate[:, bass.ds(b, 1), :].squeeze(1),
                                      ALU.mult).then_inc(rows_done, 1)
                    dve.wait_ge(rows_done, b + 1)
                    dve.tensor_tensor(xb, xb, y_rows[:, :], ALU.add).then_inc(add_done, 1)
                dve.wait_ge(add_done, b + 1)
                dve.bn_stats(g.stats[:, bass.ds(b, 1), :].squeeze(1), xb)

            def body(b, first, last):
                for m in range(KC + CK):
                    keys_values(b, m)
                if clip:
                    for u in range(2 * CK):
                        clip_scores(SU * b + u, b, u % CK)
                    if not first:
                        add(b - 1)
                    for c in range(KC):
                        out_group(b, c)
                        for kc in range(CK):
                            if c + 2 < KC:
                                clip_scores(SU * b + (c + 2) * CK + kc, b, kc)
                else:
                    top(H * b, 0)
                    top(H * b + 1, 1)
                    if not first:
                        add(b - 1)
                    for h in range(H):
                        n = H * b + h
                        dve.wait_ge(t_done, n + 1)
                        dve.tensor_copy(pT[:, h % 2], ps_t[h % 2][0:CW, 0:CK * S].rearrange("p (c s) -> p c s", c=CK)
                                        ).then_inc(pT_done, 1)
                        if h + 2 < H:
                            top(n + 2, h + 2)
                        if h % 4 == 0 and h:
                            out_group(b, h // 4 - 1)
                    out_group(b, KC - 1)
                normalise_rows(b)

            dve.sem_inc(kv_done, KV0)
            dve.sem_inc(or_done, OR0)
            if clip:
                dve.sem_inc(clip_done, CK)
                dve.sem_inc(exp_done, CK)
            dve.wait_ge(v_set, 2)
            each_batch(dve, body)
            add(B - 1)

        @block.tensor
        def _(pe):
            def keys(b, m):
                pe.wait_ge(kv_done, 7 * b + m + 1)
                for k in range(KC):
                    y = mm3(pe, ps_kv[m % 2][:, 0:S2P], w_hi[:, 0, k, m * P:(m + 1) * P], w_lo[:, 0, k, m * P:(m + 1) * P],
                            c_hi[:, k, :], c_lo[:, k, :], k == 0, k == KC - 1)
                y.then_inc(kv_mm, 1)

            def values(b, c):
                pe.wait_ge(kv_done, 7 * b + KC + c + 1)
                for k in range(KC):
                    y = mm3(pe, ps_kv[(KC + c) % 2][0:CW, :], c_hi[:, k, c * CW:(c + 1) * CW],
                            c_lo[:, k, c * CW:(c + 1) * CW], w_hi[:, 1, k, :], w_lo[:, 1, k, :], k == 0, k == KC - 1)
                y.then_inc(kv_mm, 1)

            def context_rows(b):
                pe.wait_ge(on_done, b + 1)
                for k in range(KC):
                    t = pe.transpose(ps_y[:, k * S:(k + 1) * S], o_norm[:, k * P:(k + 1) * P],
                                     g.const("ident")[0:S, 0:S])
                t.then_inc(c_done, 1)

            def out_rows(b):
                pe.wait_ge(oT_done, b + 1)
                for k in range(KC):
                    y = pe.matmul(ps_y[0:S, :], oT[:, k, :], wo[:, k, :], start=(k == 0), stop=(k == KC - 1))
                y.then_inc(y_done, 1)

            def scores_clip(b, c):
                pe.wait_ge(qd_done, KC * b + c + 1)
                for kc in range(CK):
                    n = SU * b + c * CK + kc
                    pe.wait_ge(clip_done, n + 1)
                    pe.matmul(ps_s[kc][0:CW, 0:4 * S], kT[:, c, kc * CW:(kc + 1) * CW], q_diag[:, c],
                              start=True, stop=True).then_inc(s_done, 1)

            def pv_clip(b, c):
                pe.wait_ge(exp_done, SU * b + (c + 1) * CK + CK)
                pe.wait_ge(or_done, KC * b + c + 1)
                for j in range(4):
                    for kc in range(CK):
                        o = pe.matmul(ps_o[c % 2][0:S, j * PVW:(j + 1) * PVW], pT[:, c % 2, kc, j, :],
                                      v[:, kc, VE * (4 * c + j):VE * (4 * c + j) + PVW],
                                      start=(kc == 0), stop=(kc == CK - 1))
                o.then_inc(pv_done, 1)

            def scores_max(b, h):
                pe.wait_ge(qd_done, KC * b + h // 4 + 1)
                pe.matmul(ps_s[h % 2][0:S, 0:S2], q_diag[:, h // 4, h % 4, :], kT[:, h // 4, 0:S2], start=True, stop=False)
                pe.matmul(ps_s[h % 2][0:S, 0:S2], one_row[:, :], mask_row[:, bass.ds(b * S2, S2)],
                          start=False, stop=True).then_inc(s_done, 1)

            def turn(b, h):
                pe.wait_ge(exp_done, H * b + h + 1)
                for kc in range(CK):
                    t = pe.transpose(ps_t[h % 2][0:CW, kc * S:(kc + 1) * S], p_rows[:, h % 2, kc * CW:(kc + 1) * CW],
                                     g.const("ident")[0:S, 0:S])
                t.then_inc(t_done, 1)

            def pv_max(b, h):
                pe.wait_ge(pT_done, H * b + h + 1)
                if h % 4 == 0:
                    pe.wait_ge(or_done, KC * b + h // 4 + 1)
                for kc in range(CK):
                    o = pe.matmul(ps_o[h // 4 % 2][0:S, h % 4 * PVW:(h % 4 + 1) * PVW], pT[:, h % 2, kc, :],
                                  v[:, kc, VE * h:VE * h + PVW], start=(kc == 0), stop=(kc == CK - 1))
                if h % 4 == 3:
                    o.then_inc(pv_done, 1)

            def body(b, first, last):
                pe.wait_ge(c_lo_done, b + 1)
                for m in range(KC):
                    keys(b, m)
                if not first:
                    context_rows(b - 1)
                for c in range(CK):
                    values(b, c)
                if first:
                    pe.wait_ge(wo_in, 16)
                else:
                    out_rows(b - 1)
                pe.wait_ge(kv_done, 7 * b + KC + KV0)
                if clip:
                    scores_clip(b, 0)
                    scores_clip(b, 1)
                    pe.wait_ge(kv_done, 7 * b + KC + CK + KV0)
                    for c in range(KC):
                        pv_clip(b, c)
                        if c + 2 < KC:
                            scores_clip(b, c + 2)
                else:
                    scores_max(b, 0)
                    scores_max(b, 1)
                    pe.wait_ge(kv_done, 7 * b + KC + CK + KV0)
                    for h in range(H):
                        turn(b, h)
                        if h + 2 < H:
                            scores_max(b, h + 2)
                        if h:
                            pv_max(b, h - 1)
                    pv_max(b, H - 1)

            pe.sem_inc(s_done, S0)
            if not clip:
                pe.wait_ge(v_set, 3)
            each_batch(pe, body)
            context_rows(B - 1)
            out_rows(B - 1)


def group_attention(nc, g, name, x2, q, kT, v, grp, wo_hi, wo_lo, causal, early=None):
    W = 4 * S
    scale = float(P) ** -0.5
    with ExitStack() as ctx:
        def sb(n, shape, dt=F32):
            return ctx.enter_context(nc.sbuf_tensor(f"{name}_{n}", shape, dt))

        sem = ctx.enter_context(semaphores(nc, name))

        q_now = sb("q_now", [P, 2, 4, S])
        v_now = sb("v_now", [S, P])
        p_rows = sb("p_rows", [S, 2, 4, S])
        pT = sb("pT", [S, 2, 4, S])
        top = sb("top", [S, 2, 4])
        den = sb("den", [S, 2, 4])
        r_den = sb("r_den", [S, 2, 4])
        oT_hi = sb("oT_hi", [P, 2, 4, S], F32R)
        oT_lo = sb("oT_lo", [P, 2, 4, S], F32R)
        ps_s, ps_t, ps_o, ps_y = g.bank[0:2], g.bank[2:4], g.bank[4:6], g.bank[6:8]
        (q_done, v_done, s_done, sr_done, top_done, sub_done, exp_done, den_done, r_done, pn_done, t_done, pT_done,
         pv_done, oh_done, ol_done, y_done, add_done) = map(sem, (
             "q", "v", "s", "sr", "top", "sub", "exp", "den", "r", "pn", "t", "pT", "pv", "oh", "ol", "y", "add"))
        if early:
            early_in, early_hi, early_lo = map(sem, ("early_in", "early_hi", "early_lo"))
        block = ctx.enter_context(nc.Block())

        def heads(ap):
            return ap[:, 0:W].rearrange("p (h s) -> p h s", h=4)

        def each_batch(e, body):
            body(0, True, 2)
            with e.Fori(1, B - 2) as b:
                body(b, False, 2)
            body(B - 2, False, 1)
            body(B - 1, False, 0)

        if early:
            @block.sync
            def _(sp):
                early.load(sp, early_in)

        @block.gpsimd
        def _(pool):
            def subtract(n, u):
                pool.wait_ge(top_done, n + 1)
                pool.tensor_tensor(p_rows[:, u], p_rows[:, u], top[:, u, :].unsqueeze(2).broadcast_to([S, 4, S]),
                                   ALU.subtract).then_inc(sub_done, 1)

            def probabilities(n, u):
                pool.wait_ge(r_done, n + 1)
                pool.tensor_tensor(p_rows[:, u], p_rows[:, u], r_den[:, u, :].unsqueeze(2).broadcast_to([S, 4, S]),
                                   ALU.mult).then_inc(pn_done, 1)

            def softmax(b):
                for u in range(2):
                    subtract(2 * b + u, u)
                for u in range(2):
                    probabilities(2 * b + u, u)

            def body(b, first, left):
                if left:
                    softmax(b + 1)

            softmax(0)
            each_batch(pool, body)
            if early:
                early.split_low(pool, early_hi, early_lo)

        @block.scalar
        def _(act):
            def take_q(b):
                for u in range(2):
                    act.activation(q_now[:, u], q[:, 4 * u:4 * u + 4, bass.ds(b * S, S)], ACT.Copy).then_inc(q_done, 1)

            def take_v(b):
                act.activation(v_now[:, :], v[:, bass.ds(b, 1), grp * P:(grp + 1) * P].squeeze(1), ACT.Copy
                               ).then_inc(v_done, 1)

            def exponents(b):
                for u in range(2):
                    act.wait_ge(sub_done, 2 * b + u + 1)
                    act.activation(p_rows[:, u], p_rows[:, u], ACT.Exp).then_inc(exp_done, 1)

            def body(b, first, left):
                for u in range(2):
                    act.wait_ge(t_done, 2 * b + u + 1)
                    act.activation(pT[:, u], heads(ps_t[u][0:S]), ACT.Copy).then_inc(pT_done, 1)
                if left:
                    exponents(b + 1)
                if left == 2:
                    act.wait_ge(s_done, 2 * b + 4)
                    take_q(b + 2)
                for u in range(2):
                    act.wait_ge(pv_done, 2 * b + u + 1)
                    act.activation(oT_hi[:, u], heads(ps_o[u]), ACT.Copy).then_inc(oh_done, 1)
                if left:
                    take_v(b + 1)

            take_q(0)
            take_v(0)
            exponents(0)
            act.wait_ge(s_done, 2)
            take_q(1)
            each_batch(act, body)
            if early:
                early.split_high(act, early_in, early_hi)

        @block.vector
        def _(dve):
            def scale_mask_max(b):
                for u in range(2):
                    dve.wait_ge(s_done, 2 * b + u + 1)
                    dve.scalar_tensor_tensor(p_rows[:, u], heads(ps_s[u][0:S]), scale, causal, ALU.mult,
                                             ALU.add).then_inc(sr_done, 1)
                    dve.wait_ge(sr_done, 2 * b + u + 1)
                    dve.tensor_reduce(top[:, u, :], p_rows[:, u], AX_X, ALU.max).then_inc(top_done, 1)

            def denominator(n, u):
                dve.wait_ge(exp_done, n + 1)
                dve.tensor_reduce(den[:, u, :], p_rows[:, u], AX_X, ALU.add).then_inc(den_done, 1)
                dve.wait_ge(den_done, n + 1)
                dve.reciprocal(r_den[:, u, :], den[:, u, :]).then_inc(r_done, 1)

            def add(n, b, u):
                dve.wait_ge(y_done, n + 1)
                dve.wait_ge(add_done, n + 2)
                dve.tensor_tensor(x2[:, bass.ds(b, 1), :], ps_y[u][0:S, :].unsqueeze(1), x2[:, bass.ds(b, 1), :],
                                  ALU.add).then_inc(add_done, 1)

            def body(b, first, left):
                if left:
                    scale_mask_max(b + 1)
                for u in range(2):
                    if not first:
                        add(2 * b - 2 + u, b - 1, u)
                    if left:
                        denominator(2 * b + 2 + u, u)
                for u in range(2):
                    dve.wait_ge(oh_done, 2 * b + u + 1)
                    dve.tensor_tensor(oT_lo[:, u], heads(ps_o[u]), oT_hi[:, u].bitcast(F32),
                                      ALU.subtract).then_inc(ol_done, 1)

            dve.sem_inc(add_done, 2)
            scale_mask_max(0)
            for u in range(2):
                denominator(u, u)
            each_batch(dve, body)
            for u in range(2):
                add(2 * B - 2 + u, B - 1, u)

        @block.tensor
        def _(pe):
            def scores(b):
                for u in range(2):
                    pe.wait_ge(q_done, 2 * b + u + 1)
                    for j in range(4):
                        s = pe.matmul(ps_s[u][0:S, j * S:(j + 1) * S], q_now[:, u, j, :], kT[:, grp, bass.ds(b * S, S)],
                                      start=True, stop=True)
                    s.then_inc(s_done, 1)

            def out_rows(b):
                for u in range(2):
                    pe.wait_ge(ol_done, 2 * b + u + 1)
                    pe.wait_ge(add_done, 2 * b + u + 1)
                    for j in range(4):
                        at = slice((4 * u + j) * D, (4 * u + j + 1) * D)
                        y = mm3(pe, ps_y[u][0:S, :], oT_hi[:, u, j, :], oT_lo[:, u, j, :], wo_hi[:, at], wo_lo[:, at],
                                j == 0, j == 3)
                    y.then_inc(y_done, 1)

            def body(b, first, left):
                for u in range(2):
                    pe.wait_ge(pn_done, 2 * b + u + 1)
                    for j in range(4):
                        t = pe.transpose(ps_t[u][0:S, j * S:(j + 1) * S], p_rows[:, u, j, :], g.const("ident")[0:S, 0:S])
                    t.then_inc(t_done, 1)
                if left:
                    scores(b + 1)
                if not first:
                    out_rows(b - 1)
                pe.wait_ge(v_done, b + 1)
                for u in range(2):
                    pe.wait_ge(pT_done, 2 * b + u + 1)
                    pe.matmul(ps_o[u][:, 0:W], v_now[:, :], pT[:, u], start=True, stop=True).then_inc(pv_done, 1)

            scores(0)
            each_batch(pe, body)
            out_rows(B - 1)


def route(nc, g, name, wr_hi, wr_lo, bias, shares_dram, x, x2):
    with ExitStack() as ctx:
        def sb(n, shape, dt=F32):
            return ctx.enter_context(nc.sbuf_tensor(f"{name}_{n}", shape, dt))

        sem = ctx.enter_context(semaphores(nc, name))

        score = sb("score", [S, B, E_MOE])
        biased = sb("biased", [S, B, E_MOE])
        largest = sb("largest", [S, B, TOPK])
        replaced = sb("replaced", [S, B, E_MOE])
        total = sb("total", [S, B])
        r_total = sb("r_total", [S, B])
        shares = sb("shares", [E_MOE + 1, T])
        mm_done, sig_done, step, t_done, sh_done, one_done, stored, x_done = map(sem, (
            "mm", "sig", "step", "t", "sh", "one", "stored", "x"))
        block = ctx.enter_context(nc.Block())

        @block.sync
        def _(sp):
            sp.wait_ge(sh_done, NH)
            sp.wait_ge(one_done, 1)
            sp.dma_start(shares_dram, shares[:, :]).then_inc(stored, 16)
            sp.wait_ge(stored, 16)

        @block.gpsimd
        def _(pool):
            pool.memset(shares[E_MOE:E_MOE + 1, :], 1.0).then_inc(one_done, 1)
            pool.wait_ge(one_done, 1)
            pool.tensor_tensor(x[:, :, :], x[:, :, :], x2[:, :, :], ALU.add).then_inc(x_done, 1)

        @block.scalar
        def _(act):
            act.wait_ge(mm_done, 1)
            act.activation(score[:, :, :], g.bank[0][0:S, 0:B * E_MOE].rearrange("p (b e) -> p b e", b=B),
                           ACT.Sigmoid).then_inc(sig_done, 1)
            for t in range(NH):
                act.wait_ge(t_done, t + 1)
                act.activation(shares[0:E_MOE, t * HT:(t + 1) * HT], g.bank[1 + t][0:E_MOE, 0:HT], ACT.Copy).then_inc(sh_done, 1)

        @block.vector
        def _(dve):
            dve.wait_ge(sig_done, 1)
            dve.tensor_tensor(biased[:, :, :], score[:, :, :], bias.unsqueeze(1).broadcast_to([S, B, E_MOE]),
                              ALU.add).then_inc(step, 1)
            dve.wait_ge(step, 1)
            for b in range(B):
                dve.max(largest[:, b, :], biased[:, b, :]).then_inc(step, 1)
            for b in range(B):
                dve.wait_ge(step, 2 + b)
                dve.match_replace(replaced[:, b, :], largest[:, b, :], biased[:, b, :], NEG).then_inc(step, 1)
            dve.wait_ge(step, 1 + 2 * B)
            dve.tensor_tensor(biased[:, :, :], biased[:, :, :], replaced[:, :, :], ALU.not_equal).then_inc(step, 1)
            dve.wait_ge(step, 2 + 2 * B)
            dve.tensor_tensor(biased[:, :, :], biased[:, :, :], score[:, :, :], ALU.mult).then_inc(step, 1)
            dve.wait_ge(step, 3 + 2 * B)
            dve.tensor_reduce(total[:, :], biased[:, :, :], AX_X, ALU.add).then_inc(step, 1)
            dve.wait_ge(step, 4 + 2 * B)
            dve.reciprocal(r_total[:, :], total[:, :]).then_inc(step, 1)
            dve.wait_ge(step, 5 + 2 * B)
            dve.tensor_tensor(score[:, :, :], biased[:, :, :], r_total[:, :].unsqueeze(2).broadcast_to([S, B, E_MOE]),
                              ALU.mult).then_inc(step, 1)

        @block.tensor
        def _(pe):
            for b in range(B):
                for k in range(KC):
                    y = mm3(pe, g.bank[0][0:S, b * E_MOE:(b + 1) * E_MOE], g.hT_hi[:, k, b * S:(b + 1) * S],
                            g.hT_lo[:, k, b * S:(b + 1) * S], wr_hi[:, k, :], wr_lo[:, k, :], k == 0, k == KC - 1)
            y.then_inc(mm_done, 1)
            pe.wait_ge(step, 6 + 2 * B)
            for b in range(B):
                t = pe.transpose(g.bank[1 + b // HB][0:E_MOE, b % HB * S:(b % HB + 1) * S], score[:, b, :],
                                 g.const("ident")[0:S, 0:S])
                if b % HB == HB - 1:
                    t.then_inc(t_done, 1)


def experts(nc, g, name, w_dram, E, acc, weights, shares_dram=None):
    U = NH * NC
    DT = NH * KC
    with ExitStack() as ctx:
        def sb(n, shape, dt=F32):
            return ctx.enter_context(nc.sbuf_tensor(f"{name}_{n}", shape, dt))

        sem = ctx.enter_context(semaphores(nc, name))

        raw, w_hi, w_lo = weights
        silu = sb("silu", [P, NC, HT])
        prod = sb("prod", [P, NC, HT])
        a_hi = sb("a_hi", [P, NH, NC, HT], F32R)
        a_lo = sb("a_lo", [P, NH, NC, HT], F32R)
        share = sb("share", [P, 2, T]) if shares_dram is not None else None
        ps_g, ps_u, ps_d = g.bank[0:2], g.bank[2:4], g.bank[4:8]
        (raw_in, hi_done, lo_done, gu_done, silu_done, prod_done, sh_done, ah_done, al_done, d_done, acc_done,
         zero) = map(sem, ("raw_in", "hi", "lo", "gu", "silu", "prod", "sh", "ah", "al", "d", "acc", "zero"))
        share_in = [sem("share_in0"), sem("share_in1")]
        block = ctx.enter_context(nc.Block())
        PR0, AC0, D0, SH0 = NC, KC, DT, 2 * U

        def each_expert(eng, body):
            body(0, 0, True, False)
            n = (E - 2) // 2
            with eng.Fori(0, n) as i:
                body(2 * i + 1, 1, False, False)
                body(2 * i + 2, 0, False, False)
            if E % 2:
                body(E - 2, 1, False, False)
                body(E - 1, 0, False, True)
            else:
                body(E - 1, 1, False, True)

        @block.sync
        def _(sp):
            def body(e, slot, first, last):
                if not first:
                    sp.wait_ge(lo_done, NP_ * e)
                    sp.dma_start(raw[:, :], w_dram[bass.ds(e, 1)].squeeze(0)).then_inc(raw_in, 16)
                if share is not None:
                    sp.wait_ge(sh_done, U * e + U)
                    sp.dma_start(share[:, slot, :],
                                 shares_dram[bass.ds(e, 1), :].squeeze(0).partition_broadcast(P)).then_inc(share_in[slot], 16)

            each_expert(sp, body)

        @block.gpsimd
        def _(pool):
            def split_low(e, slot, i):
                pool.wait_ge(hi_done, NP_ * e + i + 1)
                pool.tensor_tensor(w_lo[:, slot, i * PW:(i + 1) * PW], raw[:, i * PW:(i + 1) * PW],
                                   w_hi[:, slot, i * PW:(i + 1) * PW].bitcast(F32), ALU.subtract).then_inc(lo_done, 1)

            def body(e, slot, first, last):
                for n in range(U):
                    t, c = divmod(n, NC)
                    if share is not None:
                        if n == 0:
                            pool.wait_ge(share_in[slot], 8 * (e - slot) + 16)
                        pool.wait_ge(prod_done, U * e + n + 1 + PR0)
                        pool.tensor_tensor(prod[:, c, :], prod[:, c, :], share[:, slot, t * HT:(t + 1) * HT],
                                           ALU.mult).then_inc(sh_done, 1)
                    if n < NP_ and not last:
                        split_low(e + 1, 1 - slot, n)

            if share is not None:
                pool.sem_inc(sh_done, SH0)
            pool.sem_inc(lo_done, NP_)
            each_expert(pool, body)

        @block.scalar
        def _(act):
            def split_high(e, slot, i):
                if i == 0:
                    act.wait_ge(raw_in, 16 * e)
                act.activation(w_hi[:, slot, i * PW:(i + 1) * PW], raw[:, i * PW:(i + 1) * PW], ACT.Copy).then_inc(hi_done, 1)

            def body(e, slot, first, last):
                for n in range(U):
                    t, c = divmod(n, NC)
                    act.wait_ge(gu_done, U * e + n + 1)
                    act.activation(silu[:, c, :], ps_g[c][:, 0:HT], ACT.Silu).then_inc(silu_done, 1)
                    if share is not None:
                        act.wait_ge(sh_done, U * e + n + 1 + SH0)
                    else:
                        act.wait_ge(prod_done, U * e + n + 1 + PR0)
                    act.activation(a_hi[:, t, c, :], prod[:, c, :], ACT.Copy).then_inc(ah_done, 1)
                    if n < NP_ and not last:
                        if n == 0:
                            act.wait_ge(d_done, DT * e + D0)
                        split_high(e + 1, 1 - slot, n)

            act.sem_inc(hi_done, NP_)
            each_expert(act, body)

        @block.vector
        def _(dve):
            def add(e, t):
                for f in range(KC):
                    n = DT * e + KC * t + f
                    dve.wait_ge(d_done, n + 1 + D0)
                    dst = acc[:, f, t * HT:(t + 1) * HT]
                    dve.tensor_tensor(dst, ps_d[f][:, 0:HT], dst, ALU.add).then_inc(acc_done, 1)

            def unit(e, n):
                t, c = divmod(n, NC)
                dve.wait_ge(silu_done, U * e + n + 1)
                dve.tensor_tensor(prod[:, c, :], ps_u[c][:, 0:HT], silu[:, c, :], ALU.mult).then_inc(prod_done, 1)
                dve.wait_ge(ah_done, U * e + n + 1)
                dve.tensor_tensor(a_lo[:, t, c, :], prod[:, c, :], a_hi[:, t, c, :].bitcast(F32),
                                  ALU.subtract).then_inc(al_done, 1)

            def body(e, slot, first, last):
                unit(e, 0)
                if not first:
                    add(e - 1, 1)
                unit(e, 1)
                unit(e, 2)
                add(e, 0)
                unit(e, 3)

            dve.sem_inc(prod_done, PR0)
            dve.sem_inc(acc_done, AC0)
            dve.memset(acc[:, :, :], 0.0).then_inc(zero, 1)
            dve.wait_ge(zero, 1)
            each_expert(dve, body)
            add(E - 1, 1)

        @block.tensor
        def _(pe):
            def gate_up(e, slot, n):
                t, c = divmod(n, NC)
                pe.wait_ge(prod_done, U * e + n + 1)
                for ps, base in ((ps_g, 0), (ps_u, KC * EI)):
                    for k in range(KC):
                        at = slice(base + k * EI + c * P, base + k * EI + (c + 1) * P)
                        y = mm3(pe, ps[c][:, 0:HT], w_hi[:, slot, at], w_lo[:, slot, at],
                                g.hT_hi[:, k, t * HT:(t + 1) * HT], g.hT_lo[:, k, t * HT:(t + 1) * HT],
                                k == 0, k == KC - 1)
                y.then_inc(gu_done, 1)

            def down(e, slot, t):
                pe.wait_ge(al_done, U * e + NC * (t + 1))
                for f in range(KC):
                    n = DT * e + KC * t + f
                    pe.wait_ge(acc_done, n + 1)
                    for c in range(NC):
                        at = slice(2 * KC * EI + c * D + f * P, 2 * KC * EI + c * D + (f + 1) * P)
                        y = mm3(pe, ps_d[f][:, 0:HT], w_hi[:, slot, at], w_lo[:, slot, at], a_hi[:, t, c, :],
                                a_lo[:, t, c, :], c == 0, c == NC - 1)
                    y.then_inc(d_done, 1)

            def body(e, slot, first, last):
                pe.wait_ge(lo_done, NP_ * (e + 1))
                gate_up(e, slot, 0)
                if not first:
                    down(e - 1, 1 - slot, 1)
                gate_up(e, slot, 1)
                gate_up(e, slot, 2)
                down(e, slot, 0)
                gate_up(e, slot, 3)

            pe.sem_inc(d_done, D0)
            each_expert(pe, body)
            down(E - 1, (E - 1) % 2, 1)


def add_back(nc, g, name, x, acc, out=None):
    with semaphores(nc, name) as sem, nc.Block() as block:
        t_done, x_done, stored = map(sem, ("t", "x", "stored"))

        @block.tensor
        def _(pe):
            for b in range(B):
                if b >= 4:
                    pe.wait_ge(x_done, b - 3)
                for k in range(KC):
                    t = pe.transpose(g.bank[b % 4][0:S, k * P:(k + 1) * P], acc[:, k, b * S:(b + 1) * S], g.const("ident"))
                t.then_inc(t_done, 1)

        @block.vector
        def _(dve):
            for b in range(B):
                dve.wait_ge(t_done, b + 1)
                dve.tensor_tensor(x[:, b, :], g.bank[b % 4][0:S, :], x[:, b, :], ALU.add).then_inc(x_done, 1)
                if out is None:
                    dve.wait_ge(x_done, b + 1)
                    dve.bn_stats(g.stats[:, b, :], x[:, b, :])

        if out is not None:
            @block.sync
            def _(sp):
                for i in range(2):
                    sp.wait_ge(x_done, HB * (i + 1))
                    sp.dma_start(out[HB * i:HB * (i + 1)].rearrange("b s d -> s b d"), x[:, HB * i:HB * (i + 1), :]
                                 ).then_inc(stored, 16)
                sp.wait_ge(stored, 32)


@contextmanager
def transposed(nc, g, name):
    with nc.sbuf_tensor(f"{name}_hT_hi", [P, KC, T], F32R) as hi, nc.sbuf_tensor(f"{name}_hT_lo", [P, KC, T], F32R) as lo:
        g.hT_hi, g.hT_lo = hi, lo
        yield


def flat(w):
    return w.rearrange("p i k n -> p (i k n)")


def vw(heads, hd):
    return heads * (hd + 1) + PVW - (hd + 1)


class Shared:
    pass


OutputNorm = namedtuple("OutputNorm", "rs bo_rs gamma beta")


def program(nc, a, out):
    with ExitStack() as ctx:
        def sb(n, shape, dt=F32):
            return ctx.enter_context(nc.sbuf_tensor(n, shape, dt))

        g = Shared()
        g.bank = [ctx.enter_context(nc.psum_tensor(f"bank{i}", [P, 512], F32)) for i in range(8)]
        consts = sb("consts", [P, NCONST])
        rows = sb("rows", [P, NROW])
        pvec = sb("pvec", [P, 16])
        x = sb("x", [S, B, D])
        g.const = lambda n: consts[:, CONSTS[n][0]:CONSTS[n][0] + CONSTS[n][1]]
        g.row = lambda n: rows[:, ROWS[n][0]:ROWS[n][0] + ROWS[n][1]]
        x_mask = sb("x_mask", [CW, B * CK], I32)
        x_high = sb("x_high", [CW, B * CK])
        y_mask = sb("y_mask", [CW, B * CK], U8)
        y_valid = sb("y_valid", [CW, B * CK])
        g.ones = sb("ones", [P, 32])
        g.stats = sb("stats", [S, B, 6])
        rs = sb("rs", [P, 1])
        bo_rs = sb("bo_rs", [P, D])
        shares = nc.dram_tensor("shares", (E_MOE + 1, T), F32).ap()
        x_in = nc.alloc_semaphore("x_in")
        loaded = nc.alloc_semaphore("loaded")
        ready = nc.alloc_semaphore("ready")

        with nc.Block() as block:
            @block.sync
            def _(sp):
                sp.dma_start(x[:, :, :], a["x"].rearrange("b s d -> s b d")).then_inc(x_in, 16)
                sp.dma_start(consts[:, :], a["consts"]).then_inc(x_in, 16)
                sp.wait_ge(x_in, 32)

            @block.scalar
            def _(act):
                act.dma_start(pvec[:, :], a["pvec"]).then_inc(loaded, 16)
                act.dma_start(x_mask[:, :], a["x_mask"]).then_inc(loaded, 16)
                act.dma_start(y_mask[:, :], a["y_mask"]).then_inc(loaded, 16)
                act.wait_ge(x_in, 32)
                act.dma_start(rows[:, :], a["rows"].partition_broadcast(P)).then_inc(loaded, 16)

        def small_parts():
            with nc.Block() as block:
                @block.vector
                def _(dve):
                    dve.memset(g.ones[:, :], 1.0).then_inc(ready, 1)
                    dve.wait_ge(loaded, 16 * 4)
                    dve.tensor_scalar(x_high[:, :], x_mask[:, :], 0.5, 100.0, ALU.is_gt, ALU.mult).then_inc(ready, 1)
                    dve.tensor_copy(y_valid[:, :], y_mask[:, :]).then_inc(ready, 1)
                    dve.tensor_scalar(rs[:, :], g.row("res_scale"), 0.0, 0.3, ALU.max, ALU.min).then_inc(ready, 1)
                    dve.wait_ge(ready, 4)
                    dve.tensor_scalar(bo_rs[:, :], g.row("x_bo"), rs[:, 0:1], None, ALU.mult).then_inc(ready, 1)
                    dve.tensor_scalar(x_high[:, :], x_high[:, :], 50.0, None, ALU.subtract).then_inc(ready, 1)

        def weight_pair(st, name):
            return tuple(st.enter_context(nc.sbuf_tensor(f"{name}_{n}", [P, 2, KC * P], dt))
                         for n, dt in (("raw", F32), ("w_hi", F32R), ("w_lo", F32R)))

        def first_pair(w_dram, weights, reuses=False):
            return Early([w_dram[u] for u in range(2)], *([w[:, u, :] for u in range(2)] for w in weights), reuses)

        def context_parts(st, name):
            return tuple(st.enter_context(nc.sbuf_tensor(f"{name}_c_{n}", [P, KC, S2P], dt))
                         for n, dt in (("raw", F32), ("hi", F32R), ("lo", F32R)))

        def expert_weights(st, name):
            return (st.enter_context(nc.sbuf_tensor(f"{name}_raw", [P, EW], F32)),
                    st.enter_context(nc.sbuf_tensor(f"{name}_w_hi", [P, 2, EW], F32R)),
                    st.enter_context(nc.sbuf_tensor(f"{name}_w_lo", [P, 2, EW], F32R)))

        def first_expert(w_dram, weights):
            raw, w_hi, w_lo = weights
            pieces = [slice(i * PW, (i + 1) * PW) for i in range(NP_)]
            return Early([w_dram[0, :, at] for at in pieces], [raw[:, at] for at in pieces],
                         [w_hi[:, 0, at] for at in pieces], [w_lo[:, 0, at] for at in pieces])

        with ExitStack() as st:
            qk = st.enter_context(nc.sbuf_tensor("a_qk", [P, 2 * KC, T], F32))
            v = st.enter_context(nc.sbuf_tensor("a_v", [S, B, vw(16, 32)], F32))
            with transposed(nc, g, "a"), ExitStack() as w:
                weights = weight_pair(w, "a")
                normalise(nc, g, "a_norm", x, "ln", first=True, early=first_pair(a["a_wqk"], weights))
                small_parts()
                project(nc, g, "a_proj", a["a_wqk"], 2 * KC, qk, weights, bias=pvec[:, 0:8],
                        value=(a["a_wv"], v, 16, 32, g.row("a_bv")[0:S]))
            causal = g.const("causal")[0:S].unsqueeze(1).broadcast_to([S, 4, S])
            self_attention(nc, g, "a_att", x, qk[:, 0:KC], qk[:, KC:2 * KC], v, 16, 32, 32 ** -0.5,
                           g.const("hm32"), lambda grp: causal, a["a_wo"], wo_bias=g.row("a_bo")[0:S])

        with ExitStack() as st:
            q = st.enter_context(nc.sbuf_tensor("x_q", [P, KC, T], F32))
            kv_hi = st.enter_context(nc.sbuf_tensor("x_kv_hi", [P, 2, KC, D], F32R))
            kv_lo = st.enter_context(nc.sbuf_tensor("x_kv_lo", [P, 2, KC, D], F32R))
            context = context_parts(st, "x")
            with transposed(nc, g, "x"), ExitStack() as w:
                weights = weight_pair(w, "x")
                kv_raw = w.enter_context(nc.sbuf_tensor("x_kv_raw", [P, KC * D], F32))
                normalise(nc, g, "x_norm", x, "ln", early=first_pair(a["x_wq"], weights))
                project(nc, g, "x_proj", a["x_wq"], KC, q, weights, bias=pvec[:, 8:12], scale=32 ** -0.5,
                        also=(a["x_wkv"], kv_raw, flat(kv_hi), flat(kv_lo)),
                        early=Early([a["ctxT"][0]], *([c[:, :, :]] for c in context)))
            cross_attention(nc, g, "x_att", x, q, a["ctxT"], context, kv_hi, kv_lo, a["x_wo"], "clip", k_bias=pvec[:, 12:16],
                            v_bias=g.row("x_bv")[0:CW], mask_cols=x_high,
                            norm=OutputNorm(rs=rs[0:S, 0:1], bo_rs=bo_rs[0:S, :], gamma=g.row("gamma")[0:S],
                                            beta=g.row("beta")[0:S]))

        with nc.sbuf_tensor("f_x2", [S, B, D], F32) as x2:
            with ExitStack() as st:
                v = st.enter_context(nc.sbuf_tensor("f_v", [S, B, D], F32))
                kT = st.enter_context(nc.sbuf_tensor("f_kT", [P, NG, T], F32))
                weights = weight_pair(st, "f")
                causal = g.const("causal")[0:S].unsqueeze(1).broadcast_to([S, 4, S])
                rope = (g.const("cos128"), g.const("sin128"))
                with transposed(nc, g, "f"), ExitStack() as inner:
                    normalise(nc, g, "f_norm", x, "ln_rms", eps2=1e-5, w=g.row("ln1_w")[0:S], keep=x2,
                              early=first_pair(a["f_wk"], weights))
                    project(nc, g, "f_k", a["f_wk"], NG, kT, weights, rope=rope, value=(a["f_wv"], v, NG, P, None),
                            early=first_pair(a["f_wq"][0], weights, reuses=True))
                    q = inner.enter_context(nc.sbuf_tensor("f_q", [P, GQ, T], F32))
                    wo_hi = inner.enter_context(nc.sbuf_tensor("f_wo_hi", [P, GQ * D], F32R))
                    wo_lo = inner.enter_context(nc.sbuf_tensor("f_wo_lo", [P, GQ * D], F32R))
                    for grp in range(NG):
                        with nc.sbuf_tensor(f"f_wo_raw{grp}", [P, 2 * D], F32) as wo_raw:
                            project(nc, g, f"f_q{grp}_proj", a["f_wq"][grp], GQ, q, weights, rope=rope,
                                    also=(a["f_wo"][grp], wo_raw, wo_hi, wo_lo))
                        group_attention(nc, g, f"f_att{grp}", x2, q, kT, v, grp, wo_hi, wo_lo, causal,
                                        first_pair(a["f_wq"][grp + 1], weights) if grp + 1 < NG else None)
            with ExitStack() as st:
                acc = st.enter_context(nc.sbuf_tensor("m_acc", [P, KC, T], F32))
                with transposed(nc, g, "m"), ExitStack() as w:
                    weights = expert_weights(w, "m")
                    router = [w.enter_context(nc.sbuf_tensor(f"m_wr_{n}", [P, KC, E_MOE], dt))
                              for n, dt in (("raw", F32), ("hi", F32R), ("lo", F32R))]
                    early = first_expert(a["m_w"], weights)
                    early.add(a["m_wr"], *(r[:, :, :] for r in router))
                    normalise(nc, g, "m_norm", x2, "rms", eps2=1e-5, w=g.row("ln2_w")[0:S],
                              early=early)
                    route(nc, g, "m_route", router[1], router[2], g.row("expert_bias")[0:S], shares, x, x2)
                    experts(nc, g, "m_exp", a["m_w"], E_MOE + 1, acc, weights, shares)
                add_back(nc, g, "m_add", x, acc)

        with ExitStack() as st:
            qk = st.enter_context(nc.sbuf_tensor("b_qk", [P, 2 * KC, T], F32))
            v = st.enter_context(nc.sbuf_tensor("b_v", [S + 1, B, vw(32, 16)], F32))
            bias = st.enter_context(nc.sbuf_tensor("b_bias", [S, 32, S], F32))
            with transposed(nc, g, "b"), ExitStack() as w:
                weights = weight_pair(w, "b")
                normalise(nc, g, "b_norm", x, "ln", early=first_pair(a["b_wqk"], weights))
                project(nc, g, "b_proj", a["b_wqk"], 2 * KC, qk, weights, rope=(g.const("cos16"), g.const("sin16")),
                        value=(a["b_wv"], v, 32, 16, None))
            self_attention(nc, g, "b_att", x, qk[:, 0:KC], qk[:, KC:2 * KC], v, 32, 16, 16 ** -0.5,
                           g.const("hm8"), lambda grp: bias[:, 4 * grp:4 * grp + 4, :], a["b_wo"],
                           sink=g.row("offset")[0:S], bias_load=(bias, a["b_bias"]))

        with ExitStack() as st:
            q = st.enter_context(nc.sbuf_tensor("y_q", [P, KC, T], F32))
            gate = st.enter_context(nc.sbuf_tensor("y_gate", [S, B, D], F32))
            kv_hi = st.enter_context(nc.sbuf_tensor("y_kv_hi", [P, 2, KC, D], F32R))
            kv_lo = st.enter_context(nc.sbuf_tensor("y_kv_lo", [P, 2, KC, D], F32R))
            context = context_parts(st, "y")
            y_mask_row = st.enter_context(nc.sbuf_tensor("y_mask_row", [1, B * S2], U8))
            y_bias = st.enter_context(nc.sbuf_tensor("y_bias", [1, B * S2], BF16))
            with semaphores(nc, "y_mask") as sem, nc.Block() as block:
                mask_in = sem("in")

                @block.sync
                def _(sp):
                    sp.dma_start(y_mask_row[:, :], a["y_mask_row"]).then_inc(mask_in, 16)

                @block.vector
                def _(dve):
                    dve.wait_ge(mask_in, 16)
                    dve.tensor_scalar(y_bias[:, :], y_mask_row[:, :], 1.0, -NEG, ALU.subtract, ALU.mult)

            with transposed(nc, g, "y"), ExitStack() as w:
                weights = weight_pair(w, "y")
                kv_raw = w.enter_context(nc.sbuf_tensor("y_kv_raw", [P, KC * D], F32))
                normalise(nc, g, "y_norm", x, "ln_rms", eps2=1e-6, w=g.row("norm_w")[0:S], keep=gate,
                          early=first_pair(a["y_wq"], weights))
                project(nc, g, "y_proj", a["y_wq"], KC, q, weights, scale=32 ** -0.5,
                        value=(a["y_wg"], gate, None, None, None), also=(a["y_wkv"], kv_raw, flat(kv_hi), flat(kv_lo)),
                        early=Early([a["ctxT"][0]], *([c[:, :, :]] for c in context)))
            cross_attention(nc, g, "y_att", x, q, a["ctxT"], context, kv_hi, kv_lo, a["y_wo"], "max", mask_cols=y_valid,
                            mask_row=y_bias, gate=gate)

        with ExitStack() as st:
            acc = st.enter_context(nc.sbuf_tensor("z_acc", [P, KC, T], F32))
            with transposed(nc, g, "z"), ExitStack() as w:
                weights = expert_weights(w, "z")
                normalise(nc, g, "z_norm", x, "ln", early=first_expert(a["z_w"], weights))
                experts(nc, g, "z_exp", a["z_w"], FFN // EI, acc, weights)
            add_back(nc, g, "z_add", x, acc, out)


def chunked(w):
    k, m = w.shape[0] // P, w.shape[1] // P
    return np.ascontiguousarray(w.reshape(k, P, m, P).transpose(2, 1, 0, 3).reshape(m, P, k * P))


def by_partition(w):
    return np.ascontiguousarray(w.reshape(-1, P, w.shape[1]).transpose(1, 0, 2))


def expert_rows(gate, up, down):
    e = gate.shape[0]
    gu = [w.reshape(e, KC, P, EI).transpose(0, 2, 1, 3).reshape(e, P, KC * EI) for w in (gate, up)]
    return np.concatenate(gu + [down.reshape(e, NC, P, D).transpose(0, 2, 1, 3).reshape(e, P, NC * D)], axis=2)


def packed(i):
    o = {}
    c = np.zeros((P, NCONST), np.float32)

    def put(name, v):
        c[:v.shape[0], CONSTS[name][0]:CONSTS[name][0] + v.shape[1]] = v

    put("ident", np.eye(P, dtype=np.float32))
    put("hm32", (np.arange(P)[:, None] // 32 == np.arange(4)).astype(np.float32))
    put("hm8", (np.arange(P)[:, None] % 64 // 8 == np.arange(8)).astype(np.float32))
    put("causal", np.where(np.tril(np.ones((S, S), bool)), 0.0, NEG).astype(np.float32))
    put("power", np.full((P, B), -0.5, np.float32))
    for hd in (16, 128):
        half = hd // 2
        inv = (1.0 / np.float32(ROPE_BASE) ** (np.arange(half, dtype=np.float32) / np.float32(half))).astype(np.float32)
        angle = (np.arange(S, dtype=np.float32)[None, :] * inv[:, None]).astype(np.float32)
        at = np.arange(P) % 64 % half
        sign = np.where(np.arange(P) < 64, -1.0, 1.0).astype(np.float32)[:, None]
        put(f"cos{hd}", np.cos(angle)[at])
        put(f"sin{hd}", np.sin(angle)[at] * sign)
    o["consts"] = c
    r = {"a_bv": "L0_attn_bv", "a_bo": "L0_attn_bo", "x_bv": "L0_xattn_bv", "x_bo": "L0_xattn_bo",
         "gamma": "L0_xattn_ln_gamma", "beta": "L0_xattn_ln_beta", "ln1_w": "L0_ffn_ln1_w", "ln2_w": "L0_ffn_ln2_w",
         "norm_w": "L1_xattn_norm_w", "expert_bias": "L0_ffn_expert_bias", "offset": "L1_attn_softmax_offset",
         "res_scale": "L0_xattn_residual_scale"}
    o["rows"] = np.concatenate([np.reshape(i[r[n]], -1) for n in ROWS])
    o["pvec"] = np.concatenate([i[n].reshape(KC, P).T for n in ("L0_attn_bq", "L0_attn_bk", "L0_xattn_bq", "L0_xattn_bk")],
                               axis=1)
    o["x"] = i["x"]
    o["a_wqk"] = chunked(np.concatenate([i["L0_attn_wq"].T, i["L0_attn_wk"].T], axis=1))
    o["a_wv"] = by_partition(i["L0_attn_wv"].T)
    o["a_wo"] = by_partition(i["L0_attn_wo"].T)
    o["f_wk"] = chunked(i["L0_ffn_Wk"])
    o["f_wv"] = by_partition(i["L0_ffn_Wv"])
    o["f_wq"] = chunked(i["L0_ffn_Wq"]).reshape(NG, GQ, P, KC * P)
    o["f_wo"] = i["L0_ffn_Wo"].reshape(NG, GQ, P, D).transpose(0, 2, 1, 3).reshape(NG, P, GQ * D)
    o["m_wr"] = by_partition(i["L0_ffn_Wr"])
    o["m_w"] = expert_rows(*(np.concatenate([i["L0_ffn_" + n], i["L0_ffn_" + m][None]])
                             for n, m in (("Wg", "Wsg"), ("Wu", "Wsu"), ("Wd", "Wsd"))))
    o["z_w"] = expert_rows(*(i["L1_ffn_" + n].reshape(FFN // EI, EI, D).transpose(0, 2, 1) for n in ("w_gate", "w_up")),
                           i["L1_ffn_w_down"].T.reshape(FFN // EI, EI, D))
    at = np.arange(D).reshape(KC, 8, 2, 8).transpose(0, 2, 1, 3).reshape(-1)
    o["b_wqk"] = chunked(np.concatenate([i["L1_attn_Wq"].T[:, at], i["L1_attn_Wk"].T[:, at]], axis=1))
    o["b_wv"] = by_partition(i["L1_attn_Wv"].T)
    o["b_wo"] = by_partition(i["L1_attn_Wo"].T)
    back = np.arange(S)[:, None] - np.arange(S)[None, :]
    o["b_bias"] = np.where(back[:, None, :] >= 0, i["L1_attn_learnable_bias"][:, np.maximum(back, 0)].transpose(1, 0, 2),
                           np.float32(NEG)).astype(np.float32)
    o["ctxT"] = np.zeros((B, P, KC, S2P), np.float32)
    o["ctxT"][:, :, :, 0:S2] = i["ctx_2048"].transpose(0, 2, 1).reshape(B, KC, P, S2).transpose(0, 2, 1, 3)
    for n, src in (("x_wq", "L0_xattn_Wq"), ("y_wq", "L1_xattn_wq")):
        o[n] = chunked(i[src].T)
    for n, keys, values in (("x_wkv", "L0_xattn_Wk", "L0_xattn_Wv"), ("y_wkv", "L1_xattn_wk", "L1_xattn_wv")):
        o[n] = np.concatenate([by_partition(i[src].T).reshape(P, KC * D) for src in (keys, values)], axis=1)
    for n, src in (("x_wo", "L0_xattn_Wo"), ("y_wo", "L1_xattn_wo"), ("y_wg", "L1_xattn_wg")):
        o[n] = by_partition(i[src].T)
    for n, src in (("x_mask", "mask_BxS2_ik0"), ("y_mask", "mask_BxS2_bk0")):
        o[n] = i[src].reshape(B, CK, CW).transpose(2, 0, 1).reshape(CW, B * CK)
    o["y_mask_row"] = i["mask_BxS2_bk0"].reshape(1, B * S2)
    return {k: np.ascontiguousarray(v) for k, v in o.items()}


def kernel(**inputs):
    import concourse.bacc as bacc
    from concourse.bass_utils import run_bass_kernel_spmd

    arrays = packed({k: np.asarray(v) for k, v in inputs.items()})
    nc = bacc.Bacc("TRN2", target_bir_lowering=False, num_devices=1)
    aps = {k: nc.dram_tensor(f"in_{k}", v.shape, mybir.dt.from_np(v.dtype), kind="ExternalInput").ap()
           for k, v in arrays.items()}
    out = nc.dram_tensor("out", (B, S, D), F32, kind="ExternalOutput").ap()
    program(nc, aps, out)
    r = run_bass_kernel_spmd(nc, [{f"in_{k}": v for k, v in arrays.items()}], core_ids=[0])
    return r.results[0]["out"]
```
